# Optimizing a Trainium2 kernel written in Bass

```python
import numpy as np
import jax
import jax.numpy as jnp

def _softmax(x, axis=-1):
    return jax.nn.softmax(x, axis=axis)

def _gelu(x):
    return jax.nn.gelu(x, approximate=True)

def _silu(x):
    return jax.nn.silu(x)

def _sigmoid(x):
    return jax.nn.sigmoid(x)

def _layernorm(x, axis=-1, eps=1e-05):
    m = jnp.mean(x, axis=axis, keepdims=True)
    v = jnp.var(x, axis=axis, keepdims=True)
    return (x - m) / jnp.sqrt(v + eps)

def _scatter_add(tgt, idx, src, axis=0):
    return tgt.at[idx].add(src)

def _segment_sum(src, seg, n):
    return jax.ops.segment_sum(src, seg, n)
kernel_name = 'mk_gnn_preln_d2_gnn_r32_1899d2'

def setup_inputs(seed: int=0):
    np.random.seed(seed)
    _w = jnp.asarray

    def _rec_inputs():
        import jax
        import jax.numpy as jnp
        _gk = jax.random.key(seed)
        x = -0.000202 + 1 * jax.random.normal(jax.random.fold_in(_gk, 1), (3125, 64), jnp.float32)
        _s = jax.random.randint(jax.random.fold_in(_gk, 2), (50000,), 0, 3125, jnp.int32)
        _d = jax.random.randint(jax.random.fold_in(_gk, 3), (50000,), 0, 3125, jnp.int32)
        _loop = jnp.arange(3125, dtype=jnp.int32)
        src = jnp.concatenate([_s, _d, _loop])
        dst = jnp.concatenate([_d, _s, _loop])
        _o = jnp.argsort(dst, stable=True)
        src = src[_o]
        dst = dst[_o]
        edge_weight = jax.random.uniform(jax.random.fold_in(_gk, 12), (103125,), jnp.float32, 0.0, 0.0625)
        return (x, src, dst, edge_weight)
    x, src, dst, edge_weight = _rec_inputs()

    def _L0_gnn_setup():
        import jax, jax.numpy as jnp
        import numpy as np
        N_NODES = 3125
        N_EDGES = 50000
        F_IN = 64
        F_HID = 64
        CURV = 1.0
        MIN_NORM = 1e-15
        PROJ_EPS = 0.004

        def _artanh(x):
            x = jnp.clip(x, -1.0 + 1e-07, 1.0 - 1e-07)
            return 0.5 * (jnp.log1p(x) - jnp.log1p(-x))

        def _norm(x):
            return jnp.sqrt(jnp.clip(jnp.sum(x * x, axis=-1, keepdims=True), MIN_NORM))

        def proj(x, c):
            maxnorm = (1.0 - PROJ_EPS) / jnp.sqrt(c)
            n = _norm(x)
            return jnp.where(n > maxnorm, x / n * maxnorm, x)

        def expmap0(u, c):
            sc = jnp.sqrt(c)
            n = _norm(u)
            return jnp.tanh(sc * n) * u / (sc * n)

        def logmap0(p, c):
            sc = jnp.sqrt(c)
            n = _norm(p)
            return _artanh(sc * n) * p / (sc * n)

        def mobius_add(x, y, c):
            x2 = jnp.sum(x * x, -1, keepdims=True)
            y2 = jnp.sum(y * y, -1, keepdims=True)
            xy = jnp.sum(x * y, -1, keepdims=True)
            num = (1.0 + 2.0 * c * xy + c * y2) * x + (1.0 - c * x2) * y
            den = 1.0 + 2.0 * c * xy + c * c * x2 * y2
            return num / jnp.clip(den, MIN_NORM)

        def mobius_matvec(M, x, c):
            sc = jnp.sqrt(c)
            xn = _norm(x)
            mx = x @ M.T
            mxn = _norm(mx)
            res = jnp.tanh(mxn / xn * _artanh(sc * xn)) * mx / (mxn * sc)
            zero = jnp.all(mx == 0, axis=-1, keepdims=True)
            return jnp.where(zero, jnp.zeros_like(res), res)

        def hyp_linear(x, W, b, c):
            res = proj(mobius_matvec(W, x, c), c)
            hyp_b = proj(expmap0(b.reshape(1, -1), c), c)
            return proj(mobius_add(res, hyp_b, c), c)

        def hyp_agg(x, src, dst, w, c, n_nodes):
            xt = logmap0(x, c)
            msg = xt[src] * w[:, None]
            agg = jax.ops.segment_sum(msg, dst, num_segments=n_nodes)
            return proj(expmap0(agg, c), c)

        def hyp_act(x, c_in, c_out):
            xt = jax.nn.relu(logmap0(x, c_in))
            return proj(expmap0(xt, c_out), c_out)

        def hgnn_layer(x, W, b, src, dst, w, c_in, c_out, n_nodes):
            h = hyp_linear(x, W, b, c_in)
            h = hyp_agg(h, src, dst, w, c_in, n_nodes)
            return hyp_act(h, c_in, c_out)
        key = jax.random.key(seed)
        ks = jax.random.split(key, 7)
        x = jax.random.normal(ks[0], (N_NODES, F_IN), dtype=jnp.float32)
        edge_index = jax.random.randint(ks[1], (2, N_EDGES), 0, N_NODES, dtype=jnp.int64 if jax.config.jax_enable_x64 else jnp.int32)
        edge_weight = jax.random.uniform(ks[2], (N_EDGES,), dtype=jnp.float32) / 16.0
        W0 = jax.random.normal(ks[3], (F_HID, F_IN), dtype=jnp.float32) * 0.1
        b0 = jax.random.normal(ks[4], (F_HID,), dtype=jnp.float32) * 0.1
        W1 = jax.random.normal(ks[5], (F_HID, F_HID), dtype=jnp.float32) * 0.1
        b1 = jax.random.normal(ks[6], (F_HID,), dtype=jnp.float32) * 0.1
        return {'x': x, 'edge_index': edge_index, 'edge_weight': edge_weight, 'W0': W0, 'b0': b0, 'W1': W1, 'b1': b1}
    _L0_gnn_all = _L0_gnn_setup()
    _L0_gnn_in = {k: v for k, v in _L0_gnn_all.items() if k in ('W0', 'b0', 'W1', 'b1')}
    del _L0_gnn_all

    def _L1_gnn_setup():
        import jax, jax.numpy as jnp
        import numpy as np
        N_NODES = 50000
        N_EDGES = 25000
        D_FEAT = 64
        D_HID = 128
        D_OUT = 64
        key = jax.random.key(seed)
        k1, k2, k3, k4 = jax.random.split(key, 4)
        x = jax.random.normal(k1, (N_NODES, D_FEAT), dtype=jnp.float32)
        edge_index = jax.random.randint(k2, (2, N_EDGES), 0, N_NODES, dtype=jnp.int64)
        W1 = jax.random.normal(k3, (2 * D_FEAT, D_HID), dtype=jnp.float32) / np.sqrt(2 * D_FEAT)
        b1 = jnp.zeros((D_HID,), dtype=jnp.float32)
        W2 = jax.random.normal(k4, (D_HID, D_OUT), dtype=jnp.float32) / np.sqrt(D_HID)
        b2 = jnp.zeros((D_OUT,), dtype=jnp.float32)
        return {'x': x, 'edge_index': edge_index, 'W1': W1, 'b1': b1, 'W2': W2, 'b2': b2}
    _L1_gnn_all = _L1_gnn_setup()
    _L1_gnn_in = {k: v for k, v in _L1_gnn_all.items() if k in ('W1', 'b1', 'W2', 'b2')}
    del _L1_gnn_all
    return {'x': x, 'src': src, 'dst': dst, 'edge_weight': edge_weight, 'L0_gnn_W0': _L0_gnn_in['W0'], 'L0_gnn_b0': _L0_gnn_in['b0'], 'L0_gnn_W1': _L0_gnn_in['W1'], 'L0_gnn_b1': _L0_gnn_in['b1'], 'L1_gnn_W1': _L1_gnn_in['W1'], 'L1_gnn_b1': _L1_gnn_in['b1'], 'L1_gnn_W2': _L1_gnn_in['W2'], 'L1_gnn_b2': _L1_gnn_in['b2']}

def reference(x, src, dst, edge_weight, L0_gnn_W0, L0_gnn_b0, L0_gnn_W1, L0_gnn_b1, L1_gnn_W1, L1_gnn_b1, L1_gnn_W2, L1_gnn_b2):
    import jax
    import jax.numpy as jnp

    def _L0_gnn_ref(x, edge_index, edge_weight, W0, b0, W1, b1):
        import jax, jax.numpy as jnp
        import numpy as np
        N_NODES = 3125
        N_EDGES = 50000
        F_IN = 64
        F_HID = 64
        CURV = 1.0
        MIN_NORM = 1e-15
        PROJ_EPS = 0.004

        def _artanh(x):
            x = jnp.clip(x, -1.0 + 1e-07, 1.0 - 1e-07)
            return 0.5 * (jnp.log1p(x) - jnp.log1p(-x))

        def _norm(x):
            return jnp.sqrt(jnp.clip(jnp.sum(x * x, axis=-1, keepdims=True), MIN_NORM))

        def proj(x, c):
            maxnorm = (1.0 - PROJ_EPS) / jnp.sqrt(c)
            n = _norm(x)
            return jnp.where(n > maxnorm, x / n * maxnorm, x)

        def expmap0(u, c):
            sc = jnp.sqrt(c)
            n = _norm(u)
            return jnp.tanh(sc * n) * u / (sc * n)

        def logmap0(p, c):
            sc = jnp.sqrt(c)
            n = _norm(p)
            return _artanh(sc * n) * p / (sc * n)

        def mobius_add(x, y, c):
            x2 = jnp.sum(x * x, -1, keepdims=True)
            y2 = jnp.sum(y * y, -1, keepdims=True)
            xy = jnp.sum(x * y, -1, keepdims=True)
            num = (1.0 + 2.0 * c * xy + c * y2) * x + (1.0 - c * x2) * y
            den = 1.0 + 2.0 * c * xy + c * c * x2 * y2
            return num / jnp.clip(den, MIN_NORM)

        def mobius_matvec(M, x, c):
            sc = jnp.sqrt(c)
            xn = _norm(x)
            mx = x @ M.T
            mxn = _norm(mx)
            res = jnp.tanh(mxn / xn * _artanh(sc * xn)) * mx / (mxn * sc)
            zero = jnp.all(mx == 0, axis=-1, keepdims=True)
            return jnp.where(zero, jnp.zeros_like(res), res)

        def hyp_linear(x, W, b, c):
            res = proj(mobius_matvec(W, x, c), c)
            hyp_b = proj(expmap0(b.reshape(1, -1), c), c)
            return proj(mobius_add(res, hyp_b, c), c)

        def hyp_agg(x, src, dst, w, c, n_nodes):
            xt = logmap0(x, c)
            msg = xt[src] * w[:, None]
            agg = jax.ops.segment_sum(msg, dst, num_segments=n_nodes)
            return proj(expmap0(agg, c), c)

        def hyp_act(x, c_in, c_out):
            xt = jax.nn.relu(logmap0(x, c_in))
            return proj(expmap0(xt, c_out), c_out)

        def hgnn_layer(x, W, b, src, dst, w, c_in, c_out, n_nodes):
            h = hyp_linear(x, W, b, c_in)
            h = hyp_agg(h, src, dst, w, c_in, n_nodes)
            return hyp_act(h, c_in, c_out)
        src, dst = (edge_index[0], edge_index[1])
        h = proj(expmap0(x, CURV), CURV)
        h = hgnn_layer(h, W0, b0, src, dst, edge_weight, CURV, CURV, N_NODES)
        h = hgnn_layer(h, W1, b1, src, dst, edge_weight, CURV, CURV, N_NODES)
        return h

    def _L1_gnn_ref(x, edge_index, W1, b1, W2, b2):
        import jax, jax.numpy as jnp
        import numpy as np
        N_NODES = 50000
        N_EDGES = 25000
        D_FEAT = 64
        D_HID = 128
        D_OUT = 64
        n = x.shape[0]
        loops = jnp.arange(n, dtype=edge_index.dtype)
        src = jnp.concatenate([edge_index[0], loops])
        dst = jnp.concatenate([edge_index[1], loops])
        edge_features = jnp.concatenate([x[src], x[dst]], axis=-1)
        h = jax.nn.relu(edge_features @ W1 + b1)
        edge_out = h @ W2 + b2
        agg = jax.ops.segment_sum(edge_out, dst, num_segments=n)
        counts = jax.ops.segment_sum(jnp.ones_like(dst, dtype=edge_out.dtype), dst, num_segments=n)
        return agg / jnp.clip(counts, 1.0)[:, None]
    edge_index = jnp.stack([src, dst])
    h = jnp.maximum(_layernorm(x, axis=-1), 0.0)
    x = x + _L0_gnn_ref(h, edge_index, edge_weight, L0_gnn_W0, L0_gnn_b0, L0_gnn_W1, L0_gnn_b1)
    h = jnp.maximum(_layernorm(x, axis=-1), 0.0)
    x = x + _L1_gnn_ref(h, edge_index, L1_gnn_W1, L1_gnn_b1, L1_gnn_W2, L1_gnn_b2)
    return x

_drawn_inputs = setup_inputs


def setup_inputs(seed=0):
    import zlib

    import numpy as np

    out = dict(_drawn_inputs(seed))
    spreads = {'L1_gnn_b1': (0.0, 0.1), 'L1_gnn_b2': (0.0, 0.1)}
    factors = {}
    for name, (base, spread) in spreads.items():
        noise = np.random.default_rng([zlib.crc32(name.encode()), seed]).standard_normal(out[name].shape)
        drawn = base * np.exp(spread * noise) if base else spread * noise
        out[name] = jnp.asarray(drawn.astype(out[name].dtype))
    for name, factor in factors.items():
        out[name] = (out[name] * factor).astype(out[name].dtype)
    return out
```

```python
import concourse.bass as bass
from concourse import mybir
from contextlib import ExitStack

N = 3125
F = 64
HID = 128
E = 103125
PN = 125
NB = N // PN
TE = 128
GT = 16
GE = GT * TE
NG = -(-E // GE)
NP = (NG - 1) // 2
TILES = NG * GT
LAST = -(-(E - (NG - 1) * GE) // TE)
W = 72
NV = -(-N // W)
NW = N + W
PRIMED = 1
MIN_NORM = 1e-15
MAXNORM = 1.0 - 0.004
CLIP = 1.0 - 1e-07
ARTANH = [1.0 / k for k in (13, 11, 9, 7, 5, 3)]
SMALL = 0.3


def gnn_kernel(nc, x, src_t, dst_t, w_t, dst_row, w0T, b0, w1T, b1, W1, eb1, W2, eb2, out):
    f32, bf16, i32 = mybir.dt.float32, mybir.dt.bfloat16, mybir.dt.int32
    ALU = mybir.AluOpType
    ACT = mybir.ActivationFunctionType
    X = mybir.AxisListType.X
    ctx = ExitStack()
    with ctx:
        def sb(name, shape, dt=f32):
            return ctx.enter_context(nc.sbuf_tensor(name, shape, dt))

        def sem(name):
            return ctx.enter_context(nc.semaphore(name))

        xt_d = nc.dram_tensor("xt_table", (N, F), f32, kind="Internal").ap()
        p_d = nc.dram_tensor("p_table", (N, HID), f32, kind="Internal").ap()
        q_d = nc.dram_tensor("q_table", (NW, 3 * HID), bf16, kind="Internal").ap()

        dstI = sb("dstI", [128, TILES], i32)
        dstT = sb("dstT", [128, TILES])
        wT = sb("wT", [128, TILES])
        x_sb = sb("x_sb", [PN, NB, F])
        A = sb("A", [PN, NB, F])
        B = sb("B", [PN, NB, F])
        C = sb("C", [PN, NB, F])
        HT = sb("HT", [F + 1, NB, PN])
        aggT = sb("aggT", [F + 1, NW])
        RT = sb("RT", [HID, NW])
        SQ = RT[0:F, 0:N].rearrange("f (b p) -> f b p", b=NB)
        PQ = sb("PQ", [PN, NB, HID])
        Q3 = sb("Q3", [PN, NB, 3, HID], bf16)
        w0_sb = sb("w0_sb", [F, F])
        w1_sb = sb("w1_sb", [F, F])
        W1a = sb("W1a", [F, HID])
        W1b = sb("W1b", [F + 1, HID])
        W2_sb = sb("W2_sb", [HID, F])
        yb = sb("yb", [128, 2, F])
        ysq = sb("ysq", [128, 2, F])
        b2b = sb("b2b", [128, F])
        ident = sb("ident", [128, 128])
        ones = sb("ones", [128, 128])
        rampi = sb("rampi", [128, W], i32)
        ramp = sb("ramp", [128, W])
        colpi = sb("colpi", [128, 1], i32)
        colp = sb("colp", [128, 1])
        vtabi = sb("vtabi", [128, NV], i32)
        vtab = sb("vtab", [128, NV])
        basef = sb("basef", [128, NG])
        tabi = sb("tabi", [1, NG], i32)
        flag = sb("flag", [128, 4])
        nvi = sb("nvi", [1, 1], i32)
        okm = sb("okm", [128, 2, TILES])
        rows = sb("rows", [128, 16, NB])
        arg = sb("arg", [128, NB])
        ans = sb("ans", [128, NB])
        idx = [sb(f"idx{k}", [128, GT], i32) for k in range(2)]
        GP = [sb(f"GP{k}", [128, GT, HID]) for k in range(2)]
        dloc = [sb(f"dloc{k}", [128, GT]) for k in range(2)]
        O = [sb(f"O{k}", [128, GT, W]) for k in range(2)]
        H = [sb(f"H{k}", [128, GT, HID]) for k in range(2)]
        G = [GP[k][:, 0:GT // 2, :].rearrange("p t (a f) -> p (t a) f", a=2) for k in range(2)]
        M = [H[k][:, :, :].rearrange("p t h -> p (t h)")[:, 0:GT * (F + 1)].rearrange("p (t f) -> p t f", t=GT)
             for k in range(2)]
        dbc = [sb(f"dbc{k}", [W, GE], i32) for k in range(2)]
        cloc = [sb(f"cloc{k}", [W, 1]) for k in range(2)]
        OT = [sb(f"OT{k}", [W, GE], bf16) for k in range(2)]
        qw = [sb(f"qw{k}", [W, 3, HID], bf16) for k in range(2)]

        PS = ctx.enter_context(nc.psum_tensor("PS", [128, 4096], f32))
        MU = PS[0:PN, 0:NB * F].rearrange("p (b f) -> p b f", b=NB)
        agg_ps = [PS[0:F + 1, 3072 + 512 * k:3072 + 512 * k + W] for k in range(2)]
        r_ps = [PS[:, 3072 + 512 * k:3072 + 512 * k + W] for k in range(2)]
        t_ps = [PS[:, 1024 * k:1024 * k + 1024].rearrange("p (t h) -> p t h", h=HID) for k in range(2)]
        row_ps = [PS[0:PN, 2048 + 512 * k:2048 + 512 * k + NB] for k in range(2)]

        edges_in, x_in, weights_in = sem("edges_in"), sem("x_in"), sem("weights_in")
        consts_set = sem("consts_set")
        vec = sem("vec")
        asked, answered = sem("asked"), sem("answered")
        act = sem("act")
        base_ps, table_set = sem("base_ps"), sem("table_set")
        norm_in, ht_ps, ht_set, mu_ps, mu_read = (sem("norm_in"), sem("ht_ps"), sem("ht_set"),
                                                  sem("mu_ps"), sem("mu_read"))
        sq_set, rows_ps = sem("sq_set"), sem("rows_ps")
        square_asked, square_set = sem("square_asked"), sem("square_set")
        xt_set, xt_stored = sem("xt_set"), sem("xt_stored")
        agg_zero = sem("agg_zero")
        h1_ps, p_ps, p_set, q_ps, q_set = sem("h1_ps"), sem("p_ps"), sem("p_set"), sem("q_ps"), sem("q_set")
        p_stored, q3_set, q_stored = sem("p_stored"), sem("q3_set"), sem("q_stored")
        self_ps, self_set = sem("self_ps"), sem("self_set")
        fin_ps, fin_set, out_stored = sem("fin_ps"), sem("fin_set"), sem("out_stored")
        q_tail = sem("q_tail")
        begun = sem("begun")

        def steps(name):
            kinds = ("idx_in", "gathered", "onehot_set", "dloc_set", "msg_set", "sum_ps", "sum_added",
                     "dst_in", "qwin_in", "cloc_set", "onehotT_set", "t_ps", "t_added", "relu_set")
            return {k: [sem(f"{name}_{k}{i}") for i in range(2)] for k in kinds[:7 if name != "edge" else 14]}

        passes = [steps("agg0"), steps("agg1")]
        edge = steps("edge")

        block = ctx.enter_context(nc.Block())

        def prime(eng, *names):
            for s in (*passes, edge):
                for name in names:
                    for one in s.get(name, ()):
                        eng.sem_inc(one, PRIMED)

        def over_steps(eng, step):
            eng.wait_ge(table_set, 1)
            nv = eng.value_load(nvi[0:1, 0:1], min_val=1, max_val=NV)
            with eng.Fori(0, NP) as j:
                with eng.Fori(0, nv) as v:
                    for k in range(2):
                        step(k, j * nv + v, 2 * j + k, v, GT, j * nv)
            with eng.Fori(0, nv) as v:
                step(0, nv * NP + v, NG - 1, v, LAST, nv * NP)

        def window(eng, group, v):
            first = eng.value_load(tabi[0:1, bass.ds(group, 1)], min_val=0, max_val=N - 1) + v * W
            return nc.s_assert_within(first, 0, N - 1, 
                                      skip_runtime_bounds_check_because="v > 0 only where the bases are 0")

        @block.sync
        def _(sp):
            sp.dma_start(x_sb[:, :, :], x.rearrange("(p b) f -> p b f", b=NB)).then_inc(x_in, 16)
            for t, d in ((dstI, dst_t), (wT, w_t)):
                sp.dma_start(t[:, :], d[:, :]).then_inc(edges_in, 16)
            sp.dma_start(yb[:, 0, :], b0.partition_broadcast(128)).then_inc(weights_in, 16)
            sp.dma_start(yb[:, 1, :], b1.partition_broadcast(128)).then_inc(weights_in, 16)
            sp.dma_start(b2b[:, :], eb2.partition_broadcast(128)).then_inc(weights_in, 16)
            sp.dma_start(w0_sb[:, :], w0T[:, :]).then_inc(weights_in, 16)
            sp.dma_start(w1_sb[:, :], w1T[:, :]).then_inc(weights_in, 16)
            sp.dma_start(W1a[:, :], W1[0:F, :]).then_inc(weights_in, 16)
            sp.dma_start(W1b[0:F, :], W1[F:2 * F, :]).then_inc(weights_in, 16)
            sp.dma_start(W1b[F:F + 1, :], eb1.partition_broadcast(1)).then_inc(weights_in, 16)
            sp.dma_start(W2_sb[:, :], W2[:, :]).then_inc(weights_in, 16)
            sp.wait_ge(consts_set, 10)
            sp.dma_start(q_d[N:NW, :], OT[1][:, 0:3 * HID]).then_inc(q_tail, 16)

            def load_indices(sems, freed, each):
                def step(k, m, group, v, tiles, whole):
                    sp.wait_ge(sems[freed][k], each * m + PRIMED)
                    sp.dma_start(idx[k][:, :], src_t[:, bass.ds(group * GT, GT)]).then_inc(sems["idx_in"][k], 16)
                return step

            for l in range(2):
                sp.wait_ge(xt_set, l + 1)
                sp.dma_start(xt_d.rearrange("(p b) f -> p b f", b=NB), A[:, :, :]).then_inc(xt_stored, 16)
                over_steps(sp, load_indices(passes[l], "msg_set", 1))
            sp.wait_ge(p_set, 1)
            sp.dma_start(p_d.rearrange("(p b) f -> p b f", b=NB), PQ[:, :, :]).then_inc(p_stored, 16)
            sp.wait_ge(q3_set, 1)
            sp.dma_start(q_d[0:N, :].rearrange("(p b) f -> p (b f)", b=NB),
                         Q3[:, :, :, :].rearrange("p b c f -> p (b c f)")).then_inc(q_stored, 16)
            sp.wait_ge(q_stored, 16)
            sp.wait_ge(q_tail, 16)
            sp.wait_ge(table_set, 1)

            def load_windows(k, m, group, v, tiles, whole):
                load_indices(edge, "relu_set", 2)(k, m, group, v, tiles, whole)
                base = window(sp, group, v)
                sp.wait_ge(edge["onehotT_set"][k], m + PRIMED)
                sp.dma_start(dbc[k][:, :], dst_row[bass.ds(group * GE, GE)].partition_broadcast(W))\
                    .then_inc(edge["dst_in"][k], 16)
                sp.wait_ge(edge["t_ps"][k], 2 * m + PRIMED)
                sp.dma_start(qw[k][:, :, :].rearrange("p c h -> p (c h)"), q_d[bass.ds(base, W), :])\
                    .then_inc(edge["qwin_in"][k], 16)

            over_steps(sp, load_windows)
            sp.wait_ge(fin_set, 1)
            sp.dma_start(out.rearrange("(p b) f -> p b f", b=NB), A[:, :, :]).then_inc(out_stored, 16)
            sp.wait_ge(out_stored, 16)
            sp.wait_ge(p_stored, 16)
            sp.wait_ge(xt_stored, 32)

        @block.gpsimd
        def _(pool):
            pool.memset(ones[:, :], 1.0).then_inc(consts_set, 1)
            pool.memset(ident[:, :], 0.0).then_inc(consts_set, 1)
            pool.iota(rampi[:, :], [[1, W]], base=0, channel_multiplier=0).then_inc(consts_set, 1)
            pool.iota(colpi[:, :], [[0, 1]], base=0, channel_multiplier=1).then_inc(consts_set, 1)
            pool.iota(vtabi[:, :], [[W, NV]], base=0, channel_multiplier=0).then_inc(consts_set, 1)
            for k in range(2):
                pool.memset(M[k][:, :, F:F + 1], 1.0).then_inc(consts_set, 1)
            pool.wait_ge(consts_set, 9)
            pool.affine_select(out=ident[:, :], in_=ident[:, :], compare_op=ALU.not_equal, fill=1.0,
                               base=0, pattern=[[-1, 128]], channel_multiplier=1).then_inc(consts_set, 1)

            def gather(sems, table, dest, freed, each):
                def step(k, m, group, v, tiles, whole):
                    pool.wait_ge(sems["idx_in"][k], 16 * (m + 1))
                    pool.wait_ge(sems[freed][k], each * m + PRIMED)
                    pool.sem_inc(begun, 1)
                    for t in range(tiles):
                        pool.indirect_dma_start(dest[k][:, t, :], None, table[:, :],
                                                bass.IndirectOffsetOnAxis(ap=idx[k][:, t:t + 1], axis=0))\
                            .then_inc(sems["gathered"][k], 16 * (GT - tiles + 1 if t == tiles - 1 else 1))
                return step

            pool.wait_ge(table_set, 1)
            for l in range(2):
                pool.wait_ge(xt_stored, 16 * (l + 1))
                over_steps(pool, gather(passes[l], xt_d, G, "msg_set", 1))
            pool.wait_ge(p_stored, 16)
            over_steps(pool, gather(edge, p_d, GP, "relu_set", 2))

        Y_FUNCS = [ACT.Sqrt, ACT.Tanh, ACT.Sqrt]
        EXP_FUNCS = [ACT.Sqrt, ACT.Tanh, ACT.Sqrt]
        LINEAR_FUNCS = [ACT.Sqrt, ACT.Ln, ACT.Sqrt, ACT.Tanh, ACT.Sqrt]
        LOG_FUNCS = [ACT.Sqrt, ACT.Sqrt, ACT.Ln]

        @block.scalar
        def _(sc):
            done = {"answers": 0, "squares": 0, "chain": 0}

            def answer(funcs):
                for fn in funcs:
                    done["answers"] += 1
                    sc.wait_ge(asked, done["answers"])
                    nc.scalar.activation(ans[0:PN, :], arg[0:PN, :], fn).then_inc(answered, 1)

            def square(dst, source):
                done["squares"] += 1
                sc.wait_ge(square_asked, done["squares"])
                nc.scalar.activation(dst, source, ACT.Square).then_inc(square_set, 1)

            def copy_ht():
                sc.wait_ge(ht_ps, 1)
                for c in range(0, NB, 4):
                    n = min(4, NB - c)
                    ps = PS[0:F, 128 * c:128 * c + 500][:, 0:PN * n].rearrange("f (b p) -> f b p", b=n)
                    last = nc.scalar.activation(HT[0:F, c:c + n, :], ps, ACT.Copy)
                return last

            prime(sc, "relu_set")
            answer([ACT.Sqrt])
            sc.wait_ge(consts_set, 10)
            copy_ht().then_inc(ht_set, 1)
            answer(Y_FUNCS)
            answer(EXP_FUNCS)
            for l in range(2):
                sc.wait_ge(mu_ps, l + 1)
                square(B[:, :, :], MU)
                answer(LINEAR_FUNCS)
                square(B[:, :, :], A[:, :, :])
                answer(LOG_FUNCS)
                sc.wait_ge(sq_set, 2 * l + 1)
                nc.scalar.activation(HT[0:F, :, :], aggT[0:F, 0:N].rearrange("f (p b) -> f b p", b=NB),
                                     ACT.Relu).then_inc(ht_set, 1)
                answer(EXP_FUNCS)
                answer([ACT.Sqrt, ACT.Ln])
                answer(EXP_FUNCS)
            answer([ACT.Sqrt])
            sc.wait_ge(h1_ps, 1)
            for c in range(0, NB, 4):
                n = min(4, NB - c)
                ps = PS[0:F, 128 * c:128 * c + 500][:, 0:PN * n].rearrange("f (b p) -> f b p", b=n)
                last = nc.scalar.activation(HT[0:F, c:c + n, :], ps, ACT.Copy)
            last.then_inc(ht_set, 1)
            sc.wait_ge(p_ps, 1)
            nc.scalar.activation(PQ[:, :, :], PS[0:PN, 0:NB * HID].rearrange("p (b h) -> p b h", b=NB),
                                 ACT.Copy).then_inc(p_set, 1)
            sc.wait_ge(self_ps, 1)
            for c in range(0, NB, 4):
                n = min(4, NB - c)
                ps = PS[:, 128 * c:128 * c + 500][:, 0:PN * n].rearrange("f (b p) -> f b p", b=n)
                last = nc.scalar.activation(RT[:, 0:N].rearrange("f (p b) -> f b p", b=NB)[:, c:c + n, :],
                                            ps, ACT.Relu)
            last.then_inc(self_set, 1)

            def edge_step(k, m, group, v, tiles, whole):
                for half in range(2):
                    sc.wait_ge(edge["t_added"][k], 2 * m + half + 1 + PRIMED)
                    if half == 0:
                        sc.wait_ge(edge["sum_ps"][k], m + PRIMED)
                    cut = slice(8 * half, 8 * half + 8)
                    nc.scalar.activation(H[k][:, cut, :], GP[k][:, cut, :], ACT.Relu)\
                        .then_inc(edge["relu_set"][k], 1)
            over_steps(sc, edge_step)

        @block.vector
        def _(ve):
            n_vec = [0]
            n_ask = [0]
            n_square = [0]

            def link(ins):
                n_vec[0] += 1
                ins.then_inc(vec, 1)
                ve.wait_ge(vec, n_vec[0])

            def ask(expr):
                n_ask[0] += 1
                expr.then_inc(asked, 1)
                ve.wait_ge(answered, n_ask[0])

            def ask_square():
                n_square[0] += 1
                ve.sem_inc(square_asked, 1)

            def squares_ready():
                ve.wait_ge(square_set, n_square[0])

            P_ = slice(0, PN)

            def row(i):
                return rows[P_, i, :]

            a_, s_ = arg[P_, :], ans[P_, :]
            SS, S, NX, ATN, T, Q_, Z, SSP, T1, T2, T3, AC, BC, MASK = range(14)

            def tt(o, i, j, op):
                link(ve.tensor_tensor(o, i, j, op))

            def ts(o, i, c1, op1, c2=None, op2=ALU.bypass):
                link(ve.tensor_scalar(o, i, c1, c2, op1, op2))

            def norm(o, ss):
                ask(ve.tensor_scalar(a_, ss, MIN_NORM, None, ALU.max))
                link(ve.tensor_copy(o, s_))

            def over(o, num, den):
                link(ve.reciprocal(row(T1), den))
                tt(o, num, row(T1), ALU.mult)

            def expmap(s, ss):
                norm(row(T2), ss)
                ask(ve.tensor_copy(a_, row(T2)))
                over(s, s_, row(T2))

            def project(s, ss):
                tt(row(T2), s, s, ALU.mult)
                tt(row(T2), row(T2), ss, ALU.mult)
                norm(row(T3), row(T2))
                link(ve.reciprocal(row(T1), row(T3)))
                ts(row(T1), row(T1), MAXNORM, ALU.mult, 1.0, ALU.min)
                tt(s, s, row(T1), ALU.mult)

            def artanh_ratio(o, n):
                ts(row(T3), n, CLIP, ALU.min)
                ts(row(T1), row(T3), -1.0, ALU.mult, 1.0, ALU.add)
                link(ve.reciprocal(row(T1), row(T1)))
                ts(row(T2), row(T3), 1.0, ALU.add)
                ask(ve.tensor_tensor(a_, row(T1), row(T2), ALU.mult))
                link(ve.reciprocal(row(T1), n))
                link(ve.scalar_tensor_tensor(row(T1), s_, 0.5, row(T1), ALU.mult, ALU.mult))
                tt(row(T2), row(T3), row(T3), ALU.mult)
                ts(o, row(T2), ARTANH[0], ALU.mult)
                for c in ARTANH[1:]:
                    link(ve.scalar_tensor_tensor(o, o, c, row(T2), ALU.add, ALU.mult))
                ts(o, o, 1.0, ALU.add)
                ts(row(T2), row(T3), SMALL, ALU.is_lt)
                tt(o, o, row(T2), ALU.mult)
                ts(row(T2), row(T3), SMALL, ALU.is_ge)
                tt(row(T1), row(T1), row(T2), ALU.mult)
                tt(o, o, row(T1), ALU.add)

            def wide(r):
                return r.unsqueeze(2).broadcast_to([PN, NB, F])

            def layer_norm(dst, source):
                link(ve.tensor_reduce(row(T1), source, X, ALU.add))
                ts(row(T1), row(T1), 1.0 / F, ALU.mult)
                tt(dst, source, wide(row(T1)), ALU.subtract)
                tt(C[:, :, :], dst, dst, ALU.mult)
                link(ve.tensor_reduce(row(T2), C[:, :, :], X, ALU.add))
                ask(ve.tensor_scalar(a_, row(T2), 1.0 / F, 1e-5, ALU.mult, ALU.add))
                link(ve.reciprocal(row(T1), s_))
                link(ve.scalar_tensor_tensor(dst, dst, 0.0, wide(row(T1)), ALU.max, ALU.mult))

            def linear(l):
                y = yb[P_, l, :].unsqueeze(1).broadcast_to([PN, NB, F])
                y2 = flag[P_, 2 + l:3 + l]
                ve.wait_ge(mu_ps, l + 1)
                tt(C[:, :, :], MU, y, ALU.mult)
                ask_square()
                link(ve.tensor_reduce(row(Z), C[:, :, :], X, ALU.add))
                squares_ready()
                link(ve.tensor_reduce(row(Q_), B[:, :, :], X, ALU.add))
                tt(row(T), row(S), row(S), ALU.mult)
                tt(row(T1), row(T), row(SS), ALU.mult)
                norm(row(NX), row(T1))
                artanh_ratio(row(ATN), row(NX))
                tt(row(T1), row(T), row(Q_), ALU.mult)
                norm(row(T), row(T1))
                ask(ve.tensor_tensor(a_, row(T), row(ATN), ALU.mult))
                over(row(T), s_, row(T))
                tt(row(T), row(T), row(S), ALU.mult)
                project(row(T), row(Q_))
                tt(row(T1), row(T), row(T), ALU.mult)
                tt(row(T1), row(T1), row(Q_), ALU.mult)
                ts(row(BC), row(T1), -1.0, ALU.mult, 1.0, ALU.add)
                tt(row(T2), row(T), row(Z), ALU.mult)
                ts(row(T2), row(T2), 2.0, ALU.mult, 1.0, ALU.add)
                link(ve.scalar_tensor_tensor(row(T3), row(T1), y2, row(T2), ALU.mult, ALU.add))
                ts(row(T3), row(T3), MIN_NORM, ALU.max)
                link(ve.reciprocal(row(T3), row(T3)))
                link(ve.scalar_tensor_tensor(row(AC), row(T2), y2, row(T), ALU.add, ALU.mult))
                tt(row(AC), row(AC), row(T3), ALU.mult)
                tt(row(BC), row(BC), row(T3), ALU.mult)
                tt(A[:, :, :], MU, wide(row(AC)), ALU.mult)
                tt(C[:, :, :], y, wide(row(BC)), ALU.mult)
                tt(A[:, :, :], A[:, :, :], C[:, :, :], ALU.add)
                ask_square()
                squares_ready()
                link(ve.tensor_reduce(row(Q_), B[:, :, :], X, ALU.add))
                link(ve.memset(row(S), 1.0))
                project(row(S), row(Q_))
                tt(row(T2), row(S), row(S), ALU.mult)
                tt(row(T2), row(T2), row(Q_), ALU.mult)
                norm(row(NX), row(T2))
                artanh_ratio(row(ATN), row(NX))
                tt(row(S), row(S), row(ATN), ALU.mult)
                ve.tensor_tensor(A[:, :, :], A[:, :, :], wide(row(S)), ALU.mult).then_inc(xt_set, 1)

            prime(ve, "onehot_set", "msg_set", "sum_added", "onehotT_set", "t_added")
            ve.memset(HT[F:F + 1, :, :], 1.0).then_inc(consts_set, 1)
            ve.memset(OT[1][:, 0:3 * HID], 0.0).then_inc(consts_set, 1)
            ve.wait_ge(edges_in, 32)
            ve.wait_ge(consts_set, 10)
            link(ve.tensor_copy(dstT[:, :], dstI[:, :]))
            ve.tensor_copy(ramp[:, :], rampi[:, :])
            ve.tensor_copy(colp[:, :], colpi[:, :])
            link(ve.tensor_copy(vtab[:, :], vtabi[:, :]))
            ve.wait_ge(base_ps, 1)
            link(ve.tensor_scalar(basef[:, :], PS[:, 3584:3584 + NG], 0.0, None, ALU.max))
            by_group = dstT[:, :].rearrange("p (g t) -> p g t", t=GT)
            off = okm[:, 0, :].rearrange("p (g t) -> p g t", t=GT)
            tt(off, by_group, basef[:, :].unsqueeze(2).broadcast_to([128, NG, GT]), ALU.subtract)
            ts(okm[:, 1, :], okm[:, 0, :], float(W), ALU.is_lt)
            link(ve.scalar_tensor_tensor(okm[:, 0, :], okm[:, 0, :], 0.0, okm[:, 1, :], ALU.is_ge, ALU.mult))
            ve.tensor_reduce(flag[:, 0:1], okm[:, 0, :], X, ALU.add).then_inc(norm_in, 1)
            ve.wait_ge(base_ps, 2)
            link(ve.tensor_scalar(flag[:, 1:2], PS[:, 3072:3073], float(E), None, ALU.is_equal))
            link(ve.tensor_scalar(nvi[0:1, 0:1], flag[0:1, 1:2], float(1 - NV), float(NV), ALU.mult, ALU.add))
            link(ve.tensor_scalar(basef[:, :], basef[:, :], flag[:, 1:2], None, ALU.mult))
            ve.tensor_copy(tabi[0:1, :], basef[0:1, :]).then_inc(table_set, 1)

            ve.wait_ge(x_in, 16)
            layer_norm(A[:, :, :], x_sb[:, :, :])
            ve.wait_ge(vec, n_vec[0])
            ve.sem_inc(norm_in, 1)
            tt(C[:, :, :], A[:, :, :], A[:, :, :], ALU.mult)
            link(ve.tensor_reduce(row(SS), C[:, :, :], X, ALU.add))
            ve.wait_ge(weights_in, 16 * 9)
            tt(ysq[:, :, :], yb[:, :, :], yb[:, :, :], ALU.mult)
            link(ve.memset(row(Q_), 1.0))
            link(ve.tensor_reduce(rows[P_, Q_, 0:2], ysq[P_, :, :], X, ALU.add))
            expmap(row(S), row(Q_))
            project(row(S), row(Q_))
            tt(yb[P_, :, :], yb[P_, :, :], rows[P_, S, 0:2].unsqueeze(2).broadcast_to([PN, 2, F]), ALU.mult)
            tt(ysq[P_, :, :], yb[P_, :, :], yb[P_, :, :], ALU.mult)
            link(ve.tensor_reduce(flag[P_, 2:4], ysq[P_, :, :], X, ALU.add))
            expmap(row(S), row(SS))
            project(row(S), row(SS))

            link(ve.memset(aggT[:, :], 0.0))

            def aggregate(l):
                s = passes[l]

                def step(k, m, group, v, tiles, whole):
                    ve.wait_ge(s["onehot_set"][k], m + PRIMED)
                    cols = bass.ds(group * GT, GT)
                    nc.vector.tensor_scalar(dloc[k][:, :], dstT[:, cols], basef[:, bass.ds(group, 1)],
                                            vtab[:, bass.ds(v, 1)], ALU.subtract, ALU.subtract)\
                        .then_inc(s["dloc_set"][k], 1)
                    ve.wait_ge(s["dloc_set"][k], m + 1)
                    ve.wait_ge(s["sum_ps"][k], m + PRIMED)
                    nc.vector.tensor_tensor(O[k][:, :, :], ramp[:, :].unsqueeze(1).broadcast_to([128, GT, W]),
                                            dloc[k][:, :].unsqueeze(2).broadcast_to([128, GT, W]),
                                            ALU.is_equal).then_inc(s["onehot_set"][k], 1)
                    ve.wait_ge(s["gathered"][k], 16 * GT * (m + 1))
                    nc.vector.tensor_tensor(M[k][:, 0:tiles, 0:F], G[k][:, 0:tiles, :],
                                            wT[:, bass.ds(group * GT, tiles)].unsqueeze(2)
                                            .broadcast_to([128, tiles, F]),
                                            ALU.mult).then_inc(s["msg_set"][k], 1)
                    base = window(ve, group, v)
                    ve.wait_ge(s["sum_ps"][k], m + 1 + PRIMED)
                    if tiles == GT:
                        ve.wait_ge(s["sum_added"][1 - k], m + k + PRIMED)
                    else:
                        ve.wait_ge(s["sum_added"][1], whole + PRIMED)
                        ve.wait_ge(s["sum_added"][0], m + PRIMED)
                    win = aggT[:, bass.ds(base, W)]
                    nc.vector.tensor_tensor(win, win, agg_ps[k], ALU.add).then_inc(s["sum_added"][k], 1)
                over_steps(ve, step)
                nv = ve.value_load(nvi[0:1, 0:1], min_val=1, max_val=NV)
                ve.wait_ge(s["sum_added"][0], nv * (NP + 1) + PRIMED)

            def act_scales(l):
                blocks = aggT[0:F, 0:N].rearrange("f (p b) -> f b p", b=NB)
                ve.tensor_tensor(SQ[:, :, :], blocks, blocks, ALU.mult).then_inc(sq_set, 1)
                ve.wait_ge(rows_ps, 2 * l + 1)
                link(ve.tensor_copy(row(Q_), row_ps[0]))
                ve.wait_ge(ht_set, l + 2)
                ve.tensor_tensor(SQ[:, :, :], HT[0:F, :, :], HT[0:F, :, :], ALU.mult).then_inc(sq_set, 1)
                expmap(row(S), row(Q_))
                project(row(S), row(Q_))
                tt(row(T2), row(S), row(S), ALU.mult)
                tt(row(T2), row(T2), row(Q_), ALU.mult)
                norm(row(NX), row(T2))
                artanh_ratio(row(ATN), row(NX))
                tt(row(ATN), row(S), row(ATN), ALU.mult)
                ve.wait_ge(rows_ps, 2 * l + 2)
                link(ve.tensor_copy(row(SS), row_ps[1]))
                tt(row(T3), row(ATN), row(ATN), ALU.mult)
                tt(row(Q_), row(T3), row(SS), ALU.mult)
                expmap(row(S), row(Q_))
                project(row(S), row(Q_))
                tt(row(S), row(S), row(ATN), ALU.mult)

            for l in range(2):
                linear(l)
                aggregate(l)
                act_scales(l)
                if l == 0:
                    link(ve.memset(aggT[:, :], 0.0))

            ve.wait_ge(mu_ps, 3)
            tt(A[:, :, :], MU, wide(row(S)), ALU.mult)
            tt(x_sb[:, :, :], x_sb[:, :, :], A[:, :, :], ALU.add)
            layer_norm(A[:, :, :], x_sb[:, :, :])
            ve.sem_inc(norm_in, 1)
            link(ve.tensor_copy(row(Z), PS[0:PN, 3584:3584 + NB]))
            ts(row(Z), row(Z), 1.0, ALU.add, 1.0, ALU.max)
            link(ve.reciprocal(row(Z), row(Z)))
            tt(x_sb[:, :, :], x_sb[:, :, :], b2b[P_, :].unsqueeze(1).broadcast_to([PN, NB, F]), ALU.add)
            link(ve.memset(RT[:, N:NW], 0.0))
            ve.wait_ge(q_ps, 1)
            ve.wait_ge(p_stored, 16)
            ps_q = PS[0:PN, 0:NB * HID].rearrange("p (b h) -> p b h", b=NB)
            link(ve.tensor_copy(Q3[:, :, 0, :], ps_q))
            tt(PQ[:, :, :], ps_q, Q3[:, :, 0, :], ALU.subtract)
            ve.sem_inc(q_set, 1)
            link(ve.tensor_copy(Q3[:, :, 1, :], PQ[:, :, :]))
            tt(PQ[:, :, :], PQ[:, :, :], Q3[:, :, 1, :], ALU.subtract)
            ve.tensor_copy(Q3[:, :, 2, :], PQ[:, :, :]).then_inc(q3_set, 1)
            ve.wait_ge(self_set, 1)

            def edge_step(k, m, group, v, tiles, whole):
                s = edge
                ve.wait_ge(s["onehot_set"][k], m + PRIMED)
                nc.vector.tensor_scalar(dloc[k][:, :], dstT[:, bass.ds(group * GT, GT)],
                                        basef[:, bass.ds(group, 1)], vtab[:, bass.ds(v, 1)],
                                        ALU.subtract, ALU.subtract).then_inc(s["dloc_set"][k], 1)
                ve.wait_ge(s["onehotT_set"][k], m + PRIMED)
                nc.vector.tensor_scalar(cloc[k][:, :], colp[0:W, :], basef[0:W, bass.ds(group, 1)],
                                        vtab[0:W, bass.ds(v, 1)], ALU.add, ALU.add)\
                    .then_inc(s["cloc_set"][k], 1)
                ve.wait_ge(s["dloc_set"][k], m + 1)
                ve.wait_ge(s["sum_ps"][k], m + PRIMED)
                nc.vector.tensor_tensor(O[k][:, :, :], ramp[:, :].unsqueeze(1).broadcast_to([128, GT, W]),
                                        dloc[k][:, :].unsqueeze(2).broadcast_to([128, GT, W]),
                                        ALU.is_equal).then_inc(s["onehot_set"][k], 1)
                ve.wait_ge(s["dst_in"][k], 16 * (m + 1))
                ve.wait_ge(s["cloc_set"][k], m + 1)
                ve.wait_ge(s["t_ps"][k], 2 * m + PRIMED)
                nc.vector.tensor_scalar(OT[k][:, :], dbc[k][:, :], cloc[k][:, :], None, ALU.is_equal)\
                    .then_inc(s["onehotT_set"][k], 1)
                ve.wait_ge(s["gathered"][k], 16 * GT * (m + 1))
                for half in range(2):
                    ve.wait_ge(s["t_ps"][k], 2 * m + half + 1 + PRIMED)
                    part = GP[k][:, 8 * half:min(8 * half + 8, max(tiles, 8 * half + 1)), :]
                    n = part.shape[1]
                    nc.vector.tensor_tensor(part, part, t_ps[k][:, 0:n, :], ALU.add)\
                        .then_inc(s["t_added"][k], 1)
                base = window(ve, group, v)
                ve.wait_ge(s["sum_ps"][k], m + 1 + PRIMED)
                if tiles == GT:
                    ve.wait_ge(s["sum_added"][1 - k], m + k + PRIMED)
                else:
                    ve.wait_ge(s["sum_added"][1], whole + PRIMED)
                    ve.wait_ge(s["sum_added"][0], m + PRIMED)
                win = RT[:, bass.ds(base, W)]
                nc.vector.tensor_tensor(win, win, r_ps[k], ALU.add).then_inc(s["sum_added"][k], 1)
            over_steps(ve, edge_step)
            nv = ve.value_load(nvi[0:1, 0:1], min_val=1, max_val=NV)
            ve.wait_ge(edge["sum_added"][0], nv * (NP + 1) + PRIMED)
            ve.sem_inc(fin_ps, 1)
            ve.wait_ge(fin_ps, 2)
            tt(A[:, :, :], MU, wide(row(Z)), ALU.mult)
            ve.tensor_tensor(A[:, :, :], A[:, :, :], x_sb[:, :, :], ALU.add).then_inc(fin_set, 1)

        @block.tensor
        def _(pe):
            mm = nc.tensor.matmul
            prime(pe, "sum_ps", "t_ps")

            def transposes():
                for b in range(NB):
                    last = nc.tensor.transpose(PS[0:F, 512 * (b // 4) + PN * (b % 4):
                                                  512 * (b // 4) + PN * (b % 4) + PN],
                                               A[:, b, :], ident[0:PN, 0:PN])
                return last

            def product(weights):
                for b in range(NB):
                    last = mm(MU[:, b, :], HT[0:F, b, :], weights, start=True, stop=True)
                return last

            pe.wait_ge(edges_in, 32)
            pe.wait_ge(consts_set, 10)
            pe.wait_ge(vec, 1)
            mm(PS[:, 3584:3584 + NG], ones[0:1, :], dstT[0:1, :].rearrange("p (g t) -> p g t", t=GT)[:, :, 0],
               start=True, stop=True).then_inc(base_ps, 1)
            pe.wait_ge(norm_in, 1)
            mm(PS[:, 3072:3073], ones[:, :], flag[:, 0:1], start=True, stop=True).then_inc(base_ps, 1)
            pe.wait_ge(norm_in, 2)
            pe.wait_ge(table_set, 1)
            transposes().then_inc(ht_ps, 1)
            pe.wait_ge(ht_set, 1)
            pe.wait_ge(weights_in, 16 * 9)
            product(w0_sb[:, :]).then_inc(mu_ps, 1)

            def aggregate(l):
                s = passes[l]

                def step(k, m, group, v, tiles, whole):
                    pe.wait_ge(s["onehot_set"][k], m + 1 + PRIMED)
                    pe.wait_ge(s["msg_set"][k], m + 1 + PRIMED)
                    pe.wait_ge(s["sum_added"][k], m + PRIMED)
                    for t in range(tiles):
                        last = mm(agg_ps[k], M[k][:, t, :], O[k][:, t, :], start=(t == 0), stop=(t == tiles - 1))
                    last.then_inc(s["sum_ps"][k], 1)
                over_steps(pe, step)

            for l in range(2):
                aggregate(l)
                for half in range(2):
                    pe.wait_ge(sq_set, 2 * l + half + 1)
                    for b in range(NB):
                        last = mm(row_ps[half][:, b:b + 1], SQ[:, b, :], ones[0:F, 0:1], start=True, stop=True)
                    last.then_inc(rows_ps, 1)
                    if half == 0:
                        pe.wait_ge(ht_set, l + 2)
                if l == 0:
                    product(w1_sb[:, :]).then_inc(mu_ps, 1)
            blocks = aggT[:, 0:N].rearrange("f (p b) -> f b p", b=NB)
            for b in range(NB):
                mm(PS[0:PN, 3584 + b:3585 + b], blocks[:, b, :], ident[0:F + 1, F:F + 1], start=True, stop=True)
            product(ident[0:F, 0:F]).then_inc(mu_ps, 1)
            pe.wait_ge(norm_in, 3)
            transposes().then_inc(h1_ps, 1)
            pe.wait_ge(ht_set, 4)
            for b in range(NB):
                last = mm(PS[0:PN, HID * b:HID * b + HID], HT[0:F, b, :], W1a[:, :], start=True, stop=True)
            last.then_inc(p_ps, 1)
            pe.wait_ge(p_set, 1)
            for b in range(NB):
                last = mm(PS[0:PN, HID * b:HID * b + HID], HT[:, b, :], W1b[:, :], start=True, stop=True)
            last.then_inc(q_ps, 1)
            pe.wait_ge(q_set, 1)
            for c in range(0, NB, 4):
                n = min(4, NB - c)
                o = PS[:, 128 * c:128 * c + PN * n]
                mm(o, W1a[:, :], HT[0:F, c:c + n, :].rearrange("f b p -> f (b p)"), start=True, stop=False)
                last = mm(o, W1b[:, :], HT[:, c:c + n, :].rearrange("f b p -> f (b p)"), start=False, stop=True)
            last.then_inc(self_ps, 1)
            pe.wait_ge(self_set, 1)

            def edge_step(k, m, group, v, tiles, whole):
                s = edge
                pe.wait_ge(s["onehotT_set"][k], m + 1 + PRIMED)
                pe.wait_ge(s["qwin_in"][k], 16 * (m + 1))
                for half in range(2):
                    pe.wait_ge(s["t_added"][k], 2 * m + half + PRIMED)
                    for i in range(8):
                        t = 8 * half + i
                        if t >= tiles:
                            if half == 1 and i == 0:
                                t = tiles - 1
                            else:
                                continue
                        for c in range(3):
                            last = mm(t_ps[k][:, i, :], OT[k][:, TE * t:TE * t + TE], qw[k][:, c, :],
                                      start=(c == 0), stop=(c == 2))
                    last.then_inc(s["t_ps"][k], 1)
                pe.wait_ge(s["onehot_set"][k], m + 1 + PRIMED)
                pe.wait_ge(s["relu_set"][k], 2 * m + 2 + PRIMED)
                pe.wait_ge(s["sum_added"][k], m + PRIMED)
                for t in range(tiles):
                    last = mm(r_ps[k], H[k][:, t, :], O[k][:, t, :], start=(t == 0), stop=(t == tiles - 1))
                last.then_inc(s["sum_ps"][k], 1)
            over_steps(pe, edge_step)
            pe.wait_ge(fin_ps, 1)
            for b in range(NB):
                last = mm(MU[:, b, :], RT[:, 0:N].rearrange("f (p b) -> f b p", b=NB)[:, b, :], W2_sb[:, :],
                          start=True, stop=True)
            last.then_inc(fin_ps, 1)


def kernel(**inputs):
    import numpy as np
    import concourse.bacc as bacc
    from concourse.bass_utils import run_bass_kernel_spmd as run

    def tiles(a, fill):
        flat = np.concatenate([np.asarray(a), np.full(TILES * TE - E, fill, np.asarray(a).dtype)])
        return flat, np.ascontiguousarray(flat.reshape(TILES, TE).T)

    dst_row, dst_t = tiles(inputs["dst"], -1)
    given = [
        ("x", inputs["x"]), ("src", tiles(inputs["src"], 0)[1]), ("dst", dst_t),
        ("weight", tiles(inputs["edge_weight"], 0)[1]), ("dst_row", dst_row),
        ("w0T", np.asarray(inputs["L0_gnn_W0"]).T), ("b0", inputs["L0_gnn_b0"]),
        ("w1T", np.asarray(inputs["L0_gnn_W1"]).T), ("b1", inputs["L0_gnn_b1"]),
        ("eW1", inputs["L1_gnn_W1"]), ("eb1", inputs["L1_gnn_b1"]),
        ("eW2", inputs["L1_gnn_W2"]), ("eb2", inputs["L1_gnn_b2"]),
    ]
    nc = bacc.Bacc("TRN2", target_bir_lowering=False, num_devices=1)
    arrays, args = {}, []
    for name, a in given:
        a = np.ascontiguousarray(a)
        arrays[f"in_{name}"] = a
        args.append(nc.dram_tensor(f"in_{name}", a.shape, mybir.dt.from_np(a.dtype), kind="ExternalInput").ap())
    args.append(nc.dram_tensor("out", (N, F), mybir.dt.float32, kind="ExternalOutput").ap())
    gnn_kernel(nc, *args)
    r = run(nc, [arrays], core_ids=[0])
    return r.results[0]["out"]
```

```python
import concourse.bass as bass
from concourse import mybir
from contextlib import ExitStack

N = 3125
F = 64
HID = 128
E = 103125
PN = 125
NB = N // PN
TE = 128
GT = 16
GE = GT * TE
NG = -(-E // GE)
PAIRS = (NG - 1) // 2
AHEAD = 2
TILES = (NG + AHEAD) * GT
LAST = -(-(E - (NG - 1) * GE) // TE)
NS = 128
FIELDS = 5
CB = 7
ROUNDS = 12
assert NG == 4 * (ROUNDS + 1) - 1
CHUNKS = [range(b, min(b + CB, NB)) for b in range(0, NB, CB)]
W = 72
NV = -(-N // W)
NW = N + W
PRIMED = 2
QUADS = [range(b, min(b + 4, NB)) for b in range(0, NB, 4)]
MIN_NORM = 1e-15
MAXNORM = 1.0 - 0.004
CLIP = 1.0 - 1e-07
ARENA = 30600
ARTANH = [1.0 / k for k in (13, 11, 9, 7, 5, 3)]
SMALL = 0.3


def gnn_kernel(nc, x, src_t, dst_t, w_t, dst_row, w0T, b0, w1T, b1, W1, eb1, W2, eb2, out):
    f32, bf16, i32 = mybir.dt.float32, mybir.dt.bfloat16, mybir.dt.int32
    ALU = mybir.AluOpType
    ACT = mybir.ActivationFunctionType
    X = mybir.AxisListType.X
    ctx = ExitStack()
    with ctx:
        def sb(name, shape, dt=f32):
            return ctx.enter_context(nc.sbuf_tensor(name, shape, dt))

        def sem(name):
            return ctx.enter_context(nc.semaphore(name))

        xt_d = nc.dram_tensor("xt_table", (N, F), f32, kind="Internal").ap()
        p_d = nc.dram_tensor("p_table", (N, HID), f32, kind="Internal").ap()
        qf_d = nc.dram_tensor("q_full", (N, HID), f32, kind="Internal").ap()
        off_d = nc.dram_tensor("offset_rows", (NG, GE), bf16, kind="Internal").ap()
        slot_d = nc.dram_tensor("slot_rows", (NG + AHEAD, 2 * NB * NS), bf16, kind="Internal").ap()
        a_d = nc.dram_tensor("adjacency", (NG, PN, NB * W), f32, kind="Internal").ap()
        q_d = nc.dram_tensor("q_table", (NW, 3 * HID), bf16, kind="Internal").ap()

        dstT = sb("dstT", [128, TILES])
        wT = sb("wT", [128, TILES])
        offT = sb("offT", [128, TILES])
        x_sb = sb("x_sb", [PN, NB, F])
        A = sb("A", [PN, NB, F])
        Bw = sb("Bw", [128, NB * F])
        Cw = sb("Cw", [128, NB * F])
        HTw = sb("HTw", [128, NB * 128])
        B = Bw[0:PN, :].rearrange("p (b f) -> p b f", b=NB)
        C = Cw[0:PN, :].rearrange("p (b f) -> p b f", b=NB)
        HT = HTw[0:F + 1, 0:NB * PN].rearrange("f (b p) -> f b p", b=NB)
        aggT = sb("aggT", [F + 1, NW])
        RT = sb("RT", [HID, NW])
        SQ = RT[0:F, 0:N].rearrange("f (b p) -> f b p", b=NB)
        w0_sb = sb("w0_sb", [F, F])
        w1_sb = sb("w1_sb", [F, F])
        W1a = sb("W1a", [F, HID])
        W1b = sb("W1b", [F + 1, HID])
        W2_sb = sb("W2_sb", [HID, F])
        yb = sb("yb", [128, 2, F])
        ZQ = sb("ZQ", [W, 3 * HID], bf16)
        ysq = sb("ysq", [128, 2, F])
        b2b = sb("b2b", [128, F])
        ident = sb("ident", [128, 128])
        ones = sb("ones", [128, 128])
        onesb = sb("onesb", [128, 128], bf16)
        before = sb("before", [128, 128], bf16)
        rampi = sb("rampi", [128, 128], i32)
        ramp = sb("ramp", [128, 128])
        rampb = sb("rampb", [128, 128], bf16)
        identb = sb("identb", [128, 128], bf16)
        colpi = sb("colpi", [128, 1], i32)
        colp = sb("colp", [128, 1])
        colp1 = sb("colp1", [128, 1])
        vtabi = sb("vtabi", [128, NV], i32)
        vtab = sb("vtab", [128, NV])
        basef = sb("basef", [128, NG + AHEAD])
        tabi = sb("tabi", [1, NG + AHEAD], i32)
        flag = sb("flag", [128, 6])
        y2s = sb("y2s", [128, 2])
        oki = sb("oki", [1, 2], i32)
        rmax = sb("rmax", [128, GT])
        rows = sb("rows", [128, 16, NB])
        arg = sb("arg", [128, NB])
        ans = sb("ans", [128, NB])
        idx = [sb(f"idx{k}", [128, GT], i32) for k in range(2)]
        dloc = [sb(f"dloc{k}", [128, GT]) for k in range(2)]
        rank = [sb(f"rank{k}", [128, GT], bf16) for k in range(2)]
        rankf = [sb(f"rankf{k}", [128, GT]) for k in range(2)]
        slot_dst = sb("slot_dst", [128, NG + AHEAD, NB], bf16)
        slot_row = [sb(f"slot_row{k}", [2 * NB, NS], bf16) for k in range(2)]
        slots = [sb(f"slots{k}", [128, FIELDS, NB], bf16) for k in range(2)]

        arena = sb("arena", [128, ARENA])
        at = [0]

        def carve(words, dt=f32, parts=128):
            at[0] += words
            assert at[0] <= ARENA, at[0]
            view = arena[0:parts, at[0] - words:at[0]]
            return view if dt == f32 else view.bitcast(dt)

        BK = [carve(GT * NB // 2, bf16).rearrange("p (t b) -> p t b", b=NB) for _ in range(2)]
        BP = carve(GT * NB).rearrange("p (t b) -> p t b", b=NB)
        S1 = [carve(GT * NS // 2, bf16).rearrange("p (s t) -> p s t", t=GT) for _ in range(2)]
        GF = [carve(GT * FIELDS * NB // 2, bf16).rearrange("p (t f b) -> p t f b", f=FIELDS, b=NB)
              for _ in range(2)]
        OS = [carve(NB * 64, bf16).rearrange("p (n b) -> p n b", b=NB) for _ in range(2)]
        OD = carve(NB * W // 2, bf16).rearrange("p (w b) -> p w b", b=NB)
        WD = [[carve(NB * W // 2, bf16).rearrange("p (w b) -> p w b", b=NB) for _ in range(3)]
              for _ in range(2)]
        AB = [carve(NB * W).rearrange("p (b w) -> p b w", w=W) for _ in range(2)]
        OC = [carve(GT * W // 2, bf16).rearrange("p (t w) -> p t w", w=W) for _ in range(2)]
        fieldT = carve(TILES * FIELDS // 2, bf16).rearrange("p (t f) -> p t f", f=FIELDS)
        bktT = carve(TILES // 2, bf16)
        row_of = carve(NB * 64, bf16).rearrange("p (n b) -> p n b", b=NB)
        slot_of = carve(NS * GT // 2, bf16).rearrange("p (s t) -> p s t", t=GT)
        at[0] = 0
        PQ = carve(NB * HID)[0:PN].rearrange("p (b h) -> p b h", h=HID)
        P3 = carve(NB * 3 * HID // 2, bf16, PN).rearrange("p (b c h) -> p b c h", c=3, h=HID)
        GP = [carve(GT * HID).rearrange("p (t h) -> p t h", h=HID) for _ in range(2)]
        early = at[0]
        H = [carve(GT * HID).rearrange("p (t h) -> p t h", h=HID) for _ in range(2)]
        O = [carve(GT * W).rearrange("p (t w) -> p t w", w=W) for _ in range(2)]
        dbc = [carve(GE // 2, bf16, W) for _ in range(2)]
        OT = [carve(GE // 2, bf16, W) for _ in range(2)]
        qw = [carve(3 * HID // 2, bf16, W).rearrange("p (c h) -> p c h", h=HID) for _ in range(2)]
        qs = [carve(3 * HID // 2, bf16, W).rearrange("p (c h) -> p c h", h=HID) for _ in range(2)]
        OTs = [carve(NB * NS // 2, bf16, PN).rearrange("p (b s) -> p b s", s=NS) for _ in range(2)]
        Os = [carve(NB * W).rearrange("p (b w) -> p b w", w=W) for _ in range(2)]
        end = at[0]
        OTd = [HTw[0:W, k * NB * NS // 2:(k + 1) * NB * NS // 2].bitcast(bf16).rearrange("p (b s) -> p b s", s=NS)
               for k in range(2)]
        src_bc, dst_bc = Bw[0:PN, :].bitcast(bf16), Cw[0:W, :].bitcast(bf16)
        Hs = arena[:, 0:NB * HID].rearrange("p (b h) -> p b h", h=HID)
        at[0] = early
        Q3 = carve(NB * 3 * HID // 2, bf16, PN).rearrange("p (b c h) -> p b c h", c=3, h=HID)
        assert at[0] <= early + 2 * GT * (HID + W)
        at[0] = early + 2 * GT * (HID + W)
        RQ = carve(NB * HID, parts=PN).rearrange("p (b h) -> p b h", h=HID)
        at[0] = end - 2 * NB * W - NB * NS
        QF = carve(NB * HID, parts=PN).rearrange("p (b h) -> p b h", h=HID)
        row_i = arena[0:NG, 7 * TILES:7 * TILES + GE].bitcast(i32)
        row_b = arena[0:NG, 7 * TILES + GE:7 * TILES + 3 * GE // 2].bitcast(bf16)
        G = GP[0][:, 0:GT // 2, :].rearrange("p t (a f) -> p (t a) f", a=2)
        M = H[0].rearrange("p t h -> p (t h)")[:, 0:GT * (F + 1)].rearrange("p (t f) -> p t f", t=GT)
        dstI = arena[:, 0:TILES].bitcast(i32)
        srcI = arena[:, TILES:2 * TILES].bitcast(i32)
        u = [arena[:, i * TILES:(i + 1) * TILES] for i in range(2, 6)]
        ui = arena[:, 6 * TILES:7 * TILES].bitcast(i32)

        PS = ctx.enter_context(nc.psum_tensor("PS", [128, 4096], f32))
        MU = PS[0:PN, 0:NB * F].rearrange("p (b f) -> p b f", b=NB)
        def bank(n):
            return PS[:, 512 * n:512 * n + 512]

        prefix_ps = bank(0)[:, 0:GT * NB].rearrange("p (t b) -> p t b", b=NB)
        slots_ps = bank(1)[:, 0:FIELDS * NB].rearrange("p (f b) -> p f b", b=NB)
        agg_ps = bank(2)[0:F, 0:W]
        row_t_ps = bank(3)[0:2 * NB, 0:NS]
        cnt_ps = bank(3)[F:F + 1, 0:W]
        blocks_ps = [bank(4 + c)[:, 0:len(bs) * W].rearrange("p (b w) -> p b w", w=W)
                     for c, bs in enumerate(CHUNKS)]
        any_ps = bank(6)[:, 0:W]
        r_ps, rs_ps = bank(6)[:, 0:W], bank(7)[:, 0:W]
        ts_ps = [bank(4 + i).rearrange("p (b h) -> p b h", h=HID) for i in range(2)]
        t_ps = [PS[:, 1024 * k:1024 * k + 1024].rearrange("p (t h) -> p t h", h=HID) for k in range(2)]
        row_ps = [PS[0:PN, 2048 + 512 * k:2048 + 512 * k + NB] for k in range(2)]

        edges_in, x_in, weights_in = sem("edges_in"), sem("x_in"), sem("weights_in")
        consts_set = sem("consts_set")
        vec = sem("vec")
        asked, answered = sem("asked"), sem("answered")
        act = sem("act")
        base_ps, table_set = sem("base_ps"), sem("table_set")
        ranks_set, ranks_ps, ranks_checked = sem("ranks_set"), sem("ranks_ps"), sem("ranks_checked")
        norm_in, ht_ps, ht_set, mu_ps, mu_read = (sem("norm_in"), sem("ht_ps"), sem("ht_set"),
                                                  sem("mu_ps"), sem("mu_read"))
        sq_set, rows_ps = sem("sq_set"), sem("rows_ps")
        square_asked, square_set = sem("square_asked"), sem("square_set")
        xt_set, xt_stored = sem("xt_set"), sem("xt_stored")
        agg_zero = sem("agg_zero")
        h1_ps, p_ps, p_set, q_ps, q_set = sem("h1_ps"), sem("p_ps"), sem("p_set"), sem("q_ps"), sem("q_set")
        p_stored, q3_set, q_stored = sem("p_stored"), sem("q3_set"), sem("q_stored")
        self_ps, self_set = sem("self_ps"), sem("self_set")
        fin_ps, fin_set, out_stored = sem("fin_ps"), sem("fin_set"), sem("out_stored")
        q_tail = sem("q_tail")
        begun = sem("begun")

        loop_sems = []

        def counts(name, n=1):
            made = [sem(f"{name}{i}") for i in range(n)]
            loop_sems.extend(made)
            return made if n > 1 else made[0]

        def nth(i):
            return i + 1 + PRIMED

        primed = sem("primed")
        bucket_set, field_set, prefix_done, picked, rank_set, slot1_set, slots_done, slots_set = (
            counts(n) for n in ("bucket_set", "field_set", "prefix_done", "picked", "rank_set", "slot1_set",
                                "slots_done", "slots_set"))
        rankb_set = counts("rankb_set")
        dst1_set, onehots_set = counts("dst1_set"), counts("onehots_set")
        blocks_done, blocks_set = (counts(n, len(CHUNKS)) for n in ("blocks_done", "blocks_set"))
        applied, added = counts("applied"), counts("added")
        saved = counts("saved")
        a_stored = sem("a_stored")
        a_in = [sem(f"a_in{k}") for k in range(2)]
        applied2, added2, counted, cdloc_set, cone_set = (counts(n) for n in (
            "applied2", "added2", "counted", "cdloc_set", "cone_set"))
        gathered = [sem(f"gathered{k}") for k in range(2)]
        idx_in = [sem(f"idx_in{k}") for k in range(2)]
        dst_in = [sem(f"dst_in{k}") for k in range(2)]
        qwin_in = [sem(f"qwin_in{k}") for k in range(2)]
        dloc_set, onehot_set, onehotT_set, t_done, t_added, relu_set, sum_done, rt_added = (
            counts(n) for n in ("dloc_set", "onehot_set", "onehotT_set", "t_done", "t_added", "relu_set",
                                "sum_done", "rt_added"))
        slots_in = sem("slots_in")
        src_onehot_set, s_onehots_set, s_t_done, s_relu_set, s_sum_done = (counts(n) for n in (
            "src_onehot_set", "s_onehots_set", "s_t_done", "s_relu_set", "s_sum_done"))
        row_done, row_set, row_saved = (counts(n) for n in ("row_done", "row_set", "row_saved"))
        row_stored, off_in, off_set, off_stored, p3_set = (sem(n) for n in (
            "row_stored", "off_in", "off_set", "off_stored", "p3_set"))
        any_idx, any_gathered, any_gathered_q = ([sem(f"{n}{i}") for i in range(3)] for n in (
            "any_idx", "any_gathered", "any_gathered_q"))
        any_rows, any_dloc, any_onehot, any_sum, any_added, any_qidx = (
            [counts(f"{n}{i}_") for i in range(3)] for n in (
                "any_rows", "any_dloc", "any_onehot", "any_sum", "any_added", "any_qidx"))
        qf_stored, any_cleared = sem("qf_stored"), sem("any_cleared")

        block = ctx.enter_context(nc.Block())

        def groups(eng, body):
            body(0, 0, 0)
            with eng.Fori(0, PAIRS) as j:
                body(2 * j + 1, 1, j)
                body(2 * j + 2, 0, j + 1)

        def step_of(j, c):
            return 2 * j + c

        def f_group(j, c):
            return 2 * step_of(j, c)

        def s_group(j, c):
            return 2 * step_of(j, c) + 1

        def f_added(j, c):
            return 2 * step_of(j, c) + (0 if is_last(j, c) else 1)

        def s_added(j, c):
            return 2 * step_of(j, c)

        def back(j, c):
            return (j, 0) if c else (j - 1, 1)

        def ahead(j, c):
            return (j + 1, 0) if c else (j, 1)

        def is_last(j, c):
            return isinstance(j, int) and j == ROUNDS and c == 1

        def rounds(eng, step):
            step(0, 0, True)
            step(0, 1, False)
            with eng.Fori(1, ROUNDS) as j:
                step(j, 0, False)
                step(j, 1, False)
            step(ROUNDS, 0, False)
            step(ROUNDS, 1, False)

        def window(eng, group):
            return eng.value_load(tabi[0:1, bass.ds(group, 1)], min_val=0, max_val=N - 1)

        def in_order(eng, stage):
            eng.wait_ge(table_set if stage == 0 else ranks_checked, 1)
            return eng.value_load(oki[0:1, stage:stage + 1], min_val=0, max_val=1)

        @block.sync
        def _(sp):
            sp.dma_start(x_sb[:, :, :], x.rearrange("(p b) f -> p b f", b=NB)).then_inc(x_in, 16)
            for t, d in ((dstI, dst_t), (srcI, src_t), (wT[:, :], w_t)):
                sp.dma_start(t, d[:, :]).then_inc(edges_in, 16)
            sp.dma_start(yb[:, 0, :], b0.partition_broadcast(128)).then_inc(weights_in, 16)
            sp.dma_start(yb[:, 1, :], b1.partition_broadcast(128)).then_inc(weights_in, 16)
            sp.dma_start(b2b[:, :], eb2.partition_broadcast(128)).then_inc(weights_in, 16)
            sp.dma_start(w0_sb[:, :], w0T[:, :]).then_inc(weights_in, 16)
            sp.dma_start(w1_sb[:, :], w1T[:, :]).then_inc(weights_in, 16)
            sp.dma_start(W1a[:, :], W1[0:F, :]).then_inc(weights_in, 16)
            sp.dma_start(W1b[0:F, :], W1[F:2 * F, :]).then_inc(weights_in, 16)
            sp.dma_start(W1b[F:F + 1, :], eb1.partition_broadcast(1)).then_inc(weights_in, 16)
            sp.dma_start(W2_sb[:, :], W2[:, :]).then_inc(weights_in, 16)
            sp.dma_start(row_i, dst_row[0:NG * GE].rearrange("(g e) -> g e", e=GE)).then_inc(off_in, 16)
            sp.wait_ge(off_set, 1)
            sp.dma_start(off_d[:, :], row_b).then_inc(off_stored, 16)
            sp.wait_ge(consts_set, 13)
            sp.dma_start(q_d[N:NW, :], ZQ[:, :]).then_inc(q_tail, 16)

            def store_blocks(g, k, n):
                sp.wait_ge(blocks_set[-1], nth(g))
                sp.dma_start(a_d[bass.ds(g, 1), :, :].rearrange("g p w -> (g p) w"),
                             AB[k][0:PN].rearrange("p b w -> p (b w)")).then_inc(a_stored, 16)
                store_rows(g + 1, 1 - k)
                sp.wait_ge(a_stored, 16 * (g + 1))
                sp.sem_inc(saved, 1)
                sp.wait_ge(row_stored, 16 * (g + 2))
                sp.sem_inc(row_saved, 1)

            def store_rows(g, k):
                sp.wait_ge(row_set, nth(g))
                last = slot_d[bass.ds(g, 1), :]
                sp.dma_start(last.rearrange("g (b s) -> (g b) s", s=NS), slot_row[k][:, :])\
                    .then_inc(row_stored, 16)

            def load_blocks(g, k, n):
                sp.wait_ge(applied2, nth(g - 2))
                sp.dma_start(AB[k][0:PN].rearrange("p b w -> p (b w)"),
                             a_d[bass.ds(g, 1), :, :].rearrange("g p w -> (g p) w")).then_inc(a_in[k], 16)

            def any_indices(i):
                with sp.Fori(0, NG) as g:
                    sp.wait_ge(any_rows[i], nth(g - 1))
                    sp.dma_start(idx[0][:, :], src_t[:, bass.ds(g * GT, GT)]).then_inc(any_idx[i], 16)

            def store_table(l):
                sp.wait_ge(xt_set, l + 1)
                sp.dma_start(xt_d.rearrange("(p b) f -> p b f", b=NB), A[:, :, :]).then_inc(xt_stored, 16)

            fast = in_order(sp, 0)
            with sp.If(fast == 1):
                sp.wait_ge(off_stored, 16)
                store_rows(0, 0)
                sp.wait_ge(row_stored, 16)
                sp.sem_inc(row_saved, 1)
                groups(sp, store_blocks)
            fast = in_order(sp, 1)
            for l in range(2):
                with sp.If(fast == 0):
                    store_table(l)
                    any_indices(l)
                if l == 1:
                    with sp.If(fast == 1):
                        sp.wait_ge(xt_set, 2)
                        groups(sp, load_blocks)
            sp.wait_ge(p_set, 1)
            sp.dma_start(p_d.rearrange("(p b) f -> p b f", b=NB), PQ).then_inc(p_stored, 16)
            with sp.If(fast == 0):
                sp.wait_ge(q_set, 1)
                sp.dma_start(qf_d.rearrange("(p b) f -> p b f", b=NB), QF).then_inc(qf_stored, 16)
                any_indices(2)
                sp.wait_ge(qf_stored, 16)

            def load_edges(j, c):
                i, k, g = step_of(j, c), c, f_group(j, c)
                sp.wait_ge(relu_set, nth(2 * (i - 2) + 1))
                sp.dma_start(idx[k][:, :], src_t[:, bass.ds(g * GT, GT)]).then_inc(idx_in[k], 16)
                base = window(sp, g)
                sp.wait_ge(onehotT_set, nth(i - 2))
                sp.dma_start(dbc[k], off_d[bass.ds(g, 1), :].rearrange("g e -> (g e)").partition_broadcast(W))\
                    .then_inc(dst_in[k], 16)
                sp.wait_ge(t_done, nth(2 * (i - 2) + 1))
                sp.dma_start(qw[k].rearrange("p c h -> p (c h)"), q_d[bass.ds(base, W), :])\
                    .then_inc(qwin_in[k], 16)

            def load_slots(j, c):
                m, g = step_of(j, c), s_group(j, c)
                row = slot_d[bass.ds(g, 1), :].rearrange("g s -> (g s)")
                base = window(sp, g)
                sp.wait_ge(s_onehots_set, nth(m - 1))
                sp.dma_start(src_bc, row[0:NB * NS].partition_broadcast(PN)).then_inc(slots_in, 16)
                sp.dma_start(dst_bc, row[NB * NS:2 * NB * NS].partition_broadcast(W)).then_inc(slots_in, 16)
                sp.wait_ge(s_sum_done, nth(m - 2))
                sp.dma_start(qs[c].rearrange("p c h -> p (c h)"), q_d[bass.ds(base, W), :])\
                    .then_inc(slots_in, 16)

            def load_step(j, c, first):
                if not is_last(j, c):
                    if not is_last(*ahead(j, c)):
                        load_slots(*ahead(j, c))
                    load_edges(*ahead(j, c))

            with sp.If(fast == 1):
                sp.wait_ge(q3_set, 1)
                sp.dma_start(q_d[0:N, :].rearrange("(p b) f -> p (b f)", b=NB),
                             Q3.rearrange("p b c f -> p (b c f)")).then_inc(q_stored, 16)
                sp.wait_ge(q_stored, 16)
                sp.wait_ge(q_tail, 16)
                load_slots(0, 0)
                load_edges(0, 0)
                rounds(sp, load_step)
            sp.wait_ge(fin_set, 1)
            sp.dma_start(out.rearrange("(p b) f -> p b f", b=NB), A[:, :, :]).then_inc(out_stored, 16)
            sp.wait_ge(out_stored, 16)
            sp.wait_ge(p_stored, 16)
            sp.wait_ge(q_tail, 16)

        @block.gpsimd
        def _(pool):
            pool.memset(ones[:, :], 1.0).then_inc(consts_set, 1)
            pool.memset(ident[:, :], 0.0).then_inc(consts_set, 1)
            pool.iota(rampi[:, :], [[1, 128]], base=0, channel_multiplier=0).then_inc(consts_set, 1)
            pool.iota(colpi[:, :], [[0, 1]], base=0, channel_multiplier=1).then_inc(consts_set, 1)
            pool.iota(vtabi[:, :], [[W, NV]], base=0, channel_multiplier=0).then_inc(consts_set, 1)
            pool.memset(onesb[:, :], 1.0).then_inc(consts_set, 1)
            pool.memset(before[:, :], 1.0).then_inc(consts_set, 1)
            pool.memset(identb[:, :], 0.0).then_inc(consts_set, 1)
            pool.wait_ge(consts_set, 10)
            pool.affine_select(out=identb[:, :], in_=identb[:, :], compare_op=ALU.not_equal, fill=1.0,
                               base=0, pattern=[[-1, 128]], channel_multiplier=1).then_inc(consts_set, 1)
            pool.affine_select(out=ident[:, :], in_=ident[:, :], compare_op=ALU.not_equal, fill=1.0,
                               base=0, pattern=[[-1, 128]], channel_multiplier=1).then_inc(consts_set, 1)

            pool.affine_select(out=before[:, :], in_=before[:, :], compare_op=ALU.is_ge, fill=0.0,
                               base=-1, pattern=[[1, 128]], channel_multiplier=-1).then_inc(consts_set, 1)
            for s in loop_sems:
                pool.sem_inc(s, PRIMED)
            pool.sem_inc(primed, 1)

            def prepare(g, k):
                pool.wait_ge(bucket_set, nth(g))
                pool.wait_ge(slots_done, nth(g - 2))
                pool.sem_inc(begun, 1)
                shape = [128, GT, FIELDS, NB]
                nc.gpsimd.tensor_tensor(GF[k], BK[k].unsqueeze(2).broadcast_to(shape),
                                        fieldT[:, bass.ds(g * GT, GT), :].unsqueeze(3).broadcast_to(shape),
                                        ALU.mult).then_inc(field_set, 1)

            def any_gather(i, table, dest):
                with pool.Fori(0, NG) as g:
                    pool.wait_ge(any_idx[i], 16 * (g + 1))
                    pool.wait_ge(any_rows[i], nth(g - 1))
                    pool.sem_inc(begun, 1)
                    for t in range(GT):
                        pool.indirect_dma_start(dest[:, t, :], None, table[:, :],
                                                bass.IndirectOffsetOnAxis(ap=idx[0][:, t:t + 1], axis=0))\
                            .then_inc(any_gathered[i], 16)
                    if i == 2:
                        pool.wait_ge(any_qidx[i], nth(g))
                        pool.sem_inc(begun, 1)
                        for t in range(GT):
                            pool.indirect_dma_start(GP[1][:, t, :], None, qf_d[:, :],
                                                    bass.IndirectOffsetOnAxis(ap=idx[1][:, t:t + 1], axis=0))\
                                .then_inc(any_gathered_q[i], 16)

            def gather(j, c, first):
                i, k = step_of(j, c), c
                pool.wait_ge(idx_in[k], 8 * (i - k) + 16)
                pool.wait_ge(relu_set, nth(2 * (i - 2) + 1))
                pool.sem_inc(begun, 1)
                for t in range(GT):
                    pool.indirect_dma_start(GP[k][:, t, :], None, p_d[:, :],
                                            bass.IndirectOffsetOnAxis(ap=idx[k][:, t:t + 1], axis=0))\
                        .then_inc(gathered[k], 16)

            fast = in_order(pool, 0)
            with pool.If(fast == 1):
                prepare(0, 0)
                prepare(1, 1)
                groups(pool, lambda g, k, n: prepare(g + AHEAD, k))
            fast = in_order(pool, 1)
            for l in range(2):
                with pool.If(fast == 0):
                    pool.wait_ge(xt_stored, 16 * (l + 1))
                    any_gather(l, xt_d, G)
            pool.wait_ge(p_stored, 16)
            with pool.If(fast == 0):
                pool.wait_ge(qf_stored, 16)
                any_gather(2, p_d, GP[0])
            with pool.If(fast == 1):
                rounds(pool, gather)

        Y_FUNCS = [ACT.Sqrt, ACT.Tanh, ACT.Sqrt]
        EXP_FUNCS = [ACT.Sqrt, ACT.Tanh, ACT.Sqrt]
        LINEAR_FUNCS = [ACT.Sqrt, ACT.Ln, ACT.Sqrt, ACT.Tanh, ACT.Sqrt]
        LOG_FUNCS = [ACT.Sqrt, ACT.Sqrt, ACT.Ln]

        @block.scalar
        def _(sc):
            done = {"answers": 0, "squares": 0, "chain": 0}

            def answer(funcs):
                for fn in funcs:
                    done["answers"] += 1
                    sc.wait_ge(asked, done["answers"])
                    nc.scalar.activation(ans[0:PN, :], arg[0:PN, :], fn).then_inc(answered, 1)

            def square(dst, source):
                done["squares"] += 1
                sc.wait_ge(square_asked, done["squares"])
                nc.scalar.activation(dst, source, ACT.Square).then_inc(square_set, 1)

            def copy_ht():
                sc.wait_ge(ht_ps, 1)
                for c in range(0, NB, 4):
                    n = min(4, NB - c)
                    ps = PS[0:F, 128 * c:128 * c + 500][:, 0:PN * n].rearrange("f (b p) -> f b p", b=n)
                    last = nc.scalar.activation(HT[0:F, c:c + n, :], ps, ACT.Copy)
                return last

            def take_slots(g, k):
                sc.wait_ge(slots_done, nth(g))
                sc.wait_ge(onehots_set, nth(g - 2))
                nc.scalar.activation(slot_dst[:, bass.ds(g, 1), :], slots_ps[:, 1:2, :], ACT.Copy)
                nc.scalar.activation(slots[k][:, :, :], slots_ps, ACT.Copy).then_inc(slots_set, 1)

            def take_rows(g, k):
                sc.wait_ge(row_done, nth(g))
                sc.wait_ge(row_saved, nth(g - 2))
                nc.scalar.activation(slot_row[k][:, :], row_t_ps, ACT.Copy).then_inc(row_set, 1)

            def evict(g, k, n):
                take_slots(g + 1, 1 - k)
                sc.wait_ge(saved, nth(g - 2))
                sc.wait_ge(applied, nth(g - 2))
                for c, bs in enumerate(CHUNKS):
                    sc.wait_ge(blocks_done[c], nth(g))
                    nc.scalar.activation(AB[k][:, bs[0]:bs[-1] + 1, :], blocks_ps[c], ACT.Copy)\
                        .then_inc(blocks_set[c], 1)
                take_rows(g + 1, 1 - k)

            answer([ACT.Sqrt])
            sc.wait_ge(primed, 1)
            sc.wait_ge(consts_set, 13)
            copy_ht().then_inc(ht_set, 1)
            answer(Y_FUNCS)
            answer(EXP_FUNCS)
            for l in range(2):
                sc.wait_ge(mu_ps, l + 1)
                square(B[:, :, :], MU)
                answer(LINEAR_FUNCS)
                square(B[:, :, :], A[:, :, :])
                answer(LOG_FUNCS)
                if l == 0:
                    fast = in_order(sc, 0)
                    with sc.If(fast == 1):
                        take_slots(0, 0)
                        take_rows(0, 0)
                        groups(sc, evict)
                    fast = in_order(sc, 1)
                sc.wait_ge(sq_set, 2 * l + 1)
                nc.scalar.activation(HT[0:F, :, :], aggT[0:F, 0:N].rearrange("f (p b) -> f b p", b=NB),
                                     ACT.Relu).then_inc(ht_set, 1)
                answer(EXP_FUNCS)
                answer([ACT.Sqrt, ACT.Ln])
                answer(EXP_FUNCS)
            answer([ACT.Sqrt])
            sc.wait_ge(h1_ps, 1)
            for c in range(0, NB, 4):
                n = min(4, NB - c)
                ps = PS[0:F, 128 * c:128 * c + 500][:, 0:PN * n].rearrange("f (b p) -> f b p", b=n)
                last = nc.scalar.activation(HT[0:F, c:c + n, :], ps, ACT.Copy)
            last.then_inc(ht_set, 1)
            sc.wait_ge(p_ps, 1)
            nc.scalar.activation(PQ, PS[0:PN, 0:NB * HID].rearrange("p (b h) -> p b h", b=NB),
                                 ACT.Copy).then_inc(p_set, 1)
            sc.wait_ge(q_ps, 1)
            nc.scalar.activation(QF, PS[0:PN, 0:NB * HID].rearrange("p (b h) -> p b h", b=NB),
                                 ACT.Copy).then_inc(q_set, 1)
            sc.wait_ge(self_ps, 1)
            for c in range(0, NB, 4):
                n = min(4, NB - c)
                ps = PS[:, 128 * c:128 * c + 500][:, 0:PN * n].rearrange("f (b p) -> f b p", b=n)
                last = nc.scalar.activation(RT[:, 0:N].rearrange("f (p b) -> f b p", b=NB)[:, c:c + n, :],
                                            ps, ACT.Relu)
            last.then_inc(self_set, 1)

            def relu_gathered(j, c):
                i, k = step_of(j, c), c
                sc.wait_ge(sum_done, nth(i - 2))
                for half in range(2):
                    sc.wait_ge(t_added, nth(2 * i + half))
                    part = slice(8 * half, 8 * half + 8)
                    nc.scalar.activation(H[k][:, part, :], GP[k][:, part, :], ACT.Relu).then_inc(relu_set, 1)

            def relu_slots(j, c):
                m = step_of(j, c)
                sc.wait_ge(s_sum_done, nth(m - 1))
                for q, bs in enumerate(QUADS):
                    sc.wait_ge(s_t_done, nth(len(QUADS) * m + q))
                    nc.scalar.activation(Hs[:, bs[0]:bs[-1] + 1, :], ts_ps[q % 2][:, 0:len(bs), :], ACT.Relu)\
                        .then_inc(s_relu_set, 1)

            def relu_step(j, c, first):
                if not first:
                    relu_gathered(*back(j, c))
                if not is_last(j, c):
                    relu_slots(j, c)

            with sc.If(fast == 1):
                sc.wait_ge(q_stored, 16)
                sc.wait_ge(p3_set, 1)
                rounds(sc, relu_step)
                relu_gathered(ROUNDS, 1)

        @block.vector
        def _(ve):
            n_vec = [0]
            n_ask = [0]
            n_square = [0]

            def link(ins):
                n_vec[0] += 1
                ins.then_inc(vec, 1)
                ve.wait_ge(vec, n_vec[0])

            def ask(expr):
                n_ask[0] += 1
                expr.then_inc(asked, 1)
                ve.wait_ge(answered, n_ask[0])

            def ask_square():
                n_square[0] += 1
                ve.sem_inc(square_asked, 1)

            def squares_ready():
                ve.wait_ge(square_set, n_square[0])

            P_ = slice(0, PN)

            def row(i):
                return rows[P_, i, :]

            a_, s_ = arg[P_, :], ans[P_, :]
            SS, S, NX, ATN, T, Q_, Z, SSP, T1, T2, T3, AC, BC, MASK = range(14)

            def tt(o, i, j, op):
                link(ve.tensor_tensor(o, i, j, op))

            def ts(o, i, c1, op1, c2=None, op2=ALU.bypass):
                link(ve.tensor_scalar(o, i, c1, c2, op1, op2))

            def norm(o, ss):
                ask(ve.tensor_scalar(a_, ss, MIN_NORM, None, ALU.max))
                link(ve.tensor_copy(o, s_))

            def over(o, num, den):
                link(ve.reciprocal(row(T1), den))
                tt(o, num, row(T1), ALU.mult)

            def expmap(s, ss):
                norm(row(T2), ss)
                ask(ve.tensor_copy(a_, row(T2)))
                over(s, s_, row(T2))

            def project(s, ss):
                tt(row(T2), s, s, ALU.mult)
                tt(row(T2), row(T2), ss, ALU.mult)
                norm(row(T3), row(T2))
                link(ve.reciprocal(row(T1), row(T3)))
                ts(row(T1), row(T1), MAXNORM, ALU.mult, 1.0, ALU.min)
                tt(s, s, row(T1), ALU.mult)

            def artanh_ratio(o, n):
                ts(row(T3), n, CLIP, ALU.min)
                ts(row(T1), row(T3), -1.0, ALU.mult, 1.0, ALU.add)
                link(ve.reciprocal(row(T1), row(T1)))
                ts(row(T2), row(T3), 1.0, ALU.add)
                ask(ve.tensor_tensor(a_, row(T1), row(T2), ALU.mult))
                link(ve.reciprocal(row(T1), n))
                link(ve.scalar_tensor_tensor(row(T1), s_, 0.5, row(T1), ALU.mult, ALU.mult))
                tt(row(T2), row(T3), row(T3), ALU.mult)
                ts(o, row(T2), ARTANH[0], ALU.mult)
                for c in ARTANH[1:]:
                    link(ve.scalar_tensor_tensor(o, o, c, row(T2), ALU.add, ALU.mult))
                ts(o, o, 1.0, ALU.add)
                ts(row(T2), row(T3), SMALL, ALU.is_lt)
                tt(o, o, row(T2), ALU.mult)
                ts(row(T2), row(T3), SMALL, ALU.is_ge)
                tt(row(T1), row(T1), row(T2), ALU.mult)
                tt(o, o, row(T1), ALU.add)

            def wide(r):
                return r.unsqueeze(2).broadcast_to([PN, NB, F])

            def layer_norm(dst, source):
                link(ve.tensor_reduce(row(T1), source, X, ALU.add))
                ts(row(T1), row(T1), 1.0 / F, ALU.mult)
                tt(dst, source, wide(row(T1)), ALU.subtract)
                tt(C[:, :, :], dst, dst, ALU.mult)
                link(ve.tensor_reduce(row(T2), C[:, :, :], X, ALU.add))
                ask(ve.tensor_scalar(a_, row(T2), 1.0 / F, 1e-5, ALU.mult, ALU.add))
                link(ve.reciprocal(row(T1), s_))
                link(ve.scalar_tensor_tensor(dst, dst, 0.0, wide(row(T1)), ALU.max, ALU.mult))

            def linear(l):
                y = yb[P_, l, :].unsqueeze(1).broadcast_to([PN, NB, F])
                y2 = y2s[P_, l:l + 1]
                ve.wait_ge(mu_ps, l + 1)
                tt(C[:, :, :], MU, y, ALU.mult)
                ask_square()
                link(ve.tensor_reduce(row(Z), C[:, :, :], X, ALU.add))
                squares_ready()
                link(ve.tensor_reduce(row(Q_), B[:, :, :], X, ALU.add))
                tt(row(T), row(S), row(S), ALU.mult)
                tt(row(T1), row(T), row(SS), ALU.mult)
                norm(row(NX), row(T1))
                artanh_ratio(row(ATN), row(NX))
                tt(row(T1), row(T), row(Q_), ALU.mult)
                norm(row(T), row(T1))
                ask(ve.tensor_tensor(a_, row(T), row(ATN), ALU.mult))
                over(row(T), s_, row(T))
                tt(row(T), row(T), row(S), ALU.mult)
                project(row(T), row(Q_))
                tt(row(T1), row(T), row(T), ALU.mult)
                tt(row(T1), row(T1), row(Q_), ALU.mult)
                ts(row(BC), row(T1), -1.0, ALU.mult, 1.0, ALU.add)
                tt(row(T2), row(T), row(Z), ALU.mult)
                ts(row(T2), row(T2), 2.0, ALU.mult, 1.0, ALU.add)
                link(ve.scalar_tensor_tensor(row(T3), row(T1), y2, row(T2), ALU.mult, ALU.add))
                ts(row(T3), row(T3), MIN_NORM, ALU.max)
                link(ve.reciprocal(row(T3), row(T3)))
                link(ve.scalar_tensor_tensor(row(AC), row(T2), y2, row(T), ALU.add, ALU.mult))
                tt(row(AC), row(AC), row(T3), ALU.mult)
                tt(row(BC), row(BC), row(T3), ALU.mult)
                tt(A[:, :, :], MU, wide(row(AC)), ALU.mult)
                tt(C[:, :, :], y, wide(row(BC)), ALU.mult)
                tt(A[:, :, :], A[:, :, :], C[:, :, :], ALU.add)
                ask_square()
                squares_ready()
                link(ve.tensor_reduce(row(Q_), B[:, :, :], X, ALU.add))
                link(ve.memset(row(S), 1.0))
                project(row(S), row(Q_))
                tt(row(T2), row(S), row(S), ALU.mult)
                tt(row(T2), row(T2), row(Q_), ALU.mult)
                norm(row(NX), row(T2))
                artanh_ratio(row(ATN), row(NX))
                tt(row(S), row(S), row(ATN), ALU.mult)
                ve.tensor_tensor(A[:, :, :], A[:, :, :], wide(row(S)), ALU.mult).then_inc(xt_set, 1)

            ve.memset(HT[F:F + 1, :, :], 1.0).then_inc(consts_set, 1)
            ve.memset(ZQ[:, :], 0.0).then_inc(consts_set, 1)
            ve.wait_ge(edges_in, 48)
            ve.wait_ge(consts_set, 13)
            link(ve.tensor_copy(dstT[:, :], dstI))
            ve.tensor_copy(ramp[:, :], rampi[:, :])
            link(ve.tensor_copy(rampb[:, :], rampi[:, :]))
            ve.tensor_copy(row_of, rampb[:, :].unsqueeze(2).broadcast_to([128, 128, NB]))
            ve.tensor_copy(slot_of, rampb[:, 0:NS].unsqueeze(2).broadcast_to([128, NS, GT]))
            ve.tensor_copy(colp[:, :], colpi[:, :])
            ve.tensor_scalar(colp1[:, :], colpi[:, :], 1.0, None, ALU.add)
            link(ve.tensor_copy(vtab[:, :], vtabi[:, :]))
            link(ve.tensor_copy(u[0], srcI))
            ts(ui, u[0], 1.0 / NB, ALU.mult)
            link(ve.tensor_copy(u[1], ui))
            link(ve.scalar_tensor_tensor(u[0], u[1], -float(NB), u[0], ALU.mult, ALU.add))
            ts(u[2], u[0], 0.0, ALU.is_lt)
            ts(u[3], u[0], float(NB), ALU.is_ge)
            tt(u[3], u[3], u[2], ALU.subtract)
            tt(u[1], u[1], u[3], ALU.add)
            link(ve.scalar_tensor_tensor(u[0], u[3], -float(NB), u[0], ALU.mult, ALU.add))
            ts(u[2], dstT[:, :], 0.0, ALU.is_ge)
            link(ve.scalar_tensor_tensor(u[0], u[0], 1.0, u[2], ALU.add, ALU.mult))
            ts(bktT, u[0], -1.0, ALU.add)
            ve.wait_ge(off_in, 16)
            ts(flag[0:NG, 5:6], row_i[:, 0:1], 0.0, ALU.max)
            ve.tensor_scalar(row_b, row_i, flag[0:NG, 5:6], None, ALU.subtract).then_inc(off_set, 1)
            ve.wait_ge(off_set, 1)
            ve.wait_ge(base_ps, 1)
            link(ve.tensor_scalar(basef[:, :], PS[:, 3584:3584 + NG + AHEAD], 0.0, None, ALU.max))
            tt(offT[:, :].rearrange("p (g t) -> p g t", t=GT), dstT[:, :].rearrange("p (g t) -> p g t", t=GT),
               basef[:, :].unsqueeze(2).broadcast_to([128, NG + AHEAD, GT]), ALU.subtract)
            ve.tensor_copy(fieldT[:, :, 0], u[1])
            ts(fieldT[:, :, 1], offT[:, :], 1.0, ALU.add)
            link(ve.tensor_copy(fieldT[:, :, 2], wT[:, :]))
            tt(u[0], wT[:, :], fieldT[:, :, 2], ALU.subtract)
            link(ve.tensor_copy(fieldT[:, :, 3], u[0]))
            tt(fieldT[:, :, 4], u[0], fieldT[:, :, 3], ALU.subtract)
            ts(u[2], offT[:, :], float(W), ALU.is_lt)
            link(ve.scalar_tensor_tensor(u[3], offT[:, :], 0.0, u[2], ALU.is_ge, ALU.mult))
            ve.tensor_reduce(flag[:, 0:1], u[3], X, ALU.add).then_inc(norm_in, 1)
            ve.wait_ge(base_ps, 2)
            link(ve.tensor_scalar(flag[:, 1:2], PS[:, 3072:3073], float(E), None, ALU.is_equal))
            link(ve.tensor_copy(oki[0:1, 0:1], flag[0:1, 1:2]))
            link(ve.memset(rmax[:, :], 0.0))
            ve.wait_ge(off_stored, 16)
            ve.tensor_copy(tabi[0:1, :], basef[0:1, :]).then_inc(table_set, 1)

            ve.wait_ge(x_in, 16)
            layer_norm(A[:, :, :], x_sb[:, :, :])
            ve.wait_ge(vec, n_vec[0])
            ve.sem_inc(norm_in, 1)
            tt(C[:, :, :], A[:, :, :], A[:, :, :], ALU.mult)
            link(ve.tensor_reduce(row(SS), C[:, :, :], X, ALU.add))
            ve.wait_ge(weights_in, 16 * 9)
            tt(ysq[:, :, :], yb[:, :, :], yb[:, :, :], ALU.mult)
            link(ve.memset(row(Q_), 1.0))
            link(ve.tensor_reduce(rows[P_, Q_, 0:2], ysq[P_, :, :], X, ALU.add))
            expmap(row(S), row(Q_))
            project(row(S), row(Q_))
            tt(yb[P_, :, :], yb[P_, :, :], rows[P_, S, 0:2].unsqueeze(2).broadcast_to([PN, 2, F]), ALU.mult)
            tt(ysq[P_, :, :], yb[P_, :, :], yb[P_, :, :], ALU.mult)
            link(ve.tensor_reduce(y2s[P_, :], ysq[P_, :, :], X, ALU.add))
            expmap(row(S), row(SS))
            project(row(S), row(SS))

            link(ve.memset(aggT[:, :], 0.0))
            ve.wait_ge(primed, 1)

            def bucket_edges(g, k):
                ve.wait_ge(prefix_done, nth(g - 2))
                ve.wait_ge(field_set, nth(g - 2))
                ve.wait_ge(picked, nth(g - 2))
                nc.vector.tensor_tensor(BK[k], rampb[:, 0:NB].unsqueeze(1).broadcast_to([128, GT, NB]),
                                        bktT[:, bass.ds(g * GT, GT)].unsqueeze(2).broadcast_to([128, GT, NB]),
                                        ALU.is_equal).then_inc(bucket_set, 1)

            def rank_edges(g, k):
                ve.wait_ge(prefix_done, nth(g))
                ve.wait_ge(bucket_set, nth(g))
                ve.wait_ge(rank_set, nth(g - 1))
                nc.vector.tensor_tensor(BP, BK[k], prefix_ps, ALU.mult).then_inc(picked, 1)
                ve.wait_ge(picked, nth(g))
                ve.wait_ge(slot1_set, nth(g - 2))
                nc.vector.tensor_reduce(rankf[k][:, :], BP, X, ALU.add).then_inc(rank_set, 1)
                ve.wait_ge(rank_set, nth(g))
                ve.wait_ge(slots_done, nth(g - 2))
                nc.vector.tensor_copy(rank[k][:, :], rankf[k][:, :]).then_inc(rankb_set, 1)
                nc.vector.tensor_tensor(rmax[:, :], rmax[:, :], rankf[k][:, :], ALU.max)
                ve.wait_ge(rankb_set, nth(g))
                nc.vector.tensor_tensor(S1[k], slot_of,
                                        rank[k][:, :].unsqueeze(1).broadcast_to([128, NS, GT]),
                                        ALU.is_equal).then_inc(slot1_set, 1)

            def slot_onehots(g, k):
                ve.wait_ge(slots_set, nth(g))
                ve.wait_ge(blocks_done[-1], nth(g - 2))
                nc.vector.tensor_tensor(OD, row_of[:, 1:1 + W, :],
                                        slots[k][:, 1, :].unsqueeze(1).broadcast_to([128, W, NB]),
                                        ALU.is_equal).then_inc(dst1_set, 1)
                nc.vector.tensor_tensor(OS[k], row_of[:, :, :],
                                        slots[k][:, 0, :].unsqueeze(1).broadcast_to([128, 128, NB]),
                                        ALU.is_equal)
                ve.wait_ge(dst1_set, nth(g))
                for i in range(3):
                    last = nc.vector.tensor_tensor(WD[k][i], OD,
                                                   slots[k][:, 2 + i, :].unsqueeze(1).broadcast_to([128, W, NB]),
                                                   ALU.mult)
                last.then_inc(onehots_set, 1)

            def add_sums(g):
                base = window(ve, g)
                ve.wait_ge(applied, nth(g))
                ve.wait_ge(added, nth(g - 1))
                win = aggT[0:F, bass.ds(base, W)]
                nc.vector.tensor_tensor(win, win, agg_ps, ALU.add).then_inc(added, 1)

            def first_layer():
                bucket_edges(0, 0)
                bucket_edges(1, 1)
                rank_edges(0, 0)
                rank_edges(1, 1)
                bucket_edges(2, 0)
                slot_onehots(0, 0)
                with ve.Fori(0, PAIRS) as j:
                    for g, k in ((2 * j + 1, 1), (2 * j + 2, 0)):
                        rank_edges(g + 1, 1 - k)
                        bucket_edges(g + 2, k)
                        slot_onehots(g, k)
                        add_sums(g - 1)
                add_sums(NG - 1)
                ve.wait_ge(added, nth(NG - 1))
                ve.wait_ge(field_set, nth(NG - 1 + AHEAD))
                ve.wait_ge(prefix_done, nth(NG - 1 + AHEAD))
                ve.wait_ge(slots_done, nth(NG))

            def second_layer():
                def body(g, k, n):
                    ve.wait_ge(cone_set, nth(g - 2))
                    nc.vector.tensor_copy(dloc[k][:, :], offT[:, bass.ds(g * GT, GT)]).then_inc(cdloc_set, 1)
                    ve.wait_ge(cdloc_set, nth(g))
                    ve.wait_ge(counted, nth(g - 2))
                    for t in range(GT):
                        last = nc.vector.tensor_scalar(OC[k][:, t, :], rampb[:, 0:W], dloc[k][:, t:t + 1], None,
                                                       ALU.is_equal)
                    last.then_inc(cone_set, 1)
                    base = window(ve, g)
                    ve.wait_ge(applied2, nth(g))
                    ve.wait_ge(added2, 2 * g + PRIMED)
                    win = aggT[0:F, bass.ds(base, W)]
                    nc.vector.tensor_tensor(win, win, agg_ps, ALU.add).then_inc(added2, 1)
                    ve.wait_ge(counted, nth(g))
                    win = aggT[F:F + 1, bass.ds(base, W)]
                    nc.vector.tensor_tensor(win, win, cnt_ps, ALU.add).then_inc(added2, 1)
                groups(ve, body)
                ve.wait_ge(added2, 2 * NG + PRIMED)

            def any_order(i):
                dest = RT if i == 2 else aggT[0:F + 1, :]
                source = any_ps if i == 2 else any_ps[0:F + 1, :]
                if i < 2:
                    ve.memset(aggT[:, :], 0.0).then_inc(any_cleared, 1)
                    ve.memset(M[:, :, F:F + 1], 1.0).then_inc(any_cleared, 1)
                    ve.wait_ge(any_cleared, 2 * (i + 1))
                with ve.Fori(0, NG) as g:
                    cols = bass.ds(g * GT, GT)
                    if i == 2:
                        ve.wait_ge(any_rows[i], nth(g - 1))
                        nc.vector.tensor_scalar(idx[1][:, :], dstT[:, cols], 0.0, None, ALU.max)\
                            .then_inc(any_qidx[i], 1)
                        ve.wait_ge(any_gathered_q[i], 16 * GT * (g + 1))
                    ve.wait_ge(any_gathered[i], 16 * GT * (g + 1))
                    ve.wait_ge(any_sum[i], NV * g + PRIMED)
                    if i == 2:
                        nc.vector.tensor_tensor(GP[0], GP[0], GP[1], ALU.add).then_inc(any_dloc[i], 1)
                        ve.wait_ge(any_dloc[i], (NV + 1) * g + 1 + PRIMED)
                        nc.vector.tensor_scalar(H[0], GP[0], 0.0, None, ALU.max).then_inc(any_rows[i], 1)
                    else:
                        nc.vector.tensor_tensor(M[:, :, 0:F], G, wT[:, cols].unsqueeze(2)
                                                .broadcast_to([128, GT, F]), ALU.mult).then_inc(any_rows[i], 1)
                    with ve.Fori(0, NV) as v:
                        n = g * NV + v
                        ve.wait_ge(any_onehot[i], nth(n - 1))
                        nc.vector.tensor_scalar(dloc[0][:, :], dstT[:, cols], vtab[:, bass.ds(v, 1)], None,
                                                ALU.subtract).then_inc(any_dloc[i], 1)
                        ve.wait_ge(any_dloc[i], nth(n + (g + 1 if i == 2 else 0)))
                        ve.wait_ge(any_sum[i], nth(n - 1))
                        for t in range(GT):
                            last = nc.vector.tensor_scalar(O[0][:, t, :], ramp[:, 0:W], dloc[0][:, t:t + 1],
                                                           None, ALU.is_equal)
                        last.then_inc(any_onehot[i], 1)
                        ve.wait_ge(any_sum[i], nth(n))
                        ve.wait_ge(any_added[i], nth(n - 1))
                        win = dest[:, bass.ds(v * W, W)]
                        nc.vector.tensor_tensor(win, win, source, ALU.add).then_inc(any_added[i], 1)
                ve.wait_ge(any_added[i], nth(NG * NV - 1))

            def check_ranks():
                link(ve.tensor_reduce(flag[:, 2:3], rmax[:, :], X, ALU.max))
                ve.tensor_scalar(flag[:, 3:4], flag[:, 2:3], float(NS - 1), None, ALU.is_le).then_inc(ranks_set, 1)
                ve.wait_ge(ranks_ps, 1)
                link(ve.tensor_scalar(flag[:, 4:5], PS[:, 3072:3073], 128.0, None, ALU.is_equal))
                link(ve.tensor_scalar(flag[:, 4:5], flag[:, 4:5], flag[:, 1:2], None, ALU.mult))
                ve.tensor_copy(oki[0:1, 1:2], flag[0:1, 4:5]).then_inc(ranks_checked, 1)

            def act_scales(l):
                blocks = aggT[0:F, 0:N].rearrange("f (p b) -> f b p", b=NB)
                ve.tensor_tensor(SQ[:, :, :], blocks, blocks, ALU.mult).then_inc(sq_set, 1)
                ve.wait_ge(rows_ps, 2 * l + 1)
                link(ve.tensor_copy(row(Q_), row_ps[0]))
                ve.wait_ge(ht_set, l + 2)
                ve.tensor_tensor(SQ[:, :, :], HT[0:F, :, :], HT[0:F, :, :], ALU.mult).then_inc(sq_set, 1)
                expmap(row(S), row(Q_))
                project(row(S), row(Q_))
                tt(row(T2), row(S), row(S), ALU.mult)
                tt(row(T2), row(T2), row(Q_), ALU.mult)
                norm(row(NX), row(T2))
                artanh_ratio(row(ATN), row(NX))
                tt(row(ATN), row(S), row(ATN), ALU.mult)
                ve.wait_ge(rows_ps, 2 * l + 2)
                link(ve.tensor_copy(row(SS), row_ps[1]))
                tt(row(T3), row(ATN), row(ATN), ALU.mult)
                tt(row(Q_), row(T3), row(SS), ALU.mult)
                expmap(row(S), row(Q_))
                project(row(S), row(Q_))
                tt(row(S), row(S), row(ATN), ALU.mult)

            for l in range(2):
                linear(l)
                if l == 0:
                    fast = in_order(ve, 0)
                    with ve.If(fast == 1):
                        ve.wait_ge(xt_set, 1)
                        first_layer()
                    check_ranks()
                    fast = in_order(ve, 1)
                else:
                    with ve.If(fast == 1):
                        ve.wait_ge(xt_set, 2)
                        second_layer()
                with ve.If(fast == 0):
                    any_order(l)
                act_scales(l)
                if l == 0:
                    link(ve.memset(aggT[:, :], 0.0))

            ve.wait_ge(mu_ps, 3)
            tt(A[:, :, :], MU, wide(row(S)), ALU.mult)
            tt(x_sb[:, :, :], x_sb[:, :, :], A[:, :, :], ALU.add)
            layer_norm(A[:, :, :], x_sb[:, :, :])
            ve.sem_inc(norm_in, 1)
            link(ve.tensor_copy(row(Z), PS[0:PN, 3584:3584 + NB]))
            ts(row(Z), row(Z), 1.0, ALU.add, 1.0, ALU.max)
            link(ve.reciprocal(row(Z), row(Z)))
            tt(x_sb[:, :, :], x_sb[:, :, :], b2b[P_, :].unsqueeze(1).broadcast_to([PN, NB, F]), ALU.add)
            link(ve.memset(RT[:, N:NW], 0.0))
            ve.wait_ge(q_set, 1)
            link(ve.tensor_copy(Q3[:, :, 0, :], QF))
            tt(RQ, QF, Q3[:, :, 0, :], ALU.subtract)
            link(ve.tensor_copy(Q3[:, :, 1, :], RQ))
            tt(RQ, RQ, Q3[:, :, 1, :], ALU.subtract)
            ve.tensor_copy(Q3[:, :, 2, :], RQ).then_inc(q3_set, 1)
            ve.wait_ge(q3_set, 1)
            ve.wait_ge(p_stored, 16)
            link(ve.tensor_copy(P3[:, :, 0, :], PQ))
            tt(PQ, PQ, P3[:, :, 0, :], ALU.subtract)
            link(ve.tensor_copy(P3[:, :, 1, :], PQ))
            tt(PQ, PQ, P3[:, :, 1, :], ALU.subtract)
            ve.tensor_copy(P3[:, :, 2, :], PQ).then_inc(p3_set, 1)
            ve.wait_ge(p3_set, 1)
            ve.wait_ge(self_set, 1)

            def destinations(j, c):
                i, k, g = step_of(j, c), c, f_group(j, c)
                ve.wait_ge(onehot_set, nth(i - 2))
                nc.vector.tensor_copy(dloc[k][:, :], offT[:, bass.ds(g * GT, GT)]).then_inc(dloc_set, 1)
                ve.wait_ge(dloc_set, nth(i))
                ve.wait_ge(sum_done, nth(i - 2))
                nc.vector.tensor_tensor(O[k], ramp[:, 0:W].unsqueeze(1).broadcast_to([128, GT, W]),
                                        dloc[k][:, :].unsqueeze(2).broadcast_to([128, GT, W]),
                                        ALU.is_equal).then_inc(onehot_set, 1)
                ve.wait_ge(dst_in[k], 8 * (i - k) + 16)
                ve.wait_ge(t_done, nth(2 * (i - 2) + 1))
                nc.vector.tensor_scalar(OT[k], dbc[k], colp[0:W, :], None, ALU.is_equal)\
                    .then_inc(onehotT_set, 1)

            def slot_rows(j, c):
                m, k, g = step_of(j, c), c, s_group(j, c)
                ve.wait_ge(slots_in, 48 * (m + 1))
                ve.wait_ge(s_sum_done, nth(m - 2))
                nc.vector.tensor_scalar(OTs[k].rearrange("p b s -> p (b s)"), src_bc, colp[0:PN, :], None,
                                        ALU.is_equal)
                nc.vector.tensor_scalar(OTd[k].rearrange("p b s -> p (b s)"), dst_bc, colp1[0:W, :], None,
                                        ALU.is_equal)
                nc.vector.tensor_tensor(Os[k], ramp[:, 1:1 + W].unsqueeze(1).broadcast_to([128, NB, W]),
                                        slot_dst[:, bass.ds(g, 1), :].rearrange("p g b -> p (g b)")
                                        .unsqueeze(2).broadcast_to([128, NB, W]),
                                        ALU.is_equal).then_inc(s_onehots_set, 1)

            def add_q(j, c):
                i, k = step_of(j, c), c
                ve.wait_ge(gathered[k], 8 * GT * (i - k) + 16 * GT)
                for half in range(2):
                    ve.wait_ge(t_done, nth(2 * i + half))
                    part = GP[k][:, 8 * half:8 * half + 8, :]
                    nc.vector.tensor_tensor(part, part, t_ps[half], ALU.add).then_inc(t_added, 1)

            def add_messages(g, q, ps):
                base = window(ve, g)
                ve.wait_ge(rt_added, nth(q - 1))
                win = RT[:, bass.ds(base, W)]
                nc.vector.tensor_tensor(win, win, ps, ALU.add).then_inc(rt_added, 1)

            def add_gathered(j, c):
                ve.wait_ge(sum_done, nth(step_of(j, c)))
                add_messages(f_group(j, c), f_added(j, c), r_ps)

            def add_slots(j, c):
                ve.wait_ge(s_sum_done, nth(step_of(j, c)))
                add_messages(s_group(j, c), s_added(j, c), rs_ps)

            def add_step(j, c, first):
                if not first:
                    add_slots(*back(j, c))
                if not is_last(j, c):
                    if not is_last(*ahead(j, c)):
                        slot_rows(*ahead(j, c))
                    destinations(*ahead(j, c))
                if not first:
                    add_gathered(*back(j, c))
                add_q(j, c)

            with ve.If(fast == 1):
                slot_rows(0, 0)
                destinations(0, 0)
                rounds(ve, add_step)
                add_gathered(ROUNDS, 1)
                ve.wait_ge(rt_added, nth(f_added(ROUNDS, 1)))
            with ve.If(fast == 0):
                any_order(2)
            ve.sem_inc(fin_ps, 1)
            ve.wait_ge(fin_ps, 2)
            tt(A[:, :, :], MU, wide(row(Z)), ALU.mult)
            ve.tensor_tensor(A[:, :, :], A[:, :, :], x_sb[:, :, :], ALU.add).then_inc(fin_set, 1)

        @block.tensor
        def _(pe):
            mm = nc.tensor.matmul
            pe.wait_ge(primed, 1)

            def transposes():
                for b in range(NB):
                    last = nc.tensor.transpose(PS[0:F, 512 * (b // 4) + PN * (b % 4):
                                                  512 * (b // 4) + PN * (b % 4) + PN],
                                               A[:, b, :], ident[0:PN, 0:PN])
                return last

            def product(weights):
                for b in range(NB):
                    last = mm(MU[:, b, :], HT[0:F, b, :], weights, start=True, stop=True)
                return last

            pe.wait_ge(edges_in, 48)
            pe.wait_ge(consts_set, 13)
            pe.wait_ge(vec, 1)
            mm(PS[:, 3584:3584 + NG + AHEAD], ones[0:1, :], dstT[0:1, :].rearrange("p (g t) -> p g t", t=GT)[:, :, 0],
               start=True, stop=True).then_inc(base_ps, 1)
            pe.wait_ge(norm_in, 1)
            mm(PS[:, 3072:3073], ones[:, :], flag[:, 0:1], start=True, stop=True).then_inc(base_ps, 1)
            pe.wait_ge(norm_in, 2)
            pe.wait_ge(table_set, 1)
            transposes().then_inc(ht_ps, 1)
            pe.wait_ge(ht_set, 1)
            pe.wait_ge(weights_in, 16 * 9)
            product(w0_sb[:, :]).then_inc(mu_ps, 1)

            def prefix(g, k):
                pe.wait_ge(bucket_set, nth(g))
                pe.wait_ge(picked, nth(g - 1))
                mm(prefix_ps, before[:, :], BK[k], start=True, stop=False)
                for d in range(1, GT):
                    last = mm(prefix_ps[:, d:GT, :], onesb[:, :], BK[k][:, 0:GT - d, :], start=False,
                              stop=(d == GT - 1))
                last.then_inc(prefix_done, 1)

            def fill_slots(g, k):
                pe.wait_ge(slot1_set, nth(g))
                pe.wait_ge(field_set, nth(g))
                pe.wait_ge(slots_set, nth(g - 1))
                for t in range(GT):
                    last = mm(slots_ps, S1[k][:, :, t], GF[k][:, t, :, :], start=(t == 0), stop=(t == GT - 1))
                last.then_inc(slots_done, 1)

            def blocks(g, k):
                pe.wait_ge(onehots_set, nth(g))
                for c, bs in enumerate(CHUNKS):
                    pe.wait_ge(blocks_set[c], nth(g - 1))
                    for i, b in enumerate(bs):
                        for part in range(3):
                            last = mm(blocks_ps[c][:, i, :], OS[k][:, :, b], WD[k][part][:, :, b],
                                      start=(part == 0), stop=(part == 2))
                    last.then_inc(blocks_done[c], 1)

            def slot_rows(g, k):
                pe.wait_ge(slots_set, nth(g))
                pe.wait_ge(row_set, nth(g - 1))
                mm(row_t_ps, slots[k][:, 0:2, :].rearrange("p f b -> p (f b)"), identb[:, :], start=True, stop=True)\
                    .then_inc(row_done, 1)

            def apply(done):
                for b in range(NB):
                    last = mm(agg_ps, A[:, b, :], AB[k_apply[0]][0:PN, b, :], start=(b == 0), stop=(b == NB - 1))
                last.then_inc(done, 1)

            k_apply = [0]

            def first_body(g, k, n):
                prefix(g + 2, k)
                fill_slots(g + 1, 1 - k)
                blocks(g, k)
                slot_rows(g + 1, 1 - k)
                pe.wait_ge(blocks_set[-1], nth(g))
                pe.wait_ge(added, nth(g - 1))
                k_apply[0] = k
                apply(applied)

            def second_body(g, k, n):
                pe.wait_ge(a_in[k], 16 * (n + 1))
                pe.wait_ge(added2, 2 * g + PRIMED)
                k_apply[0] = k
                apply(applied2)
                pe.wait_ge(cone_set, nth(g))
                for t in range(GT):
                    last = mm(cnt_ps, onesb[:, 0:1], OC[k][:, t, :], start=(t == 0), stop=(t == GT - 1))
                last.then_inc(counted, 1)

            def any_order(i):
                with pe.Fori(0, NG) as g:
                    with pe.Fori(0, NV) as v:
                        n = g * NV + v
                        pe.wait_ge(any_rows[i], nth(g))
                        pe.wait_ge(any_onehot[i], nth(n))
                        pe.wait_ge(any_added[i], nth(n - 1))
                        for t in range(GT):
                            last = mm(any_ps if i == 2 else any_ps[0:F + 1, :],
                                      H[0][:, t, :] if i == 2 else M[:, t, :], O[0][:, t, :],
                                      start=(t == 0), stop=(t == GT - 1))
                        last.then_inc(any_sum[i], 1)

            for l in range(2):
                if l == 0:
                    fast = in_order(pe, 0)
                    with pe.If(fast == 1):
                        prefix(0, 0)
                        prefix(1, 1)
                        fill_slots(0, 0)
                        slot_rows(0, 0)
                        pe.wait_ge(xt_set, 1)
                        groups(pe, first_body)
                    pe.wait_ge(ranks_set, 1)
                    mm(PS[:, 3072:3073], ones[:, :], flag[:, 3:4], start=True, stop=True).then_inc(ranks_ps, 1)
                    fast = in_order(pe, 1)
                else:
                    with pe.If(fast == 1):
                        pe.wait_ge(xt_set, 2)
                        groups(pe, second_body)
                with pe.If(fast == 0):
                    any_order(l)
                for half in range(2):
                    pe.wait_ge(sq_set, 2 * l + half + 1)
                    for b in range(NB):
                        last = mm(row_ps[half][:, b:b + 1], SQ[:, b, :], ones[0:F, 0:1], start=True, stop=True)
                    last.then_inc(rows_ps, 1)
                    if half == 0:
                        pe.wait_ge(ht_set, l + 2)
                if l == 0:
                    product(w1_sb[:, :]).then_inc(mu_ps, 1)
            blocks = aggT[:, 0:N].rearrange("f (p b) -> f b p", b=NB)
            for b in range(NB):
                mm(PS[0:PN, 3584 + b:3585 + b], blocks[:, b, :], ident[0:F + 1, F:F + 1], start=True, stop=True)
            product(ident[0:F, 0:F]).then_inc(mu_ps, 1)
            pe.wait_ge(norm_in, 3)
            transposes().then_inc(h1_ps, 1)
            pe.wait_ge(ht_set, 4)
            for b in range(NB):
                last = mm(PS[0:PN, HID * b:HID * b + HID], HT[0:F, b, :], W1a[:, :], start=True, stop=True)
            last.then_inc(p_ps, 1)
            pe.wait_ge(p_set, 1)
            for b in range(NB):
                last = mm(PS[0:PN, HID * b:HID * b + HID], HT[:, b, :], W1b[:, :], start=True, stop=True)
            last.then_inc(q_ps, 1)
            pe.wait_ge(q_set, 1)
            for c in range(0, NB, 4):
                n = min(4, NB - c)
                o = PS[:, 128 * c:128 * c + PN * n]
                mm(o, W1a[:, :], HT[0:F, c:c + n, :].rearrange("f b p -> f (b p)"), start=True, stop=False)
                last = mm(o, W1b[:, :], HT[:, c:c + n, :].rearrange("f b p -> f (b p)"), start=False, stop=True)
            last.then_inc(self_ps, 1)
            pe.wait_ge(self_set, 1)

            def spread_q(j, c):
                i, k = step_of(j, c), c
                pe.wait_ge(onehotT_set, nth(i))
                pe.wait_ge(qwin_in[k], 8 * (i - k) + 16)
                for half in range(2):
                    pe.wait_ge(t_added, nth(2 * (i - 1) + half))
                    for e in range(8):
                        t = 8 * half + e
                        for part in range(3):
                            last = mm(t_ps[half][:, e, :], OT[k][:, TE * t:TE * t + TE], qw[k][:, part, :],
                                      start=(part == 0), stop=(part == 2))
                    last.then_inc(t_done, 1)

            def sum_gathered(j, c):
                i, k = step_of(j, c), c
                pe.wait_ge(onehot_set, nth(i))
                pe.wait_ge(relu_set, nth(2 * i + 1))
                if not (isinstance(j, int) and i == 0):
                    pe.wait_ge(rt_added, nth(f_added(*back(j, c))))
                for t in range(GT):
                    last = mm(r_ps, H[k][:, t, :], O[k][:, t, :], start=(t == 0), stop=(t == GT - 1))
                last.then_inc(sum_done, 1)

            def spread_slots(j, c, q):
                m, k, n = step_of(j, c), c, len(QUADS)
                if q == 0:
                    pe.wait_ge(s_onehots_set, nth(m))
                    pe.wait_ge(slots_in, 48 * (m + 1))
                pe.wait_ge(s_relu_set, nth(n * m + (q - 2 if q > 1 else -1)))
                for i, b in enumerate(QUADS[q]):
                    for part in range(3):
                        mm(ts_ps[q % 2][:, i, :], OTs[k][:, b, :], P3[:, b, part, :], start=(part == 0), stop=False)
                    for part in range(3):
                        last = mm(ts_ps[q % 2][:, i, :], OTd[k][:, b, :], qs[k][:, part, :],
                                  start=False, stop=(part == 2))
                last.then_inc(s_t_done, 1)

            def sum_slots(j, c, q):
                m, k, n = step_of(j, c), c, len(QUADS)
                if q == 0 and not (isinstance(j, int) and m == 0):
                    pe.wait_ge(rt_added, nth(s_added(*back(j, c))))
                pe.wait_ge(s_relu_set, nth(n * m + q))
                for b in QUADS[q]:
                    last = mm(rs_ps, Hs[:, b, :], Os[k][:, b, :], start=(b == 0), stop=(b == NB - 1))
                if q == n - 1:
                    last.then_inc(s_sum_done, 1)

            def sum_step(j, c, first):
                if not is_last(j, c):
                    for q in range(4):
                        spread_slots(j, c, q)
                        if q:
                            sum_slots(j, c, q - 1)
                if not first:
                    sum_gathered(*back(j, c))
                spread_q(j, c)
                if not is_last(j, c):
                    for q in range(4, len(QUADS)):
                        spread_slots(j, c, q)
                        sum_slots(j, c, q - 1)
                    sum_slots(j, c, len(QUADS) - 1)

            with pe.If(fast == 1):
                pe.wait_ge(p3_set, 1)
                rounds(pe, sum_step)
                sum_gathered(ROUNDS, 1)
            with pe.If(fast == 0):
                any_order(2)
            pe.wait_ge(fin_ps, 1)
            for b in range(NB):
                last = mm(MU[:, b, :], RT[:, 0:N].rearrange("f (p b) -> f b p", b=NB)[:, b, :], W2_sb[:, :],
                          start=True, stop=True)
            last.then_inc(fin_ps, 1)


def kernel(**inputs):
    import numpy as np
    import concourse.bacc as bacc
    from concourse.bass_utils import run_bass_kernel_spmd as run

    def tiles(a, fill):
        flat = np.concatenate([np.asarray(a), np.full(TILES * TE - E, fill, np.asarray(a).dtype)])
        return flat, np.ascontiguousarray(flat.reshape(TILES, TE).T)

    dst_row, dst_t = tiles(inputs["dst"], -1)
    given = [
        ("x", inputs["x"]), ("src", tiles(inputs["src"], 0)[1]), ("dst", dst_t),
        ("weight", tiles(inputs["edge_weight"], 0)[1]), ("dst_row", dst_row),
        ("w0T", np.asarray(inputs["L0_gnn_W0"]).T), ("b0", inputs["L0_gnn_b0"]),
        ("w1T", np.asarray(inputs["L0_gnn_W1"]).T), ("b1", inputs["L0_gnn_b1"]),
        ("eW1", inputs["L1_gnn_W1"]), ("eb1", inputs["L1_gnn_b1"]),
        ("eW2", inputs["L1_gnn_W2"]), ("eb2", inputs["L1_gnn_b2"]),
    ]
    nc = bacc.Bacc("TRN2", target_bir_lowering=False, num_devices=1)
    arrays, args = {}, []
    for name, a in given:
        a = np.ascontiguousarray(a)
        arrays[f"in_{name}"] = a
        args.append(nc.dram_tensor(f"in_{name}", a.shape, mybir.dt.from_np(a.dtype), kind="ExternalInput").ap())
    args.append(nc.dram_tensor("out", (N, F), mybir.dt.float32, kind="ExternalOutput").ap())
    gnn_kernel(nc, *args)
    r = run(nc, [arrays], core_ids=[0])
    return r.results[0]["out"]
```

```python
import concourse.bass as bass
from concourse import mybir
from contextlib import ExitStack

N = 3125
F = 64
HID = 128
E = 103125
PN = 125
NB = N // PN
TE = 128
GT = 16
GE = GT * TE
NG = -(-E // GE)
PAIRS = (NG - 1) // 2
AHEAD = 2
TILES = (NG + AHEAD) * GT
LAST = -(-(E - (NG - 1) * GE) // TE)
NS = 128
FIELDS = 5
CB = 7
ROUNDS = 12
assert NG == 4 * (ROUNDS + 1) - 1
CHUNKS = [range(b, min(b + CB, NB)) for b in range(0, NB, CB)]
W = 72
HW = W // 2
HR = 3 * HW
NV = -(-N // W)
NW = N + W
SECOND = 6
PRIMED = 2
QUADS = [range(b, min(b + 4, NB)) for b in range(0, NB, 4)]
MIN_NORM = 1e-15
MAXNORM = 1.0 - 0.004
CLIP = 1.0 - 1e-07
ARENA = 31000
ARTANH = [1.0 / k for k in (13, 11, 9, 7, 5, 3)]
SMALL = 0.3


def gnn_kernel(nc, x, src_t, dst_t, w_t, dst_row, w0T, b0, w1T, b1, W1, eb1, W2, eb2, out):
    f32, bf16, i32 = mybir.dt.float32, mybir.dt.bfloat16, mybir.dt.int32
    ALU = mybir.AluOpType
    ACT = mybir.ActivationFunctionType
    X = mybir.AxisListType.X
    ctx = ExitStack()
    with ctx:
        def sb(name, shape, dt=f32):
            return ctx.enter_context(nc.sbuf_tensor(name, shape, dt))

        def sem(name):
            return ctx.enter_context(nc.semaphore(name))

        xt_d = nc.dram_tensor("xt_table", (N, F), f32, kind="Internal").ap()
        p_d = nc.dram_tensor("p_table", (N, HID), f32, kind="Internal").ap()
        qf_d = nc.dram_tensor("q_full", (N, HID), f32, kind="Internal").ap()
        off_d = nc.dram_tensor("offset_rows", (NG, GE), bf16, kind="Internal").ap()
        slot_d = nc.dram_tensor("slot_rows", (NG + AHEAD, 2 * NB * NS), bf16, kind="Internal").ap()
        a_d = nc.dram_tensor("adjacency", (NG, PN, NB * W), f32, kind="Internal").ap()
        q_d = nc.dram_tensor("q_table", (NW, 3 * HID), bf16, kind="Internal").ap()

        dstT = sb("dstT", [128, TILES])
        wT = sb("wT", [128, TILES])
        offT = sb("offT", [128, TILES])
        x_sb = sb("x_sb", [PN, NB, F])
        A = sb("A", [PN, NB, F])
        Bw = sb("Bw", [128, NB * F])
        Cw = sb("Cw", [128, NB * F])
        HTw = sb("HTw", [128, NB * 128])
        B = Bw[0:PN, :].rearrange("p (b f) -> p b f", b=NB)
        C = Cw[0:PN, :].rearrange("p (b f) -> p b f", b=NB)
        HT = HTw[0:F + 1, 0:NB * PN].rearrange("f (b p) -> f b p", b=NB)
        aggTw = sb("aggTw", [128, NW])
        aggT = aggTw[0:F + 1, :]
        RT = sb("RT", [HID, NW])
        w0_sb = sb("w0_sb", [F, F])
        w1_sb = sb("w1_sb", [F, F])
        W1a = sb("W1a", [F, HID])
        W1b = sb("W1b", [F + 1, HID])
        W1ab = sb("W1ab", [F + 1, HID])
        W2_sb = sb("W2_sb", [HID, F])
        yb = sb("yb", [128, 2, F])
        ZQ = sb("ZQ", [W, 3 * HID], bf16)
        ysq = sb("ysq", [128, 2, F])
        b2b = sb("b2b", [128, F])
        ident = sb("ident", [128, 128])
        ones = sb("ones", [128, 128])
        onesb = sb("onesb", [128, 128], bf16)
        before = sb("before", [128, 128], bf16)
        rampi = sb("rampi", [128, 128], i32)
        ramp = sb("ramp", [128, 128])
        rampb = sb("rampb", [128, 128], bf16)
        identb = sb("identb", [128, 128], bf16)
        colpi = sb("colpi", [128, 1], i32)
        colp = sb("colp", [128, 1])
        halfp = sb("halfp", [128, 4])
        vtabi = sb("vtabi", [128, NV], i32)
        vtab = sb("vtab", [128, NV])
        basef = sb("basef", [128, NG + AHEAD])
        tabi = sb("tabi", [1, NG + AHEAD], i32)
        flag = sb("flag", [128, 6])
        y2s = sb("y2s", [128, 2])
        oki = sb("oki", [1, 2], i32)
        rmax = sb("rmax", [128, GT])
        rows = sb("rows", [128, 12, NB])
        arg = sb("arg", [128, NB])
        ans = sb("ans", [128, NB])
        idx = [sb(f"idx{k}", [128, GT], i32) for k in range(2)]
        dloc = [sb(f"dloc{k}", [128, GT]) for k in range(2)]
        rank = [sb(f"rank{k}", [128, GT], bf16) for k in range(2)]
        rankf = [sb(f"rankf{k}", [128, GT]) for k in range(2)]
        slot_dst = sb("slot_dst", [128, NG + AHEAD, NB], bf16)
        slot_row = [sb(f"slot_row{k}", [2 * NB, NS], bf16) for k in range(2)]
        slots = [sb(f"slots{k}", [128, FIELDS, NB], bf16) for k in range(2)]

        arena = sb("arena", [128, ARENA])
        at = [0]

        def carve(words, dt=f32, parts=128):
            at[0] += words
            assert at[0] <= ARENA, at[0]
            view = arena[0:parts, at[0] - words:at[0]]
            return view if dt == f32 else view.bitcast(dt)

        BK = [carve(GT * NB // 2, bf16).rearrange("p (t b) -> p t b", b=NB) for _ in range(2)]
        BP = carve(GT * NB).rearrange("p (t b) -> p t b", b=NB)
        S1 = [carve(GT * NS // 2, bf16).rearrange("p (s t) -> p s t", t=GT) for _ in range(2)]
        GF = [carve(GT * FIELDS * NB // 2, bf16).rearrange("p (t f b) -> p t f b", f=FIELDS, b=NB)
              for _ in range(2)]
        OS = [carve(NB * 64, bf16).rearrange("p (n b) -> p n b", b=NB) for _ in range(2)]
        OD = carve(NB * W // 2, bf16).rearrange("p (w b) -> p w b", b=NB)
        WD = [carve(3 * NB * W // 2, bf16).rearrange("p (c w b) -> p c w b", c=3, b=NB) for _ in range(2)]
        AB = [carve(NB * W).rearrange("p (b w) -> p b w", w=W) for _ in range(2)]
        ABS = AB + [arena[:, i * NB * W:(i + 1) * NB * W].rearrange("p (b w) -> p b w", w=W)
                    for i in range(SECOND - 2)]
        OC = [carve(GT * W // 2, bf16).rearrange("p (t w) -> p t w", w=W) for _ in range(2)]
        fieldT = carve(TILES * FIELDS // 2, bf16).rearrange("p (t f) -> p t f", f=FIELDS)
        bktT = carve(TILES // 2, bf16)
        row_of = carve(NB * 64, bf16).rearrange("p (n b) -> p n b", b=NB)
        slot_of = carve(NS * GT // 2, bf16).rearrange("p (s t) -> p s t", t=GT)
        at[0] = 0
        PQ = carve(NB * HID)[0:PN].rearrange("p (b h) -> p b h", h=HID)
        P3 = carve(NB * 3 * HID // 2, bf16, PN).rearrange("p (b c h) -> p b c h", c=3, h=HID)
        GP = [carve(GT * HID).rearrange("p (t h) -> p t h", h=HID) for _ in range(2)]
        early = at[0]
        H = [carve(GT * HID).rearrange("p (t h) -> p t h", h=HID) for _ in range(2)]
        O = [carve(GT * W).rearrange("p (t w) -> p t w", w=W) for _ in range(2)]
        dbc = [carve(GE // 2, bf16, HR) for _ in range(2)]
        OT = [[carve(GE // 2, bf16, HR), aggTw[0:HR, 0:GE // 2].bitcast(bf16)],
              [carve(GE // 2, bf16, HR) for _ in range(2)]]
        qw = [carve(HID, bf16, HR).rearrange("p (a h) -> p a h", h=HID) for _ in range(2)]
        qs = [carve(HID, bf16, HR).rearrange("p (a h) -> p a h", h=HID) for _ in range(2)]
        OTs = [carve(NB * NS // 2, bf16, PN).rearrange("p (b s) -> p b s", s=NS) for _ in range(2)]
        Os = [carve(NB * W).rearrange("p (b w) -> p b w", w=W) for _ in range(2)]
        end = at[0]
        OTd = [[v.bitcast(bf16).rearrange("p (b s) -> p b s", s=NS) for v in pair] for pair in (
            (HTw[0:HR, 0:NB * NS // 2], HTw[0:HR, NB * NS // 2:NB * NS]),
            (A[0:HR, :, :].rearrange("p b f -> p (b f)"), aggTw[0:HR, GE // 2:GE // 2 + NB * NS // 2]))]
        src_bc, dst_bc = Bw[0:PN, :].bitcast(bf16), Cw[0:HR, :].bitcast(bf16)
        Hs = arena[:, 0:NB * HID].rearrange("p (b h) -> p b h", h=HID)
        at[0] = early
        Q3 = carve(NB * 3 * HID // 2, bf16, PN).rearrange("p (b c h) -> p b c h", c=3, h=HID)
        assert at[0] <= early + 2 * GT * (HID + W)
        at[0] = early + 2 * GT * (HID + W)
        RQ = carve(NB * HID, parts=PN).rearrange("p (b h) -> p b h", h=HID)
        at[0] = end - 2 * NB * W - NB * NS
        QF = carve(NB * HID, parts=PN).rearrange("p (b h) -> p b h", h=HID)
        row_i = arena[0:NG, 7 * TILES:7 * TILES + GE].bitcast(i32)
        row_b = arena[0:NG, 7 * TILES + GE:7 * TILES + 3 * GE // 2].bitcast(bf16)
        G = GP[0][:, 0:GT // 2, :].rearrange("p t (a f) -> p (t a) f", a=2)
        M = H[0].rearrange("p t h -> p (t h)")[:, 0:GT * (F + 1)].rearrange("p (t f) -> p t f", t=GT)
        dstI = arena[:, 0:TILES].bitcast(i32)
        srcI = arena[:, TILES:2 * TILES].bitcast(i32)
        u = [arena[:, i * TILES:(i + 1) * TILES] for i in range(2, 6)]
        ui = arena[:, 6 * TILES:7 * TILES].bitcast(i32)

        PS = ctx.enter_context(nc.psum_tensor("PS", [128, 4096], f32))
        MU = PS[0:PN, 0:NB * F].rearrange("p (b f) -> p b f", b=NB)

        def bank(n):
            return PS[:, 512 * n:512 * n + 512]

        prefix_ps = bank(0)[:, 0:GT * NB].rearrange("p (t b) -> p t b", b=NB)
        slots_ps = bank(1)[:, 0:FIELDS * NB].rearrange("p (f b) -> p f b", b=NB)
        agg_ps = bank(2)[0:F, 0:W]
        row_t_ps = bank(3)[0:2 * NB, 0:NS]
        agg2_ps = [bank(4 + k)[0:F, 0:W] for k in range(2)]
        cnt_ps = bank(3)[F:F + 1, 0:W]
        blocks_ps = [bank(4 + c)[:, 0:len(bs) * W].rearrange("p (b w) -> p b w", w=W)
                     for c, bs in enumerate(CHUNKS)]
        any_ps = bank(6)[:, 0:W]
        r_ps, rs_ps = bank(6)[:, 0:W], bank(7)[:, 0:W]
        ts_ps = [bank(4 + i).rearrange("p (b h) -> p b h", h=HID) for i in range(2)]
        t_ps = [PS[:, 1024 * k:1024 * k + 1024].rearrange("p (t h) -> p t h", h=HID) for k in range(2)]
        sums_ps = [PS[0:PN, o:o + NB * F].rearrange("p (b f) -> p b f", b=NB) for o in (2048, 2048 - F)]

        edges_in, x_in, weights_in = sem("edges_in"), sem("x_in"), sem("weights_in")
        consts_set = sem("consts_set")
        vec = sem("vec")
        asked, answered = sem("asked"), sem("answered")
        base_ps, table_set = sem("base_ps"), sem("table_set")
        ranks_set, ranks_ps, ranks_checked = sem("ranks_set"), sem("ranks_ps"), sem("ranks_checked")
        norm_in, ht_ps, ht_set, mu_ps = sem("norm_in"), sem("ht_ps"), sem("ht_set"), sem("mu_ps")
        sums_set, rows_ps, counts_ps = sem("sums_set"), sem("rows_ps"), sem("counts_ps")
        agg_cleared = sem("agg_cleared")
        rest_set, parts_set = sem("rest_set"), sem("parts_set")
        square_asked, square_set = sem("square_asked"), sem("square_set")
        xt_set, xt_stored = sem("xt_set"), sem("xt_stored")
        h1_ps, p_ps, p_set, q_ps, q_set = sem("h1_ps"), sem("p_ps"), sem("p_set"), sem("q_ps"), sem("q_set")
        p_stored, q3_set, q_stored = sem("p_stored"), sem("q3_set"), sem("q_stored")
        self_ps, self_set = sem("self_ps"), sem("self_set")
        fin_ps, fin_set, out_stored = sem("fin_ps"), sem("fin_set"), sem("out_stored")
        q_tail = sem("q_tail")
        begun = sem("begun")

        loop_sems = []

        def counts(name, n=1):
            made = [sem(f"{name}{i}") for i in range(n)]
            loop_sems.extend(made)
            return made if n > 1 else made[0]

        def nth(i):
            return i + 1 + PRIMED

        primed = sem("primed")
        bucket_set, field_set, prefix_done, picked, rank_set, slot1_set, slots_done, slots_set = (
            counts(n) for n in ("bucket_set", "field_set", "prefix_done", "picked", "rank_set", "slot1_set",
                                "slots_done", "slots_set"))
        rankb_set = counts("rankb_set")
        dst1_set, onehots_set = counts("dst1_set"), counts("onehots_set")
        blocks_done, blocks_set = (counts(n, len(CHUNKS)) for n in ("blocks_done", "blocks_set"))
        applied, added = counts("applied"), counts("added")
        saved = counts("saved")
        a_stored = sem("a_stored")
        a_in = [sem(f"a_in{k}") for k in range(SECOND)]
        applied2, added2, counted, cdloc_set, cone_set = (counts(n) for n in (
            "applied2", "added2", "counted", "cdloc_set", "cone_set"))
        gathered = [sem(f"gathered{k}") for k in range(2)]
        idx_in = [sem(f"idx_in{k}") for k in range(2)]
        dst_in = [sem(f"dst_in{k}") for k in range(2)]
        qwin_in = [sem(f"qwin_in{k}") for k in range(2)]
        dloc_set, onehot_set, onehotT_set, t_done, t_added, relu_set, sum_done, rt_added = (
            counts(n) for n in ("dloc_set", "onehot_set", "onehotT_set", "t_done", "t_added", "relu_set",
                                "sum_done", "rt_added"))
        slots_in = sem("slots_in")
        s_onehots_set, s_t_done, s_relu_set, s_sum_done = (counts(n) for n in (
            "s_onehots_set", "s_t_done", "s_relu_set", "s_sum_done"))
        row_done, row_set, row_saved = (counts(n) for n in ("row_done", "row_set", "row_saved"))
        row_stored, off_in, off_set, off_stored, p3_set = (sem(n) for n in (
            "row_stored", "off_in", "off_set", "off_stored", "p3_set"))
        any_idx, any_gathered, any_gathered_q = ([sem(f"{n}{i}") for i in range(3)] for n in (
            "any_idx", "any_gathered", "any_gathered_q"))
        any_rows, any_dloc, any_onehot, any_sum, any_added, any_qidx = (
            [counts(f"{n}{i}_") for i in range(3)] for n in (
                "any_rows", "any_dloc", "any_onehot", "any_sum", "any_added", "any_qidx"))
        qf_stored, any_cleared = sem("qf_stored"), sem("any_cleared")

        block = ctx.enter_context(nc.Block())

        def groups(eng, body):
            body(0, 0, 0)
            with eng.Fori(0, PAIRS) as j:
                body(2 * j + 1, 1, j)
                body(2 * j + 2, 0, j + 1)

        def step_of(j, c):
            return 2 * j + c

        def f_group(j, c):
            return 2 * step_of(j, c)

        def s_group(j, c):
            return 2 * step_of(j, c) + 1

        def f_added(j, c):
            return 2 * step_of(j, c) + (0 if is_last(j, c) else 1)

        def s_added(j, c):
            return 2 * step_of(j, c)

        def back(j, c):
            return (j, 0) if c else (j - 1, 1)

        def ahead(j, c):
            return (j + 1, 0) if c else (j, 1)

        def is_last(j, c):
            return isinstance(j, int) and j == ROUNDS and c == 1

        def rounds(eng, step):
            step(0, 0, True)
            step(0, 1, False)
            with eng.Fori(1, ROUNDS) as j:
                step(j, 0, False)
                step(j, 1, False)
            step(ROUNDS, 0, False)
            step(ROUNDS, 1, False)

        def second_groups(eng, body):
            whole = (NG - SECOND) // SECOND - 1
            first = NG - whole * SECOND
            for g in range(first):
                body(g, g % SECOND, g // SECOND, g % 2)
            with eng.Fori(0, whole) as j:
                for i in range(SECOND):
                    g = first + i
                    body(SECOND * j + g, g % SECOND, j + g // SECOND, g % 2)

        def window(eng, group):
            return eng.value_load(tabi[0:1, bass.ds(group, 1)], min_val=0, max_val=N - 1)

        def in_order(eng, stage):
            eng.wait_ge(table_set if stage == 0 else ranks_checked, 1)
            return eng.value_load(oki[0:1, stage:stage + 1], min_val=0, max_val=1)

        @block.sync
        def _(sp):
            sp.dma_start(x_sb[:, :, :], x.rearrange("(p b) f -> p b f", b=NB)).then_inc(x_in, 16)
            for t, d in ((dstI, dst_t), (srcI, src_t), (wT[:, :], w_t)):
                sp.dma_start(t, d[:, :]).then_inc(edges_in, 16)
            sp.dma_start(yb[:, 0, :], b0.partition_broadcast(128)).then_inc(weights_in, 16)
            sp.dma_start(yb[:, 1, :], b1.partition_broadcast(128)).then_inc(weights_in, 16)
            sp.dma_start(b2b[:, :], eb2.partition_broadcast(128)).then_inc(weights_in, 16)
            sp.dma_start(w0_sb[:, :], w0T[:, :]).then_inc(weights_in, 16)
            sp.dma_start(w1_sb[:, :], w1T[:, :]).then_inc(weights_in, 16)
            sp.dma_start(W1a[:, :], W1[0:F, :]).then_inc(weights_in, 16)
            sp.dma_start(W1b[0:F, :], W1[F:2 * F, :]).then_inc(weights_in, 16)
            sp.dma_start(W1b[F:F + 1, :], eb1.partition_broadcast(1)).then_inc(weights_in, 16)
            sp.dma_start(W2_sb[:, :], W2[:, :]).then_inc(weights_in, 16)
            sp.dma_start(row_i, dst_row[0:NG * GE].rearrange("(g e) -> g e", e=GE)).then_inc(off_in, 16)
            sp.wait_ge(off_set, 1)
            sp.dma_start(off_d[:, :], row_b).then_inc(off_stored, 16)
            sp.wait_ge(consts_set, 13)
            sp.dma_start(q_d[N:NW, :], ZQ[:, :]).then_inc(q_tail, 16)

            def store_blocks(g, k, n):
                sp.wait_ge(blocks_set[-1], nth(g))
                sp.dma_start(a_d[bass.ds(g, 1), :, :].rearrange("g p w -> (g p) w"),
                             AB[k][0:PN].rearrange("p b w -> p (b w)")).then_inc(a_stored, 16)
                store_rows(g + 1, 1 - k)
                sp.wait_ge(a_stored, 16 * (g + 1))
                sp.sem_inc(saved, 1)
                sp.wait_ge(row_stored, 16 * (g + 2))
                sp.sem_inc(row_saved, 1)

            def store_rows(g, k):
                sp.wait_ge(row_set, nth(g))
                last = slot_d[bass.ds(g, 1), :]
                sp.dma_start(last.rearrange("g (b s) -> (g b) s", s=NS), slot_row[k][:, :])\
                    .then_inc(row_stored, 16)

            def load_blocks(g, k, n, c):
                if not (isinstance(g, int) and g < SECOND):
                    sp.wait_ge(applied2, nth(g - SECOND))
                sp.dma_start(ABS[k][0:PN].rearrange("p b w -> p (b w)"),
                             a_d[bass.ds(g, 1), :, :].rearrange("g p w -> (g p) w")).then_inc(a_in[k], 16)

            def any_indices(i):
                with sp.Fori(0, NG) as g:
                    sp.wait_ge(any_rows[i], nth(g - 1))
                    sp.dma_start(idx[0][:, :], src_t[:, bass.ds(g * GT, GT)]).then_inc(any_idx[i], 16)

            def store_table(l):
                sp.wait_ge(xt_set, l + 1)
                sp.dma_start(xt_d.rearrange("(p b) f -> p b f", b=NB), A[:, :, :]).then_inc(xt_stored, 16)

            fast = in_order(sp, 0)
            with sp.If(fast == 1):
                sp.wait_ge(off_stored, 16)
                store_rows(0, 0)
                sp.wait_ge(row_stored, 16)
                sp.sem_inc(row_saved, 1)
                groups(sp, store_blocks)
            fast = in_order(sp, 1)
            for l in range(2):
                with sp.If(fast == 0):
                    store_table(l)
                    any_indices(l)
                if l == 1:
                    with sp.If(fast == 1):
                        second_groups(sp, load_blocks)
            sp.wait_ge(p_set, 1)
            sp.dma_start(p_d.rearrange("(p b) f -> p b f", b=NB), PQ).then_inc(p_stored, 16)
            with sp.If(fast == 0):
                sp.wait_ge(q_set, 1)
                sp.dma_start(qf_d.rearrange("(p b) f -> p b f", b=NB), QF).then_inc(qf_stored, 16)
                any_indices(2)
                sp.wait_ge(qf_stored, 16)

            def load_q(dest, base, done):
                for part in range(3):
                    sp.dma_start(dest[HW * part:HW * part + HW, :, :],
                                 q_d[bass.ds(base, W), HID * part:HID * part + HID]
                                 .rearrange("(a n) h -> n a h", a=2)).then_inc(done, 16)

            def load_indices(j, c):
                sp.wait_ge(relu_set, nth(2 * (step_of(j, c) - 2) + 1))
                sp.dma_start(idx[c][:, :], src_t[:, bass.ds(f_group(j, c) * GT, GT)]).then_inc(idx_in[c], 16)

            def load_edges(j, c):
                i, k, g = step_of(j, c), c, f_group(j, c)
                base = window(sp, g)
                sp.wait_ge(onehotT_set, nth(i - 2))
                sp.dma_start(dbc[k], off_d[bass.ds(g, 1), :].rearrange("g e -> (g e)").partition_broadcast(HR))\
                    .then_inc(dst_in[k], 16)
                sp.wait_ge(t_done, nth(2 * (i - 2) + 1))
                load_q(qw[k], base, qwin_in[k])

            def load_slots(j, c):
                m, g = step_of(j, c), s_group(j, c)
                row = slot_d[bass.ds(g, 1), :].rearrange("g s -> (g s)")
                base = window(sp, g)
                sp.wait_ge(s_onehots_set, nth(m - 1))
                sp.dma_start(src_bc, row[0:NB * NS].partition_broadcast(PN)).then_inc(slots_in, 16)
                sp.dma_start(dst_bc, row[NB * NS:2 * NB * NS].partition_broadcast(HR)).then_inc(slots_in, 16)
                sp.wait_ge(s_sum_done, nth(m - 2))
                load_q(qs[c], base, slots_in)

            def load_step(j, c, first):
                if not is_last(j, c):
                    if not is_last(*ahead(j, c)):
                        load_slots(*ahead(j, c))
                    if not first:
                        load_indices(*ahead(j, c))
                    load_edges(*ahead(j, c))

            with sp.If(fast == 1):
                load_indices(0, 0)
                load_indices(0, 1)
                sp.wait_ge(q3_set, 1)
                sp.dma_start(q_d[0:N, :].rearrange("(p b) f -> p (b f)", b=NB),
                             Q3.rearrange("p b c f -> p (b c f)")).then_inc(q_stored, 16)
                sp.wait_ge(q_stored, 16)
                sp.wait_ge(q_tail, 16)
                load_slots(0, 0)
                load_edges(0, 0)
                rounds(sp, load_step)
            sp.wait_ge(fin_set, 1)
            sp.dma_start(out.rearrange("(p b) f -> p b f", b=NB), A[:, :, :]).then_inc(out_stored, 16)
            sp.wait_ge(out_stored, 16)
            sp.wait_ge(p_stored, 16)
            sp.wait_ge(q_tail, 16)

        @block.gpsimd
        def _(pool):
            pool.memset(ones[:, :], 1.0).then_inc(consts_set, 1)
            pool.memset(ident[:, :], 0.0).then_inc(consts_set, 1)
            pool.iota(rampi[:, :], [[1, 128]], base=0, channel_multiplier=0).then_inc(consts_set, 1)
            pool.iota(colpi[:, :], [[0, 1]], base=0, channel_multiplier=1).then_inc(consts_set, 1)
            pool.iota(vtabi[:, :], [[W, NV]], base=0, channel_multiplier=0).then_inc(consts_set, 1)
            pool.memset(onesb[:, :], 1.0).then_inc(consts_set, 1)
            pool.memset(before[:, :], 1.0).then_inc(consts_set, 1)
            pool.memset(identb[:, :], 0.0).then_inc(consts_set, 1)
            pool.wait_ge(consts_set, 10)
            pool.affine_select(out=identb[:, :], in_=identb[:, :], compare_op=ALU.not_equal, fill=1.0,
                               base=0, pattern=[[-1, 128]], channel_multiplier=1).then_inc(consts_set, 1)
            pool.affine_select(out=ident[:, :], in_=ident[:, :], compare_op=ALU.not_equal, fill=1.0,
                               base=0, pattern=[[-1, 128]], channel_multiplier=1).then_inc(consts_set, 1)

            pool.affine_select(out=before[:, :], in_=before[:, :], compare_op=ALU.is_ge, fill=0.0,
                               base=-1, pattern=[[1, 128]], channel_multiplier=-1).then_inc(consts_set, 1)
            for s in loop_sems:
                pool.sem_inc(s, PRIMED)
            pool.sem_inc(primed, 1)
            pool.memset(aggT[:, :], 0.0).then_inc(agg_cleared, 1)

            def prepare(g, k):
                pool.wait_ge(bucket_set, nth(g))
                pool.wait_ge(slots_done, nth(g - 2))
                pool.sem_inc(begun, 1)
                shape = [128, GT, FIELDS, NB]
                nc.gpsimd.tensor_tensor(GF[k], BK[k].unsqueeze(2).broadcast_to(shape),
                                        fieldT[:, bass.ds(g * GT, GT), :].unsqueeze(3).broadcast_to(shape),
                                        ALU.mult).then_inc(field_set, 1)

            def any_gather(i, table, dest):
                with pool.Fori(0, NG) as g:
                    pool.wait_ge(any_idx[i], 16 * (g + 1))
                    pool.wait_ge(any_rows[i], nth(g - 1))
                    pool.sem_inc(begun, 1)
                    for t in range(GT):
                        pool.indirect_dma_start(dest[:, t, :], None, table[:, :],
                                                bass.IndirectOffsetOnAxis(ap=idx[0][:, t:t + 1], axis=0))\
                            .then_inc(any_gathered[i], 16)
                    if i == 2:
                        pool.wait_ge(any_qidx[i], nth(g))
                        pool.sem_inc(begun, 1)
                        for t in range(GT):
                            pool.indirect_dma_start(GP[1][:, t, :], None, qf_d[:, :],
                                                    bass.IndirectOffsetOnAxis(ap=idx[1][:, t:t + 1], axis=0))\
                                .then_inc(any_gathered_q[i], 16)

            def gather(j, c, first):
                i, k = step_of(j, c), c
                tiles = LAST if is_last(j, c) else GT
                pool.wait_ge(idx_in[k], 8 * (i - k) + 16)
                pool.wait_ge(relu_set, nth(2 * (i - 2) + 1))
                pool.sem_inc(begun, 1)
                for t in range(tiles):
                    pool.indirect_dma_start(GP[k][:, t, :], None, p_d[:, :],
                                            bass.IndirectOffsetOnAxis(ap=idx[k][:, t:t + 1], axis=0))\
                        .then_inc(gathered[k], 16)

            fast = in_order(pool, 0)
            with pool.If(fast == 1):
                prepare(0, 0)
                prepare(1, 1)
                groups(pool, lambda g, k, n: prepare(g + AHEAD, k))
            fast = in_order(pool, 1)
            for l in range(2):
                if l == 1:
                    with pool.If(fast == 1):
                        pool.wait_ge(ht_set, 2)
                        pool.wait_ge(rows_ps, 1)
                        pool.memset(aggT[:, :], 0.0).then_inc(agg_cleared, 1)
                with pool.If(fast == 0):
                    pool.wait_ge(xt_stored, 16 * (l + 1))
                    any_gather(l, xt_d, G)
            pool.wait_ge(p_stored, 16)
            with pool.If(fast == 0):
                pool.wait_ge(qf_stored, 16)
                any_gather(2, p_d, GP[0])
            with pool.If(fast == 1):
                rounds(pool, gather)

        Y_FUNCS = [ACT.Sqrt, ACT.Tanh, ACT.Sqrt]
        EXP_FUNCS = [ACT.Sqrt, ACT.Tanh, ACT.Sqrt]
        LINEAR_FUNCS = [ACT.Sqrt, ACT.Ln, ACT.Sqrt, ACT.Tanh, ACT.Sqrt]
        LOG_FUNCS = [ACT.Sqrt, ACT.Sqrt, ACT.Ln]

        @block.scalar
        def _(sc):
            done = {"answers": 0, "squares": 0}

            def answer(funcs):
                for fn in funcs:
                    done["answers"] += 1
                    sc.wait_ge(asked, done["answers"])
                    nc.scalar.activation(ans[0:PN, :], arg[0:PN, :], fn).then_inc(answered, 1)

            def square(dst, source):
                done["squares"] += 1
                sc.wait_ge(square_asked, done["squares"])
                nc.scalar.activation(dst, source, ACT.Square).then_inc(square_set, 1)

            def copy_ht():
                sc.wait_ge(ht_ps, 1)
                for c in range(0, NB, 4):
                    n = min(4, NB - c)
                    ps = PS[0:F, 128 * c:128 * c + 500][:, 0:PN * n].rearrange("f (b p) -> f b p", b=n)
                    last = nc.scalar.activation(HT[0:F, c:c + n, :], ps, ACT.Copy)
                return last

            def take_slots(g, k):
                sc.wait_ge(slots_done, nth(g))
                sc.wait_ge(onehots_set, nth(g - 2))
                nc.scalar.activation(slot_dst[:, bass.ds(g, 1), :], slots_ps[:, 1:2, :], ACT.Copy)
                nc.scalar.activation(slots[k][:, :, :], slots_ps, ACT.Copy).then_inc(slots_set, 1)

            def take_rows(g, k):
                sc.wait_ge(row_done, nth(g))
                sc.wait_ge(row_saved, nth(g - 2))
                nc.scalar.activation(slot_row[k][:, :], row_t_ps, ACT.Copy).then_inc(row_set, 1)

            def evict(g, k, n):
                take_slots(g + 1, 1 - k)
                sc.wait_ge(saved, nth(g - 2))
                sc.wait_ge(applied, nth(g - 2))
                for c, bs in enumerate(CHUNKS):
                    sc.wait_ge(blocks_done[c], nth(g))
                    nc.scalar.activation(AB[k][:, bs[0]:bs[-1] + 1, :], blocks_ps[c], ACT.Copy)\
                        .then_inc(blocks_set[c], 1)
                take_rows(g + 1, 1 - k)

            answer([ACT.Sqrt])
            sc.wait_ge(primed, 1)
            sc.wait_ge(consts_set, 13)
            copy_ht().then_inc(ht_set, 1)
            answer(Y_FUNCS)
            answer(EXP_FUNCS)
            for l in range(2):
                sc.wait_ge(mu_ps, l + 1)
                square(B[:, :, :], MU)
                answer(LINEAR_FUNCS)
                square(B[:, :, :], A[:, :, :])
                answer(LOG_FUNCS)
                if l == 0:
                    fast = in_order(sc, 0)
                    with sc.If(fast == 1):
                        take_slots(0, 0)
                        take_rows(0, 0)
                        groups(sc, evict)
                    fast = in_order(sc, 1)
                if l == 0:
                    sc.wait_ge(sums_set, 1)
                    nc.scalar.activation(HT[0:F, :, :], aggT[0:F, 0:N].rearrange("f (p b) -> f b p", b=NB),
                                         ACT.Relu).then_inc(ht_set, 1)
                square(B[:, :, :], sums_ps[l])
                answer(EXP_FUNCS)
                answer([ACT.Sqrt, ACT.Ln])
                answer(EXP_FUNCS)
            answer([ACT.Sqrt])
            sc.wait_ge(h1_ps, 1)
            for c in range(0, NB, 4):
                n = min(4, NB - c)
                ps = PS[0:F, 128 * c:128 * c + 500][:, 0:PN * n].rearrange("f (b p) -> f b p", b=n)
                last = nc.scalar.activation(HT[0:F, c:c + n, :], ps, ACT.Copy)
            last.then_inc(ht_set, 1)
            sc.wait_ge(p_ps, 1)
            nc.scalar.activation(PQ, PS[0:PN, 0:NB * HID].rearrange("p (b h) -> p b h", b=NB),
                                 ACT.Copy).then_inc(p_set, 1)
            sc.wait_ge(p_set, 1)
            nc.scalar.activation(P3[:, :, 0, :], PQ, ACT.Copy).then_inc(parts_set, 1)
            sc.wait_ge(q_ps, 1)
            nc.scalar.activation(QF, PS[0:PN, 0:NB * HID].rearrange("p (b h) -> p b h", b=NB),
                                 ACT.Copy).then_inc(q_set, 1)
            sc.wait_ge(q_set, 1)
            nc.scalar.activation(Q3[:, :, 0, :], QF, ACT.Copy).then_inc(parts_set, 1)
            for i, (whole, parts) in enumerate(((PQ, P3), (RQ, Q3))):
                sc.wait_ge(rest_set, i + 1)
                nc.scalar.activation(parts[:, :, 1, :], whole, ACT.Copy).then_inc(parts_set, 1)
            sc.wait_ge(rest_set, 3)
            nc.scalar.activation(P3[:, :, 2, :], PQ, ACT.Copy).then_inc(p3_set, 1)
            sc.wait_ge(rest_set, 4)
            nc.scalar.activation(Q3[:, :, 2, :], RQ, ACT.Copy).then_inc(q3_set, 1)
            sc.wait_ge(self_ps, 1)
            for c in range(0, NB, 4):
                n = min(4, NB - c)
                ps = PS[:, 128 * c:128 * c + 500][:, 0:PN * n].rearrange("f (b p) -> f b p", b=n)
                last = nc.scalar.activation(RT[:, 0:N].rearrange("f (p b) -> f b p", b=NB)[:, c:c + n, :],
                                            ps, ACT.Relu)
            last.then_inc(self_set, 1)

            def relu_gathered(j, c):
                i, k = step_of(j, c), c
                sc.wait_ge(sum_done, nth(i - 2))
                for half in range(2):
                    sc.wait_ge(t_added, nth(2 * i + half))
                    part = slice(8 * half, 8 * half + 8)
                    nc.scalar.activation(H[k][:, part, :], GP[k][:, part, :], ACT.Relu).then_inc(relu_set, 1)

            def relu_slots(j, c):
                m = step_of(j, c)
                sc.wait_ge(s_sum_done, nth(m - 1))
                for q, bs in enumerate(QUADS):
                    sc.wait_ge(s_t_done, nth(len(QUADS) * m + q))
                    nc.scalar.activation(Hs[:, bs[0]:bs[-1] + 1, :], ts_ps[q % 2][:, 0:len(bs), :], ACT.Relu)\
                        .then_inc(s_relu_set, 1)

            def relu_step(j, c, first):
                if not first:
                    relu_gathered(*back(j, c))
                if not is_last(j, c):
                    relu_slots(j, c)

            with sc.If(fast == 1):
                sc.wait_ge(q_stored, 16)
                sc.wait_ge(p3_set, 1)
                rounds(sc, relu_step)
                relu_gathered(ROUNDS, 1)

        @block.vector
        def _(ve):
            n_vec = [0]
            n_ask = [0]
            n_square = [0]

            def link(ins):
                n_vec[0] += 1
                ins.then_inc(vec, 1)
                ve.wait_ge(vec, n_vec[0])

            def ask(expr):
                n_ask[0] += 1
                expr.then_inc(asked, 1)
                ve.wait_ge(answered, n_ask[0])

            def ask_square():
                n_square[0] += 1
                ve.sem_inc(square_asked, 1)

            def squares_ready():
                ve.wait_ge(square_set, n_square[0])

            P_ = slice(0, PN)

            def row(i):
                return rows[P_, i, :]

            a_, s_ = arg[P_, :], ans[P_, :]
            SS, S, NX, ATN, T, Q_, Z, T1, T2, T3, AC, BC = range(12)

            def tt(o, i, j, op):
                link(ve.tensor_tensor(o, i, j, op))

            def ts(o, i, c1, op1, c2=None, op2=ALU.bypass):
                link(ve.tensor_scalar(o, i, c1, c2, op1, op2))

            def norm(o, ss):
                ask(ve.tensor_scalar(a_, ss, MIN_NORM, None, ALU.max))
                link(ve.tensor_copy(o, s_))

            def over(o, num, den):
                link(ve.reciprocal(row(T1), den))
                tt(o, num, row(T1), ALU.mult)

            def expmap(s, ss):
                norm(row(T2), ss)
                ask(ve.tensor_copy(a_, row(T2)))
                over(s, s_, row(T2))

            def project(s, ss):
                tt(row(T2), s, s, ALU.mult)
                tt(row(T2), row(T2), ss, ALU.mult)
                norm(row(T3), row(T2))
                link(ve.reciprocal(row(T1), row(T3)))
                ts(row(T1), row(T1), MAXNORM, ALU.mult, 1.0, ALU.min)
                tt(s, s, row(T1), ALU.mult)

            def artanh_ratio(o, n):
                ts(row(T3), n, CLIP, ALU.min)
                ts(row(T1), row(T3), -1.0, ALU.mult, 1.0, ALU.add)
                link(ve.reciprocal(row(T1), row(T1)))
                ts(row(T2), row(T3), 1.0, ALU.add)
                ask(ve.tensor_tensor(a_, row(T1), row(T2), ALU.mult))
                link(ve.reciprocal(row(T1), n))
                link(ve.scalar_tensor_tensor(row(T1), s_, 0.5, row(T1), ALU.mult, ALU.mult))
                tt(row(T2), row(T3), row(T3), ALU.mult)
                ts(o, row(T2), ARTANH[0], ALU.mult)
                for c in ARTANH[1:]:
                    link(ve.scalar_tensor_tensor(o, o, c, row(T2), ALU.add, ALU.mult))
                ts(o, o, 1.0, ALU.add)
                ts(row(T2), row(T3), SMALL, ALU.is_lt)
                tt(o, o, row(T2), ALU.mult)
                ts(row(T2), row(T3), SMALL, ALU.is_ge)
                tt(row(T1), row(T1), row(T2), ALU.mult)
                tt(o, o, row(T1), ALU.add)

            def wide(r):
                return r.unsqueeze(2).broadcast_to([PN, NB, F])

            def layer_norm(dst, source):
                link(ve.tensor_reduce(row(T1), source, X, ALU.add))
                ts(row(T1), row(T1), 1.0 / F, ALU.mult)
                tt(dst, source, wide(row(T1)), ALU.subtract)
                tt(C[:, :, :], dst, dst, ALU.mult)
                link(ve.tensor_reduce(row(T2), C[:, :, :], X, ALU.add))
                ask(ve.tensor_scalar(a_, row(T2), 1.0 / F, 1e-5, ALU.mult, ALU.add))
                link(ve.reciprocal(row(T1), s_))
                link(ve.scalar_tensor_tensor(dst, dst, 0.0, wide(row(T1)), ALU.max, ALU.mult))

            def linear(l):
                y = yb[P_, l, :].unsqueeze(1).broadcast_to([PN, NB, F])
                y2 = y2s[P_, l:l + 1]
                ve.wait_ge(mu_ps, l + 1)
                tt(C[:, :, :], MU, y, ALU.mult)
                ask_square()
                link(ve.tensor_reduce(row(Z), C[:, :, :], X, ALU.add))
                squares_ready()
                link(ve.tensor_reduce(row(Q_), B[:, :, :], X, ALU.add))
                tt(row(T), row(S), row(S), ALU.mult)
                tt(row(T1), row(T), row(SS), ALU.mult)
                norm(row(NX), row(T1))
                artanh_ratio(row(ATN), row(NX))
                tt(row(T1), row(T), row(Q_), ALU.mult)
                norm(row(T), row(T1))
                ask(ve.tensor_tensor(a_, row(T), row(ATN), ALU.mult))
                over(row(T), s_, row(T))
                tt(row(T), row(T), row(S), ALU.mult)
                project(row(T), row(Q_))
                tt(row(T1), row(T), row(T), ALU.mult)
                tt(row(T1), row(T1), row(Q_), ALU.mult)
                ts(row(BC), row(T1), -1.0, ALU.mult, 1.0, ALU.add)
                tt(row(T2), row(T), row(Z), ALU.mult)
                ts(row(T2), row(T2), 2.0, ALU.mult, 1.0, ALU.add)
                link(ve.scalar_tensor_tensor(row(T3), row(T1), y2, row(T2), ALU.mult, ALU.add))
                ts(row(T3), row(T3), MIN_NORM, ALU.max)
                link(ve.reciprocal(row(T3), row(T3)))
                link(ve.scalar_tensor_tensor(row(AC), row(T2), y2, row(T), ALU.add, ALU.mult))
                tt(row(AC), row(AC), row(T3), ALU.mult)
                tt(row(BC), row(BC), row(T3), ALU.mult)
                tt(A[:, :, :], MU, wide(row(AC)), ALU.mult)
                tt(C[:, :, :], y, wide(row(BC)), ALU.mult)
                tt(A[:, :, :], A[:, :, :], C[:, :, :], ALU.add)
                ask_square()
                squares_ready()
                link(ve.tensor_reduce(row(Q_), B[:, :, :], X, ALU.add))
                link(ve.memset(row(S), 1.0))
                project(row(S), row(Q_))
                tt(row(T2), row(S), row(S), ALU.mult)
                tt(row(T2), row(T2), row(Q_), ALU.mult)
                norm(row(NX), row(T2))
                artanh_ratio(row(ATN), row(NX))
                tt(row(S), row(S), row(ATN), ALU.mult)
                ve.tensor_tensor(A[:, :, :], A[:, :, :], wide(row(S)), ALU.mult).then_inc(xt_set, 1)

            ve.memset(HT[F:F + 1, :, :], 1.0).then_inc(consts_set, 1)
            ve.memset(ZQ[:, :], 0.0).then_inc(consts_set, 1)
            ve.wait_ge(edges_in, 48)
            ve.wait_ge(consts_set, 13)
            link(ve.tensor_copy(dstT[:, :], dstI))
            ve.tensor_copy(ramp[:, :], rampi[:, :])
            link(ve.tensor_copy(rampb[:, :], rampi[:, :]))
            ve.tensor_copy(row_of, rampb[:, :].unsqueeze(2).broadcast_to([128, 128, NB]))
            ve.tensor_copy(slot_of, rampb[:, 0:NS].unsqueeze(2).broadcast_to([128, NS, GT]))
            ve.tensor_copy(colp[:, :], colpi[:, :])
            link(ve.tensor_copy(vtab[:, :], vtabi[:, :]))
            for a in range(2):
                ts(halfp[:, 2 + a:3 + a], colp[:, :], float((a + 1) * HW), ALU.is_ge, -float(HW), ALU.mult)
            tt(halfp[:, 2:3], halfp[:, 2:3], halfp[:, 3:4], ALU.add)
            tt(halfp[:, 0:1], halfp[:, 2:3], colp[:, :], ALU.add)
            ts(halfp[:, 1:2], halfp[:, 0:1], float(HW), ALU.add)
            ts(halfp[:, 2:4], halfp[:, 0:2], 1.0, ALU.add)
            link(ve.tensor_copy(u[0], srcI))
            ts(ui, u[0], 1.0 / NB, ALU.mult)
            link(ve.tensor_copy(u[1], ui))
            link(ve.scalar_tensor_tensor(u[0], u[1], -float(NB), u[0], ALU.mult, ALU.add))
            ts(u[2], u[0], 0.0, ALU.is_lt)
            ts(u[3], u[0], float(NB), ALU.is_ge)
            tt(u[3], u[3], u[2], ALU.subtract)
            tt(u[1], u[1], u[3], ALU.add)
            link(ve.scalar_tensor_tensor(u[0], u[3], -float(NB), u[0], ALU.mult, ALU.add))
            ts(u[2], dstT[:, :], 0.0, ALU.is_ge)
            link(ve.scalar_tensor_tensor(u[0], u[0], 1.0, u[2], ALU.add, ALU.mult))
            ts(bktT, u[0], -1.0, ALU.add)
            ve.wait_ge(off_in, 16)
            ts(flag[0:NG, 5:6], row_i[:, 0:1], 0.0, ALU.max)
            ve.tensor_scalar(row_b, row_i, flag[0:NG, 5:6], None, ALU.subtract).then_inc(off_set, 1)
            ve.wait_ge(off_set, 1)
            ve.wait_ge(base_ps, 1)
            link(ve.tensor_scalar(basef[:, :], PS[:, 3584:3584 + NG + AHEAD], 0.0, None, ALU.max))
            tt(offT[:, :].rearrange("p (g t) -> p g t", t=GT), dstT[:, :].rearrange("p (g t) -> p g t", t=GT),
               basef[:, :].unsqueeze(2).broadcast_to([128, NG + AHEAD, GT]), ALU.subtract)
            ve.tensor_copy(fieldT[:, :, 0], u[1])
            ts(fieldT[:, :, 1], offT[:, :], 1.0, ALU.add)
            link(ve.tensor_copy(fieldT[:, :, 2], wT[:, :]))
            tt(u[0], wT[:, :], fieldT[:, :, 2], ALU.subtract)
            link(ve.tensor_copy(fieldT[:, :, 3], u[0]))
            tt(fieldT[:, :, 4], u[0], fieldT[:, :, 3], ALU.subtract)
            ts(u[2], offT[:, :], float(W), ALU.is_lt)
            link(ve.scalar_tensor_tensor(u[3], offT[:, :], 0.0, u[2], ALU.is_ge, ALU.mult))
            ve.tensor_reduce(flag[:, 0:1], u[3], X, ALU.add).then_inc(norm_in, 1)
            ve.wait_ge(base_ps, 2)
            link(ve.tensor_scalar(flag[:, 1:2], PS[:, 3072:3073], float(E), None, ALU.is_equal))
            link(ve.tensor_copy(oki[0:1, 0:1], flag[0:1, 1:2]))
            link(ve.memset(rmax[:, :], 0.0))
            ve.wait_ge(off_stored, 16)
            ve.tensor_copy(tabi[0:1, :], basef[0:1, :]).then_inc(table_set, 1)

            ve.wait_ge(x_in, 16)
            layer_norm(A[:, :, :], x_sb[:, :, :])
            ve.wait_ge(vec, n_vec[0])
            ve.sem_inc(norm_in, 1)
            tt(C[:, :, :], A[:, :, :], A[:, :, :], ALU.mult)
            link(ve.tensor_reduce(row(SS), C[:, :, :], X, ALU.add))
            ve.wait_ge(weights_in, 16 * 9)
            tt(W1ab[0:F, :], W1a[:, :], W1b[0:F, :], ALU.add)
            link(ve.tensor_copy(W1ab[F:F + 1, :], W1b[F:F + 1, :]))
            tt(ysq[:, :, :], yb[:, :, :], yb[:, :, :], ALU.mult)
            link(ve.memset(row(Q_), 1.0))
            link(ve.tensor_reduce(rows[P_, Q_, 0:2], ysq[P_, :, :], X, ALU.add))
            expmap(row(S), row(Q_))
            project(row(S), row(Q_))
            tt(yb[P_, :, :], yb[P_, :, :], rows[P_, S, 0:2].unsqueeze(2).broadcast_to([PN, 2, F]), ALU.mult)
            tt(ysq[P_, :, :], yb[P_, :, :], yb[P_, :, :], ALU.mult)
            link(ve.tensor_reduce(y2s[P_, :], ysq[P_, :, :], X, ALU.add))
            expmap(row(S), row(SS))
            project(row(S), row(SS))

            ve.wait_ge(primed, 1)

            def bucket_edges(g, k):
                ve.wait_ge(prefix_done, nth(g - 2))
                ve.wait_ge(field_set, nth(g - 2))
                ve.wait_ge(picked, nth(g - 2))
                nc.vector.tensor_tensor(BK[k], rampb[:, 0:NB].unsqueeze(1).broadcast_to([128, GT, NB]),
                                        bktT[:, bass.ds(g * GT, GT)].unsqueeze(2).broadcast_to([128, GT, NB]),
                                        ALU.is_equal).then_inc(bucket_set, 1)

            def pick(g, k):
                ve.wait_ge(prefix_done, nth(g))
                ve.wait_ge(bucket_set, nth(g))
                ve.wait_ge(rank_set, nth(g - 1))
                nc.vector.tensor_tensor(BP, BK[k], prefix_ps, ALU.mult).then_inc(picked, 1)

            def rank_edges(g, k):
                ve.wait_ge(picked, nth(g))
                ve.wait_ge(slot1_set, nth(g - 2))
                nc.vector.tensor_reduce(rankf[k][:, :], BP, X, ALU.add).then_inc(rank_set, 1)

            def round_ranks(g, k):
                ve.wait_ge(rank_set, nth(g))
                nc.vector.tensor_copy(rank[k][:, :], rankf[k][:, :]).then_inc(rankb_set, 1)
                nc.vector.tensor_tensor(rmax[:, :], rmax[:, :], rankf[k][:, :], ALU.max)

            def rank_onehots(g, k):
                ve.wait_ge(slots_done, nth(g - 2))
                ve.wait_ge(rankb_set, nth(g))
                nc.vector.tensor_tensor(S1[k], slot_of,
                                        rank[k][:, :].unsqueeze(1).broadcast_to([128, NS, GT]),
                                        ALU.is_equal).then_inc(slot1_set, 1)

            def slot_destinations(g, k):
                ve.wait_ge(slots_set, nth(g))
                nc.vector.tensor_tensor(OD, row_of[:, 1:1 + W, :],
                                        slots[k][:, 1, :].unsqueeze(1).broadcast_to([128, W, NB]),
                                        ALU.is_equal).then_inc(dst1_set, 1)

            def slot_sources(g, k):
                ve.wait_ge(blocks_done[-1], nth(g - 2))
                nc.vector.tensor_tensor(OS[k], row_of[:, :, :],
                                        slots[k][:, 0, :].unsqueeze(1).broadcast_to([128, 128, NB]),
                                        ALU.is_equal)

            def slot_weights(g, k):
                ve.wait_ge(dst1_set, nth(g))
                shape = [128, 3, W, NB]
                nc.vector.tensor_tensor(WD[k], OD.unsqueeze(1).broadcast_to(shape),
                                        slots[k][:, 2:5, :].unsqueeze(2).broadcast_to(shape),
                                        ALU.mult).then_inc(onehots_set, 1)

            def add_sums(g):
                base = window(ve, g)
                ve.wait_ge(applied, nth(g))
                ve.wait_ge(added, nth(g - 1))
                win = aggT[0:F, bass.ds(base, W)]
                nc.vector.tensor_tensor(win, win, agg_ps, ALU.add).then_inc(added, 1)

            def first_layer():
                bucket_edges(0, 0)
                bucket_edges(1, 1)
                for g in range(2):
                    pick(g, g)
                    rank_edges(g, g)
                    round_ranks(g, g)
                    rank_onehots(g, g)
                bucket_edges(2, 0)
                slot_destinations(0, 0)
                slot_sources(0, 0)
                slot_weights(0, 0)
                with ve.Fori(0, PAIRS) as j:
                    for g, k in ((2 * j + 1, 1), (2 * j + 2, 0)):
                        pick(g + 1, 1 - k)
                        bucket_edges(g + 2, k)
                        rank_edges(g + 1, 1 - k)
                        slot_destinations(g, k)
                        round_ranks(g + 1, 1 - k)
                        slot_sources(g, k)
                        rank_onehots(g + 1, 1 - k)
                        slot_weights(g, k)
                        add_sums(g - 1)
                add_sums(NG - 1)
                ve.wait_ge(added, nth(NG - 1))
                ve.wait_ge(field_set, nth(NG - 1 + AHEAD))
                ve.wait_ge(prefix_done, nth(NG - 1 + AHEAD))
                ve.wait_ge(slots_done, nth(NG))

            def second_layer():
                def body(g, _, n, k):
                    ve.wait_ge(cone_set, nth(g - 2))
                    nc.vector.tensor_copy(dloc[k][:, :], offT[:, bass.ds(g * GT, GT)]).then_inc(cdloc_set, 1)
                    ve.wait_ge(cdloc_set, nth(g))
                    ve.wait_ge(counted, nth(g - 2))
                    for t in range(GT):
                        last = nc.vector.tensor_scalar(OC[k][:, t, :], rampb[:, 0:W], dloc[k][:, t:t + 1], None,
                                                       ALU.is_equal)
                    last.then_inc(cone_set, 1)
                    base = window(ve, g)
                    ve.wait_ge(applied2, nth(g))
                    ve.wait_ge(added2, 2 * g + PRIMED)
                    win = aggT[0:F, bass.ds(base, W)]
                    nc.vector.tensor_tensor(win, win, agg2_ps[k], ALU.add).then_inc(added2, 1)
                    ve.wait_ge(counted, nth(g))
                    win = aggT[F:F + 1, bass.ds(base, W)]
                    nc.vector.tensor_tensor(win, win, cnt_ps, ALU.add).then_inc(added2, 1)
                second_groups(ve, body)
                ve.wait_ge(added2, 2 * NG + PRIMED)

            def any_order(i):
                dest = RT if i == 2 else aggT[0:F + 1, :]
                source = any_ps if i == 2 else any_ps[0:F + 1, :]
                if i < 2:
                    if i == 0:
                        ve.wait_ge(agg_cleared, 1)
                    else:
                        ve.wait_ge(ht_set, 2)
                    ve.memset(aggT[:, :], 0.0).then_inc(any_cleared, 1)
                    ve.memset(M[:, :, F:F + 1], 1.0).then_inc(any_cleared, 1)
                    ve.wait_ge(any_cleared, 2 * (i + 1))
                with ve.Fori(0, NG) as g:
                    cols = bass.ds(g * GT, GT)
                    if i == 2:
                        ve.wait_ge(any_rows[i], nth(g - 1))
                        nc.vector.tensor_scalar(idx[1][:, :], dstT[:, cols], 0.0, None, ALU.max)\
                            .then_inc(any_qidx[i], 1)
                        ve.wait_ge(any_gathered_q[i], 16 * GT * (g + 1))
                    ve.wait_ge(any_gathered[i], 16 * GT * (g + 1))
                    ve.wait_ge(any_sum[i], NV * g + PRIMED)
                    if i == 2:
                        nc.vector.tensor_tensor(GP[0], GP[0], GP[1], ALU.add).then_inc(any_dloc[i], 1)
                        ve.wait_ge(any_dloc[i], (NV + 1) * g + 1 + PRIMED)
                        nc.vector.tensor_scalar(H[0], GP[0], 0.0, None, ALU.max).then_inc(any_rows[i], 1)
                    else:
                        nc.vector.tensor_tensor(M[:, :, 0:F], G, wT[:, cols].unsqueeze(2)
                                                .broadcast_to([128, GT, F]), ALU.mult).then_inc(any_rows[i], 1)
                    with ve.Fori(0, NV) as v:
                        n = g * NV + v
                        ve.wait_ge(any_onehot[i], nth(n - 1))
                        nc.vector.tensor_scalar(dloc[0][:, :], dstT[:, cols], vtab[:, bass.ds(v, 1)], None,
                                                ALU.subtract).then_inc(any_dloc[i], 1)
                        ve.wait_ge(any_dloc[i], nth(n + (g + 1 if i == 2 else 0)))
                        ve.wait_ge(any_sum[i], nth(n - 1))
                        for t in range(GT):
                            last = nc.vector.tensor_scalar(O[0][:, t, :], ramp[:, 0:W], dloc[0][:, t:t + 1],
                                                           None, ALU.is_equal)
                        last.then_inc(any_onehot[i], 1)
                        ve.wait_ge(any_sum[i], nth(n))
                        ve.wait_ge(any_added[i], nth(n - 1))
                        win = dest[:, bass.ds(v * W, W)]
                        nc.vector.tensor_tensor(win, win, source, ALU.add).then_inc(any_added[i], 1)
                ve.wait_ge(any_added[i], nth(NG * NV - 1))

            def check_ranks():
                link(ve.tensor_reduce(flag[:, 2:3], rmax[:, :], X, ALU.max))
                ve.tensor_scalar(flag[:, 3:4], flag[:, 2:3], float(NS - 1), None, ALU.is_le).then_inc(ranks_set, 1)
                ve.wait_ge(ranks_ps, 1)
                link(ve.tensor_scalar(flag[:, 4:5], PS[:, 3072:3073], 128.0, None, ALU.is_equal))
                link(ve.tensor_scalar(flag[:, 4:5], flag[:, 4:5], flag[:, 1:2], None, ALU.mult))
                ve.tensor_copy(oki[0:1, 1:2], flag[0:1, 4:5]).then_inc(ranks_checked, 1)

            def act_scales(l):
                ve.sem_inc(sums_set, 1)
                ve.wait_ge(rows_ps, l + 1)
                ask_square()
                squares_ready()
                link(ve.tensor_reduce(row(Q_), B[:, :, :], X, ALU.add))
                link(ve.scalar_tensor_tensor(C[:, :, :], sums_ps[l], 0.0, B[:, :, :], ALU.is_gt, ALU.mult))
                link(ve.tensor_reduce(row(SS), C[:, :, :], X, ALU.add))
                expmap(row(S), row(Q_))
                project(row(S), row(Q_))
                tt(row(T2), row(S), row(S), ALU.mult)
                tt(row(T2), row(T2), row(Q_), ALU.mult)
                norm(row(NX), row(T2))
                artanh_ratio(row(ATN), row(NX))
                tt(row(ATN), row(S), row(ATN), ALU.mult)
                tt(row(T3), row(ATN), row(ATN), ALU.mult)
                tt(row(Q_), row(T3), row(SS), ALU.mult)
                expmap(row(S), row(Q_))
                project(row(S), row(Q_))
                tt(row(S), row(S), row(ATN), ALU.mult)

            for l in range(2):
                linear(l)
                if l == 0:
                    fast = in_order(ve, 0)
                    with ve.If(fast == 1):
                        ve.wait_ge(xt_set, 1)
                        ve.wait_ge(agg_cleared, 1)
                        first_layer()
                    check_ranks()
                    fast = in_order(ve, 1)
                else:
                    with ve.If(fast == 1):
                        ve.wait_ge(xt_set, 2)
                        ve.wait_ge(agg_cleared, 2)
                        second_layer()
                with ve.If(fast == 0):
                    any_order(l)
                act_scales(l)

            link(ve.scalar_tensor_tensor(A[:, :, :], sums_ps[1], 0.0, wide(row(S)), ALU.max, ALU.mult))
            tt(x_sb[:, :, :], x_sb[:, :, :], A[:, :, :], ALU.add)
            layer_norm(A[:, :, :], x_sb[:, :, :])
            ve.sem_inc(norm_in, 1)
            ve.wait_ge(counts_ps, 1)
            link(ve.tensor_copy(row(Z), PS[0:PN, 3584:3584 + NB]))
            ts(row(Z), row(Z), 1.0, ALU.add, 1.0, ALU.max)
            link(ve.reciprocal(row(Z), row(Z)))
            tt(x_sb[:, :, :], x_sb[:, :, :], b2b[P_, :].unsqueeze(1).broadcast_to([PN, NB, F]), ALU.add)
            link(ve.memset(RT[:, N:NW], 0.0))
            ve.wait_ge(p_stored, 16)
            for c in range(2):
                ve.wait_ge(parts_set, 2 * c + 1)
                ve.tensor_tensor(PQ, PQ, P3[:, :, c, :], ALU.subtract).then_inc(rest_set, 1)
                ve.wait_ge(parts_set, 2 * c + 2)
                ve.tensor_tensor(RQ, RQ if c else QF, Q3[:, :, c, :], ALU.subtract).then_inc(rest_set, 1)
            ve.wait_ge(self_set, 1)

            def destinations(j, c):
                i, k, g = step_of(j, c), c, f_group(j, c)
                ve.wait_ge(onehot_set, nth(i - 2))
                nc.vector.tensor_copy(dloc[k][:, :], offT[:, bass.ds(g * GT, GT)]).then_inc(dloc_set, 1)
                ve.wait_ge(dloc_set, nth(i))
                ve.wait_ge(sum_done, nth(i - 2))
                nc.vector.tensor_tensor(O[k], ramp[:, 0:W].unsqueeze(1).broadcast_to([128, GT, W]),
                                        dloc[k][:, :].unsqueeze(2).broadcast_to([128, GT, W]),
                                        ALU.is_equal).then_inc(onehot_set, 1)
                ve.wait_ge(dst_in[k], 8 * (i - k) + 16)
                ve.wait_ge(t_done, nth(2 * (i - 2) + 1))
                for a in range(2):
                    last = nc.vector.tensor_scalar(OT[k][a], dbc[k], halfp[0:HR, a:a + 1], None, ALU.is_equal)
                last.then_inc(onehotT_set, 1)

            def slot_rows(j, c):
                m, k, g = step_of(j, c), c, s_group(j, c)
                ve.wait_ge(slots_in, 80 * (m + 1))
                ve.wait_ge(s_sum_done, nth(m - 2))
                nc.vector.tensor_scalar(OTs[k].rearrange("p b s -> p (b s)"), src_bc, colp[0:PN, :], None,
                                        ALU.is_equal)
                for a in range(2):
                    nc.vector.tensor_scalar(OTd[k][a].rearrange("p b s -> p (b s)"), dst_bc,
                                            halfp[0:HR, 2 + a:3 + a], None, ALU.is_equal)
                nc.vector.tensor_tensor(Os[k], ramp[:, 1:1 + W].unsqueeze(1).broadcast_to([128, NB, W]),
                                        slot_dst[:, bass.ds(g, 1), :].rearrange("p g b -> p (g b)")
                                        .unsqueeze(2).broadcast_to([128, NB, W]),
                                        ALU.is_equal).then_inc(s_onehots_set, 1)

            def add_q(j, c):
                i, k = step_of(j, c), c
                tiles = LAST if is_last(j, c) else GT
                ve.wait_ge(gathered[k], 8 * GT * (i - k) + 16 * tiles)
                for half in range(2):
                    ve.wait_ge(t_done, nth(2 * i + half))
                    part = GP[k][:, 8 * half:8 * half + 8, :]
                    nc.vector.tensor_tensor(part, part, t_ps[half], ALU.add).then_inc(t_added, 1)

            def add_messages(g, q, ps):
                base = window(ve, g)
                ve.wait_ge(rt_added, nth(q - 1))
                win = RT[:, bass.ds(base, W)]
                nc.vector.tensor_tensor(win, win, ps, ALU.add).then_inc(rt_added, 1)

            def add_gathered(j, c):
                ve.wait_ge(sum_done, nth(step_of(j, c)))
                add_messages(f_group(j, c), f_added(j, c), r_ps)

            def add_slots(j, c):
                ve.wait_ge(s_sum_done, nth(step_of(j, c)))
                add_messages(s_group(j, c), s_added(j, c), rs_ps)

            def add_step(j, c, first):
                if not first:
                    add_slots(*back(j, c))
                if not is_last(j, c):
                    if not is_last(*ahead(j, c)):
                        slot_rows(*ahead(j, c))
                    destinations(*ahead(j, c))
                if not first:
                    add_gathered(*back(j, c))
                add_q(j, c)

            with ve.If(fast == 1):
                slot_rows(0, 0)
                destinations(0, 0)
                rounds(ve, add_step)
                add_gathered(ROUNDS, 1)
                ve.wait_ge(rt_added, nth(f_added(ROUNDS, 1)))
            with ve.If(fast == 0):
                any_order(2)
            ve.sem_inc(fin_ps, 1)
            ve.wait_ge(fin_ps, 2)
            tt(A[:, :, :], MU, wide(row(Z)), ALU.mult)
            ve.tensor_tensor(A[:, :, :], A[:, :, :], x_sb[:, :, :], ALU.add).then_inc(fin_set, 1)

        @block.tensor
        def _(pe):
            mm = nc.tensor.matmul
            pe.wait_ge(primed, 1)

            def transposes():
                for b in range(NB):
                    last = nc.tensor.transpose(PS[0:F, 512 * (b // 4) + PN * (b % 4):
                                                  512 * (b // 4) + PN * (b % 4) + PN],
                                               A[:, b, :], ident[0:PN, 0:PN])
                return last

            def product(weights):
                for b in range(NB):
                    last = mm(MU[:, b, :], HT[0:F, b, :], weights, start=True, stop=True)
                return last

            pe.wait_ge(edges_in, 48)
            pe.wait_ge(consts_set, 13)
            pe.wait_ge(vec, 1)
            mm(PS[:, 3584:3584 + NG + AHEAD], ones[0:1, :], dstT[0:1, :].rearrange("p (g t) -> p g t", t=GT)[:, :, 0],
               start=True, stop=True).then_inc(base_ps, 1)
            pe.wait_ge(norm_in, 1)
            mm(PS[:, 3072:3073], ones[:, :], flag[:, 0:1], start=True, stop=True).then_inc(base_ps, 1)
            pe.wait_ge(norm_in, 2)
            pe.wait_ge(table_set, 1)
            transposes().then_inc(ht_ps, 1)
            pe.wait_ge(ht_set, 1)
            pe.wait_ge(weights_in, 16 * 9)
            product(w0_sb[:, :]).then_inc(mu_ps, 1)

            def prefix(g, k):
                pe.wait_ge(bucket_set, nth(g))
                pe.wait_ge(picked, nth(g - 1))
                mm(prefix_ps, before[:, :], BK[k], start=True, stop=False)
                for d in range(1, GT):
                    last = mm(prefix_ps[:, d:GT, :], onesb[:, :], BK[k][:, 0:GT - d, :], start=False,
                              stop=(d == GT - 1))
                last.then_inc(prefix_done, 1)

            def fill_slots(g, k):
                pe.wait_ge(slot1_set, nth(g))
                pe.wait_ge(field_set, nth(g))
                pe.wait_ge(slots_set, nth(g - 1))
                for t in range(GT):
                    last = mm(slots_ps, S1[k][:, :, t], GF[k][:, t, :, :], start=(t == 0), stop=(t == GT - 1))
                last.then_inc(slots_done, 1)

            def blocks(g, k):
                pe.wait_ge(onehots_set, nth(g))
                for c, bs in enumerate(CHUNKS):
                    pe.wait_ge(blocks_set[c], nth(g - 1))
                    for i, b in enumerate(bs):
                        for part in range(3):
                            last = mm(blocks_ps[c][:, i, :], OS[k][:, :, b], WD[k][:, part, :, b],
                                      start=(part == 0), stop=(part == 2))
                    last.then_inc(blocks_done[c], 1)

            def slot_rows(g, k):
                pe.wait_ge(slots_set, nth(g))
                pe.wait_ge(row_set, nth(g - 1))
                mm(row_t_ps, slots[k][:, 0:2, :].rearrange("p f b -> p (f b)"), identb[:, :], start=True, stop=True)\
                    .then_inc(row_done, 1)

            def apply(done, sums, adjacency):
                for b in range(NB):
                    last = mm(sums, A[:, b, :], adjacency[0:PN, b, :], start=(b == 0), stop=(b == NB - 1))
                last.then_inc(done, 1)

            def first_body(g, k, n):
                prefix(g + 2, k)
                fill_slots(g + 1, 1 - k)
                blocks(g, k)
                slot_rows(g + 1, 1 - k)
                pe.wait_ge(blocks_set[-1], nth(g))
                pe.wait_ge(added, nth(g - 1))
                apply(applied, agg_ps, AB[k])

            def second_body(g, blocks_at, n, k):
                pe.wait_ge(a_in[blocks_at], 16 * (n + 1))
                if not (isinstance(g, int) and g < 2):
                    pe.wait_ge(added2, 2 * g - 3 + PRIMED)
                apply(applied2, agg2_ps[k], ABS[blocks_at])
                pe.wait_ge(cone_set, nth(g))
                pe.wait_ge(added2, 2 * g + PRIMED)
                for t in range(GT):
                    last = mm(cnt_ps, onesb[:, 0:1], OC[k][:, t, :], start=(t == 0), stop=(t == GT - 1))
                last.then_inc(counted, 1)

            def any_order(i):
                with pe.Fori(0, NG) as g:
                    with pe.Fori(0, NV) as v:
                        n = g * NV + v
                        pe.wait_ge(any_rows[i], nth(g))
                        pe.wait_ge(any_onehot[i], nth(n))
                        pe.wait_ge(any_added[i], nth(n - 1))
                        for t in range(GT):
                            last = mm(any_ps if i == 2 else any_ps[0:F + 1, :],
                                      H[0][:, t, :] if i == 2 else M[:, t, :], O[0][:, t, :],
                                      start=(t == 0), stop=(t == GT - 1))
                        last.then_inc(any_sum[i], 1)

            for l in range(2):
                if l == 0:
                    fast = in_order(pe, 0)
                    with pe.If(fast == 1):
                        prefix(0, 0)
                        prefix(1, 1)
                        fill_slots(0, 0)
                        slot_rows(0, 0)
                        pe.wait_ge(xt_set, 1)
                        groups(pe, first_body)
                    pe.wait_ge(ranks_set, 1)
                    mm(PS[:, 3072:3073], ones[:, :], flag[:, 3:4], start=True, stop=True).then_inc(ranks_ps, 1)
                    fast = in_order(pe, 1)
                else:
                    with pe.If(fast == 1):
                        pe.wait_ge(xt_set, 2)
                        second_groups(pe, second_body)
                with pe.If(fast == 0):
                    any_order(l)
                blocks = aggT[0:F, 0:N].rearrange("f (p b) -> f b p", b=NB)
                pe.wait_ge(sums_set, l + 1)
                for b in range(NB):
                    last = nc.tensor.transpose(sums_ps[l][:, b, :], blocks[:, b, :], ident[0:F, 0:F])
                last.then_inc(rows_ps, 1)
                if l == 0:
                    pe.wait_ge(ht_set, 2)
                    product(w1_sb[:, :]).then_inc(mu_ps, 1)
            blocks = aggT[:, 0:N].rearrange("f (p b) -> f b p", b=NB)
            for b in range(NB):
                last = mm(PS[0:PN, 3584 + b:3585 + b], blocks[:, b, :], ident[0:F + 1, F:F + 1],
                          start=True, stop=True)
            last.then_inc(counts_ps, 1)
            pe.wait_ge(norm_in, 3)
            transposes().then_inc(h1_ps, 1)
            pe.wait_ge(ht_set, 3)
            for b in range(NB):
                last = mm(PS[0:PN, HID * b:HID * b + HID], HT[0:F, b, :], W1a[:, :], start=True, stop=True)
            last.then_inc(p_ps, 1)
            pe.wait_ge(p_set, 1)
            for b in range(NB):
                last = mm(PS[0:PN, HID * b:HID * b + HID], HT[:, b, :], W1b[:, :], start=True, stop=True)
            last.then_inc(q_ps, 1)
            pe.wait_ge(q_set, 1)
            for c in range(0, NB, 4):
                n = min(4, NB - c)
                o = PS[:, 128 * c:128 * c + PN * n]
                last = mm(o, W1ab[:, :], HT[:, c:c + n, :].rearrange("f b p -> f (b p)"), start=True, stop=True)
            last.then_inc(self_ps, 1)
            pe.wait_ge(self_set, 1)

            def spread_q(j, c):
                i, k = step_of(j, c), c
                pe.wait_ge(onehotT_set, nth(i))
                pe.wait_ge(qwin_in[k], 24 * (i - k) + 48)
                for half in range(2):
                    pe.wait_ge(t_added, nth(2 * (i - 1) + half))
                    for e in range(8):
                        t = 8 * half + e
                        for a in range(2):
                            last = mm(t_ps[half][:, e, :], OT[k][a][:, TE * t:TE * t + TE], qw[k][:, a, :],
                                      start=(a == 0), stop=(a == 1))
                    last.then_inc(t_done, 1)

            def sum_gathered(j, c):
                i, k = step_of(j, c), c
                pe.wait_ge(onehot_set, nth(i))
                pe.wait_ge(relu_set, nth(2 * i + 1))
                if not (isinstance(j, int) and i == 0):
                    pe.wait_ge(rt_added, nth(f_added(*back(j, c))))
                tiles = LAST if is_last(j, c) else GT
                for t in range(tiles):
                    last = mm(r_ps, H[k][:, t, :], O[k][:, t, :], start=(t == 0), stop=(t == tiles - 1))
                last.then_inc(sum_done, 1)

            def spread_slots(j, c, q):
                m, k, n = step_of(j, c), c, len(QUADS)
                if q == 0:
                    pe.wait_ge(s_onehots_set, nth(m))
                    pe.wait_ge(slots_in, 80 * (m + 1))
                pe.wait_ge(s_relu_set, nth(n * m + (q - 2 if q > 1 else -1)))
                for i, b in enumerate(QUADS[q]):
                    for part in range(3):
                        mm(ts_ps[q % 2][:, i, :], OTs[k][:, b, :], P3[:, b, part, :], start=(part == 0), stop=False)
                    for a in range(2):
                        last = mm(ts_ps[q % 2][:, i, :], OTd[k][a][:, b, :], qs[k][:, a, :],
                                  start=False, stop=(a == 1))
                last.then_inc(s_t_done, 1)

            def sum_slots(j, c, q):
                m, k, n = step_of(j, c), c, len(QUADS)
                if q == 0 and not (isinstance(j, int) and m == 0):
                    pe.wait_ge(rt_added, nth(s_added(*back(j, c))))
                pe.wait_ge(s_relu_set, nth(n * m + q))
                for b in QUADS[q]:
                    last = mm(rs_ps, Hs[:, b, :], Os[k][:, b, :], start=(b == 0), stop=(b == NB - 1))
                if q == n - 1:
                    last.then_inc(s_sum_done, 1)

            def sum_step(j, c, first):
                if not is_last(j, c):
                    for q in range(4):
                        spread_slots(j, c, q)
                        if q:
                            sum_slots(j, c, q - 1)
                if not first:
                    sum_gathered(*back(j, c))
                spread_q(j, c)
                if not is_last(j, c):
                    for q in range(4, len(QUADS)):
                        spread_slots(j, c, q)
                        sum_slots(j, c, q - 1)
                    sum_slots(j, c, len(QUADS) - 1)

            with pe.If(fast == 1):
                pe.wait_ge(p3_set, 1)
                rounds(pe, sum_step)
                sum_gathered(ROUNDS, 1)
            with pe.If(fast == 0):
                any_order(2)
            pe.wait_ge(fin_ps, 1)
            for b in range(NB):
                last = mm(MU[:, b, :], RT[:, 0:N].rearrange("f (p b) -> f b p", b=NB)[:, b, :], W2_sb[:, :],
                          start=True, stop=True)
            last.then_inc(fin_ps, 1)


def kernel(**inputs):
    import numpy as np
    import concourse.bacc as bacc
    from concourse.bass_utils import run_bass_kernel_spmd as run

    def tiles(a, fill):
        flat = np.concatenate([np.asarray(a), np.full(TILES * TE - E, fill, np.asarray(a).dtype)])
        return flat, np.ascontiguousarray(flat.reshape(TILES, TE).T)

    dst_row, dst_t = tiles(inputs["dst"], -1)
    given = [
        ("x", inputs["x"]), ("src", tiles(inputs["src"], 0)[1]), ("dst", dst_t),
        ("weight", tiles(inputs["edge_weight"], 0)[1]), ("dst_row", dst_row),
        ("w0T", np.asarray(inputs["L0_gnn_W0"]).T), ("b0", inputs["L0_gnn_b0"]),
        ("w1T", np.asarray(inputs["L0_gnn_W1"]).T), ("b1", inputs["L0_gnn_b1"]),
        ("eW1", inputs["L1_gnn_W1"]), ("eb1", inputs["L1_gnn_b1"]),
        ("eW2", inputs["L1_gnn_W2"]), ("eb2", inputs["L1_gnn_b2"]),
    ]
    nc = bacc.Bacc("TRN2", target_bir_lowering=False, num_devices=1)
    arrays, args = {}, []
    for name, a in given:
        a = np.ascontiguousarray(a)
        arrays[f"in_{name}"] = a
        args.append(nc.dram_tensor(f"in_{name}", a.shape, mybir.dt.from_np(a.dtype), kind="ExternalInput").ap())
    args.append(nc.dram_tensor("out", (N, F), mybir.dt.float32, kind="ExternalOutput").ap())
    gnn_kernel(nc, *args)
    r = run(nc, [arrays], core_ids=[0])
    return r.results[0]["out"]
```
